# Optimizing a Trainium2 kernel written in Bass

```python
import numpy as np
import jax
import jax.numpy as jnp

def _softmax(x, axis=-1):
    return jax.nn.softmax(x, axis=axis)

def _gelu(x):
    return jax.nn.gelu(x, approximate=True)

def _silu(x):
    return jax.nn.silu(x)

def _sigmoid(x):
    return jax.nn.sigmoid(x)

def _layernorm(x, axis=-1, eps=1e-05):
    m = jnp.mean(x, axis=axis, keepdims=True)
    v = jnp.var(x, axis=axis, keepdims=True)
    return (x - m) / jnp.sqrt(v + eps)

def _scatter_add(tgt, idx, src, axis=0):
    return tgt.at[idx].add(src)

def _segment_sum(src, seg, n):
    return jax.ops.segment_sum(src, seg, n)
kernel_name = 'mk_xattn_seq_d4_seqx_r8_5333d6'

def setup_inputs(seed: int=0):
    np.random.seed(seed)
    _w = jnp.asarray

    def _rec_inputs():
        import jax
        import jax.numpy as jnp
        _rk = jax.random.key(seed)
        x = -0.0005146 + 1 * jax.random.normal(jax.random.fold_in(_rk, 1), (16, 128, 256), jnp.float32)
        _lenS = 128 - jax.random.randint(jax.random.fold_in(_rk, 7), (16,), 0, max(1, 128 // 4) + 1, jnp.int32)
        _lenS2 = 128 - jax.random.randint(jax.random.fold_in(_rk, 8), (16,), 0, max(1, 128 // 4) + 1, jnp.int32)
        _ctx_2048P = jax.random.normal(jax.random.fold_in(_rk, 11), (16, 16, 256), jnp.float32)
        _ctx_2048c = jax.random.dirichlet(jax.random.fold_in(_rk, 511), 0.3 * jnp.ones((16,), jnp.float32), (16, 128))
        _ctx_2048t = jnp.einsum('bsk,bkd->bsd', _ctx_2048c, _ctx_2048P)
        _ctx_2048t = _ctx_2048t * jax.lax.rsqrt(jnp.mean(jnp.square(_ctx_2048t)) + 1e-12) * 0.953939
        ctx_2048 = -0.000392918 + 0.999932 * (_ctx_2048t + 0.3 * jax.random.normal(jax.random.fold_in(_rk, 611), (16, 128, 256), jnp.float32))
        _validS = jnp.arange(128)[None, :] < _lenS[:, None]
        _validS2 = jnp.arange(128)[None, :] < _lenS2[:, None]
        _causal = jnp.tril(jnp.ones((128, 128), dtype=bool))
        mask_BxS2_ik0 = jnp.where(jnp.broadcast_to(_validS2[:, :], (16, 128)), 0, 1).astype(jnp.int32)
        mask_Bx1xSxS2_ff0 = jnp.where(jnp.ones((16, 1, 128, 128), dtype=bool), 0.0, -1000000000.0).astype(jnp.float32)
        mask_BxS2_bf1 = jnp.ones((16, 128), dtype=bool)
        return (x, ctx_2048, mask_BxS2_ik0, mask_Bx1xSxS2_ff0, mask_BxS2_bf1)
    x, ctx_2048, mask_BxS2_ik0, mask_Bx1xSxS2_ff0, mask_BxS2_bf1 = _rec_inputs()

    def _L0_xattn_setup():
        import jax, jax.numpy as jnp
        import numpy as np
        B, P, K, H, NH = (4, 256, 32, 256, 16)
        DH = H // NH
        EPS = 1e-06

        def rmsnorm(x, w):
            var = jnp.mean(jnp.square(x), axis=-1, keepdims=True)
            return x * jax.lax.rsqrt(var + EPS) * w
        key = jax.random.key(seed)
        ks = jax.random.split(key, 12)
        s = 0.02
        return {'x': jax.random.normal(ks[0], (B, P, H), jnp.float32), 'latents': jax.random.normal(ks[1], (B, K, H), jnp.float32), 'attention_mask': jax.random.randint(ks[2], (B, P), 0, 2, jnp.int32), 'q_w': s * jax.random.normal(ks[3], (H, H), jnp.float32), 'q_b': jnp.zeros((H,), jnp.float32), 'kv_w': s * jax.random.normal(ks[4], (H, 2 * H), jnp.float32), 'kv_b': jnp.zeros((2 * H,), jnp.float32), 'out_w': s * jax.random.normal(ks[5], (H, H), jnp.float32), 'out_b': jnp.zeros((H,), jnp.float32), 'postnorm_w': jnp.ones((H,), jnp.float32), 'mlp_w1': s * jax.random.normal(ks[6], (H, 4 * H), jnp.float32), 'mlp_b1': jnp.zeros((4 * H,), jnp.float32), 'mlp_w2': s * jax.random.normal(ks[7], (4 * H, H), jnp.float32), 'mlp_b2': jnp.zeros((H,), jnp.float32)}
    _L0_xattn_all = _L0_xattn_setup()
    _L0_xattn_in = {k: v for k, v in _L0_xattn_all.items() if k in ('q_w', 'q_b', 'kv_w', 'kv_b', 'out_w', 'out_b', 'postnorm_w', 'mlp_w1', 'mlp_b1', 'mlp_w2', 'mlp_b2')}
    del _L0_xattn_all

    def _L1_xattn_setup():
        import jax, jax.numpy as jnp
        import numpy as np
        H = 256
        NH = 32
        KVH = 8
        HD = H // NH
        GROUPS = NH // KVH
        EPS = 1e-06
        B, L, S = (4, 128, 128)

        def _gqa_forward(hidden_state, encoder_hidden_state, encoder_attention_mask, Wq, bq, Wk, bk, Wv, bv, Wo, bo, gamma, beta):
            b, l, _ = hidden_state.shape
            s = encoder_hidden_state.shape[1]
            q = hidden_state @ Wq + bq
            k = encoder_hidden_state @ Wk + bk
            v = encoder_hidden_state @ Wv + bv
            q = q.reshape(b, l, KVH, GROUPS, HD).transpose(0, 2, 3, 1, 4)
            k = k.reshape(b, s, KVH, HD).transpose(0, 2, 1, 3)
            v = v.reshape(b, s, KVH, HD).transpose(0, 2, 1, 3)
            scale = 1.0 / jnp.sqrt(jnp.asarray(HD, q.dtype))
            scores = jnp.einsum('bkgld,bksd->bkgls', q, k) * scale
            scores = scores + encoder_attention_mask[:, :, None, :, :]
            attn = jax.nn.softmax(scores, axis=-1)
            out = jnp.einsum('bkgls,bksd->bkgld', attn, v)
            out = out.transpose(0, 3, 1, 2, 4).reshape(b, l, H)
            out = out @ Wo + bo
            x = out + hidden_state
            mu = jnp.mean(x, axis=-1, keepdims=True)
            var = jnp.var(x, axis=-1, keepdims=True)
            return (x - mu) * jax.lax.rsqrt(var + EPS) * gamma + beta
        key = jax.random.key(seed)
        ks = jax.random.split(key, 12)
        sd = 0.02
        return {'hidden_state': jax.random.normal(ks[0], (B, L, H), jnp.float32), 'encoder_hidden_state': jax.random.normal(ks[1], (B, S, H), jnp.float32), 'encoder_attention_mask': jnp.zeros((B, 1, L, S), jnp.float32), 'Wq': jax.random.normal(ks[2], (H, H), jnp.float32) * sd, 'bq': jnp.zeros((H,), jnp.float32), 'Wk': jax.random.normal(ks[3], (H, KVH * HD), jnp.float32) * sd, 'bk': jnp.zeros((KVH * HD,), jnp.float32), 'Wv': jax.random.normal(ks[4], (H, KVH * HD), jnp.float32) * sd, 'bv': jnp.zeros((KVH * HD,), jnp.float32), 'Wo': jax.random.normal(ks[5], (H, H), jnp.float32) * sd, 'bo': jnp.zeros((H,), jnp.float32), 'gamma': jnp.ones((H,), jnp.float32), 'beta': jnp.zeros((H,), jnp.float32)}
    _L1_xattn_all = _L1_xattn_setup()
    _L1_xattn_in = {k: v for k, v in _L1_xattn_all.items() if k in ('Wq', 'bq', 'Wk', 'bk', 'Wv', 'bv', 'Wo', 'bo', 'gamma', 'beta')}
    del _L1_xattn_all

    def _L2_xattn_setup():
        import jax, jax.numpy as jnp
        import numpy as np
        N_HEAD = 32
        EPS = 1e-05

        def _ln(x, w, b):
            m = jnp.mean(x, axis=-1, keepdims=True)
            v = jnp.mean((x - m) ** 2, axis=-1, keepdims=True)
            return (x - m) * jax.lax.rsqrt(v + EPS) * w + b

        def _forward(x, state, i, ln1_w, ln1_b, ln2_w, ln2_b, maa_x, maa_w, maa_k, maa_v, maa_r, maa_g, maa_w1, maa_w2, time_decay, decay_w1, decay_w2, faaaa, Wr, Wk, Wv, Wg, Wo, gn_w, gn_b, fmaa_k, fmaa_r, fWk, fWr, fWv):
            B, L, C = x.shape
            H = N_HEAD
            S = C // H
            i0 = (2 + S) * i
            xa = _ln(x, ln1_w, ln1_b)
            sx = jnp.concatenate([state[:, i0 + 1][:, None], xa[:, :-1]], axis=1) - xa
            xxx = xa + sx * maa_x
            t = jnp.tanh(xxx @ maa_w1).reshape(B, L, 5, -1)
            m = jnp.einsum('blfd,fdc->blfc', t, maa_w2)
            mw, mk, mv, mr, mg = (m[:, :, j] for j in range(5))
            xw = xa + sx * (maa_w + mw)
            xk = xa + sx * (maa_k + mk)
            xv = xa + sx * (maa_v + mv)
            xr = xa + sx * (maa_r + mr)
            xg = xa + sx * (maa_g + mg)
            w = time_decay + jnp.tanh(xw @ decay_w1) @ decay_w2
            w = jnp.exp(-jnp.exp(w)).reshape(B, L, H, S)
            r = (xr @ Wr.T).reshape(B, L, H, S)
            k = (xk @ Wk.T).reshape(B, L, H, S)
            v = (xv @ Wv.T).reshape(B, L, H, S)
            g = jax.nn.silu(xg @ Wg.T)
            s0 = state[:, i0 + 2:i0 + 2 + S].reshape(B, H, S, S)

            def step(s, inp):
                k_l, v_l, w_l, r_l = inp
                a = k_l[..., :, None] * v_l[..., None, :]
                out = jnp.einsum('bhs,bhst->bht', r_l, faaaa * a + s)
                s_new = a + w_l[..., None] * s
                return (s_new, out)
            seq = tuple((z.transpose(1, 0, 2, 3) for z in (k, v, w, r)))
            _, outs = jax.lax.scan(step, s0, seq)
            y = outs.transpose(1, 0, 2, 3)
            gm = jnp.mean(y, axis=-1, keepdims=True)
            gv = jnp.mean((y - gm) ** 2, axis=-1, keepdims=True)
            y = ((y - gm) * jax.lax.rsqrt(gv + EPS)).reshape(B, L, C) * gn_w + gn_b
            x = x + y * g @ Wo.T
            xc = _ln(x, ln2_w, ln2_b)
            sxc = jnp.concatenate([state[:, i0][:, None], xc[:, :-1]], axis=1) - xc
            xk2 = xc + sxc * fmaa_k
            xr2 = xc + sxc * fmaa_r
            rr = jax.nn.sigmoid(xr2 @ fWr.T)
            kk = jnp.square(jax.nn.relu(xk2 @ fWk.T))
            x = x + rr * (kk @ fWv.T)
            return x
        key = jax.random.key(seed)
        B, L, C, H = (8, 64, 256, N_HEAD)
        S = C // H
        DM, DD = (32, 64)
        ks = jax.random.split(key, 32)
        n = lambda k, shp, s=1.0: jax.random.normal(k, shp, dtype=jnp.float32) * s
        u = lambda k, shp: jax.random.uniform(k, shp, dtype=jnp.float32)
        inp = {'x': n(ks[0], (B, L, C)), 'state': n(ks[1], (B, 2 + S, C), 0.1), 'i': 0, 'ln1_w': jnp.ones((C,), jnp.float32), 'ln1_b': jnp.zeros((C,), jnp.float32), 'ln2_w': jnp.ones((C,), jnp.float32), 'ln2_b': jnp.zeros((C,), jnp.float32), 'maa_x': u(ks[2], (C,)), 'maa_w': u(ks[3], (C,)), 'maa_k': u(ks[4], (C,)), 'maa_v': u(ks[5], (C,)), 'maa_r': u(ks[6], (C,)), 'maa_g': u(ks[7], (C,)), 'maa_w1': n(ks[8], (C, 5 * DM), 0.02), 'maa_w2': n(ks[9], (5, DM, C), 0.02), 'time_decay': n(ks[10], (C,), 0.5), 'decay_w1': n(ks[11], (C, DD), 0.02), 'decay_w2': n(ks[12], (DD, C), 0.02), 'faaaa': n(ks[13], (H, S, 1), 0.1), 'Wr': n(ks[14], (C, C), 0.02), 'Wk': n(ks[15], (C, C), 0.02), 'Wv': n(ks[16], (C, C), 0.02), 'Wg': n(ks[17], (C, C), 0.02), 'Wo': n(ks[18], (C, C), 0.02), 'gn_w': jnp.ones((C,), jnp.float32), 'gn_b': jnp.zeros((C,), jnp.float32), 'fmaa_k': u(ks[19], (C,)), 'fmaa_r': u(ks[20], (C,)), 'fWk': n(ks[21], (C, C), 0.02), 'fWr': n(ks[22], (C, C), 0.02), 'fWv': n(ks[23], (C, C), 0.02)}
        return inp
    _L2_xattn_all = _L2_xattn_setup()
    _L2_xattn_in = {k: v for k, v in _L2_xattn_all.items() if k in ('ln1_w', 'ln1_b', 'ln2_w', 'ln2_b', 'maa_x', 'maa_w', 'maa_k', 'maa_v', 'maa_r', 'maa_g', 'maa_w1', 'maa_w2', 'time_decay', 'decay_w1', 'decay_w2', 'faaaa', 'Wr', 'Wk', 'Wv', 'Wg', 'Wo', 'gn_w', 'gn_b', 'fmaa_k', 'fmaa_r', 'fWk', 'fWr', 'fWv')}
    del _L2_xattn_all

    def _L3_xattn_setup():
        import jax, jax.numpy as jnp
        import numpy as np
        HIDDEN = 256
        HEADS = 16
        HEAD_DIM = HIDDEN // HEADS
        LN_EPS = 1e-05
        GATE_INIT = 0.5

        def _layer_norm(x, gamma, beta):
            mu = jnp.mean(x, axis=-1, keepdims=True)
            var = jnp.mean(jnp.square(x - mu), axis=-1, keepdims=True)
            return (x - mu) * jax.lax.rsqrt(var + LN_EPS) * gamma + beta
        key = jax.random.key(seed)
        ks = jax.random.split(key, 8)
        B, T_TEXT, T_AUDIO = (4, 256, 1500)
        s = 0.02
        return {'hidden_states': jax.random.normal(ks[0], (B, T_TEXT, HIDDEN), jnp.float32), 'audio_kv': jax.random.normal(ks[1], (B, T_AUDIO, HIDDEN), jnp.float32), 'audio_attention_mask': jnp.ones((B, T_AUDIO), dtype=bool), 'Wq': jax.random.normal(ks[2], (HIDDEN, HIDDEN), jnp.float32) * s, 'Wk': jax.random.normal(ks[3], (HIDDEN, HIDDEN), jnp.float32) * s, 'Wv': jax.random.normal(ks[4], (HIDDEN, HIDDEN), jnp.float32) * s, 'Wo': jax.random.normal(ks[5], (HIDDEN, HIDDEN), jnp.float32) * s, 'ln_gamma': jnp.ones((HIDDEN,), jnp.float32), 'ln_beta': jnp.zeros((HIDDEN,), jnp.float32), 'gate': jnp.array([GATE_INIT], jnp.float32)}
    _L3_xattn_all = _L3_xattn_setup()
    _L3_xattn_in = {k: v for k, v in _L3_xattn_all.items() if k in ('Wq', 'Wk', 'Wv', 'Wo', 'ln_gamma', 'ln_beta', 'gate')}
    del _L3_xattn_all
    return {'x': x, 'ctx_2048': ctx_2048, 'mask_BxS2_ik0': mask_BxS2_ik0, 'mask_Bx1xSxS2_ff0': mask_Bx1xSxS2_ff0, 'mask_BxS2_bf1': mask_BxS2_bf1, 'L0_xattn_q_w': _L0_xattn_in['q_w'], 'L0_xattn_q_b': _L0_xattn_in['q_b'], 'L0_xattn_kv_w': _L0_xattn_in['kv_w'], 'L0_xattn_kv_b': _L0_xattn_in['kv_b'], 'L0_xattn_out_w': _L0_xattn_in['out_w'], 'L0_xattn_out_b': _L0_xattn_in['out_b'], 'L0_xattn_postnorm_w': _L0_xattn_in['postnorm_w'], 'L0_xattn_mlp_w1': _L0_xattn_in['mlp_w1'], 'L0_xattn_mlp_b1': _L0_xattn_in['mlp_b1'], 'L0_xattn_mlp_w2': _L0_xattn_in['mlp_w2'], 'L0_xattn_mlp_b2': _L0_xattn_in['mlp_b2'], 'L1_xattn_Wq': _L1_xattn_in['Wq'], 'L1_xattn_bq': _L1_xattn_in['bq'], 'L1_xattn_Wk': _L1_xattn_in['Wk'], 'L1_xattn_bk': _L1_xattn_in['bk'], 'L1_xattn_Wv': _L1_xattn_in['Wv'], 'L1_xattn_bv': _L1_xattn_in['bv'], 'L1_xattn_Wo': _L1_xattn_in['Wo'], 'L1_xattn_bo': _L1_xattn_in['bo'], 'L1_xattn_gamma': _L1_xattn_in['gamma'], 'L1_xattn_beta': _L1_xattn_in['beta'], 'L2_xattn_ln1_w': _L2_xattn_in['ln1_w'], 'L2_xattn_ln1_b': _L2_xattn_in['ln1_b'], 'L2_xattn_ln2_w': _L2_xattn_in['ln2_w'], 'L2_xattn_ln2_b': _L2_xattn_in['ln2_b'], 'L2_xattn_maa_x': _L2_xattn_in['maa_x'], 'L2_xattn_maa_w': _L2_xattn_in['maa_w'], 'L2_xattn_maa_k': _L2_xattn_in['maa_k'], 'L2_xattn_maa_v': _L2_xattn_in['maa_v'], 'L2_xattn_maa_r': _L2_xattn_in['maa_r'], 'L2_xattn_maa_g': _L2_xattn_in['maa_g'], 'L2_xattn_maa_w1': _L2_xattn_in['maa_w1'], 'L2_xattn_maa_w2': _L2_xattn_in['maa_w2'], 'L2_xattn_time_decay': _L2_xattn_in['time_decay'], 'L2_xattn_decay_w1': _L2_xattn_in['decay_w1'], 'L2_xattn_decay_w2': _L2_xattn_in['decay_w2'], 'L2_xattn_faaaa': _L2_xattn_in['faaaa'], 'L2_xattn_Wr': _L2_xattn_in['Wr'], 'L2_xattn_Wk': _L2_xattn_in['Wk'], 'L2_xattn_Wv': _L2_xattn_in['Wv'], 'L2_xattn_Wg': _L2_xattn_in['Wg'], 'L2_xattn_Wo': _L2_xattn_in['Wo'], 'L2_xattn_gn_w': _L2_xattn_in['gn_w'], 'L2_xattn_gn_b': _L2_xattn_in['gn_b'], 'L2_xattn_fmaa_k': _L2_xattn_in['fmaa_k'], 'L2_xattn_fmaa_r': _L2_xattn_in['fmaa_r'], 'L2_xattn_fWk': _L2_xattn_in['fWk'], 'L2_xattn_fWr': _L2_xattn_in['fWr'], 'L2_xattn_fWv': _L2_xattn_in['fWv'], 'L3_xattn_Wq': _L3_xattn_in['Wq'], 'L3_xattn_Wk': _L3_xattn_in['Wk'], 'L3_xattn_Wv': _L3_xattn_in['Wv'], 'L3_xattn_Wo': _L3_xattn_in['Wo'], 'L3_xattn_ln_gamma': _L3_xattn_in['ln_gamma'], 'L3_xattn_ln_beta': _L3_xattn_in['ln_beta'], 'L3_xattn_gate': _L3_xattn_in['gate']}

def reference(x, ctx_2048, mask_BxS2_ik0, mask_Bx1xSxS2_ff0, mask_BxS2_bf1, L0_xattn_q_w, L0_xattn_q_b, L0_xattn_kv_w, L0_xattn_kv_b, L0_xattn_out_w, L0_xattn_out_b, L0_xattn_postnorm_w, L0_xattn_mlp_w1, L0_xattn_mlp_b1, L0_xattn_mlp_w2, L0_xattn_mlp_b2, L1_xattn_Wq, L1_xattn_bq, L1_xattn_Wk, L1_xattn_bk, L1_xattn_Wv, L1_xattn_bv, L1_xattn_Wo, L1_xattn_bo, L1_xattn_gamma, L1_xattn_beta, L2_xattn_ln1_w, L2_xattn_ln1_b, L2_xattn_ln2_w, L2_xattn_ln2_b, L2_xattn_maa_x, L2_xattn_maa_w, L2_xattn_maa_k, L2_xattn_maa_v, L2_xattn_maa_r, L2_xattn_maa_g, L2_xattn_maa_w1, L2_xattn_maa_w2, L2_xattn_time_decay, L2_xattn_decay_w1, L2_xattn_decay_w2, L2_xattn_faaaa, L2_xattn_Wr, L2_xattn_Wk, L2_xattn_Wv, L2_xattn_Wg, L2_xattn_Wo, L2_xattn_gn_w, L2_xattn_gn_b, L2_xattn_fmaa_k, L2_xattn_fmaa_r, L2_xattn_fWk, L2_xattn_fWr, L2_xattn_fWv, L3_xattn_Wq, L3_xattn_Wk, L3_xattn_Wv, L3_xattn_Wo, L3_xattn_ln_gamma, L3_xattn_ln_beta, L3_xattn_gate):
    import jax
    import jax.numpy as jnp

    def _L0_xattn_ref(x, latents, attention_mask, q_w, q_b, kv_w, kv_b, out_w, out_b, postnorm_w, mlp_w1, mlp_b1, mlp_w2, mlp_b2):
        import jax, jax.numpy as jnp
        import numpy as np
        B, P, K, H, NH = (4, 256, 32, 256, 16)
        DH = H // NH
        EPS = 1e-06

        def rmsnorm(x, w):
            var = jnp.mean(jnp.square(x), axis=-1, keepdims=True)
            return x * jax.lax.rsqrt(var + EPS) * w
        b, p, _ = x.shape
        k_len = latents.shape[1]
        residual = latents
        h = jnp.concatenate([x, latents], axis=1)
        q = (latents @ q_w + q_b).reshape(b, k_len, NH, DH)
        kv = (h @ kv_w + kv_b).reshape(b, p + k_len, NH, DH, 2)
        kmat, v = (kv[..., 0], kv[..., 1])
        attn = jnp.einsum('bkhd,bnhd->bhkn', q, kmat) / DH
        full_mask = jnp.concatenate([attention_mask.astype(bool), jnp.ones((b, k_len), bool)], axis=-1)
        attn = jnp.where(full_mask[:, None, None, :], attn, -jnp.inf)
        attn = jax.nn.softmax(attn.astype(jnp.float32), axis=-1).astype(q.dtype)
        attn_out = jnp.einsum('bhkn,bnhd->bkhd', attn, v).reshape(b, k_len, H)
        attn_out = attn_out @ out_w + out_b + residual
        out = rmsnorm(attn_out, postnorm_w)
        out = jax.nn.gelu(out @ mlp_w1 + mlp_b1) @ mlp_w2 + mlp_b2
        return out + residual

    def _L1_xattn_ref(hidden_state, encoder_hidden_state, encoder_attention_mask, Wq, bq, Wk, bk, Wv, bv, Wo, bo, gamma, beta):
        import jax, jax.numpy as jnp
        import numpy as np
        H = 256
        NH = 32
        KVH = 8
        HD = H // NH
        GROUPS = NH // KVH
        EPS = 1e-06
        B, L, S = (4, 128, 128)

        def _gqa_forward(hidden_state, encoder_hidden_state, encoder_attention_mask, Wq, bq, Wk, bk, Wv, bv, Wo, bo, gamma, beta):
            b, l, _ = hidden_state.shape
            s = encoder_hidden_state.shape[1]
            q = hidden_state @ Wq + bq
            k = encoder_hidden_state @ Wk + bk
            v = encoder_hidden_state @ Wv + bv
            q = q.reshape(b, l, KVH, GROUPS, HD).transpose(0, 2, 3, 1, 4)
            k = k.reshape(b, s, KVH, HD).transpose(0, 2, 1, 3)
            v = v.reshape(b, s, KVH, HD).transpose(0, 2, 1, 3)
            scale = 1.0 / jnp.sqrt(jnp.asarray(HD, q.dtype))
            scores = jnp.einsum('bkgld,bksd->bkgls', q, k) * scale
            scores = scores + encoder_attention_mask[:, :, None, :, :]
            attn = jax.nn.softmax(scores, axis=-1)
            out = jnp.einsum('bkgls,bksd->bkgld', attn, v)
            out = out.transpose(0, 3, 1, 2, 4).reshape(b, l, H)
            out = out @ Wo + bo
            x = out + hidden_state
            mu = jnp.mean(x, axis=-1, keepdims=True)
            var = jnp.var(x, axis=-1, keepdims=True)
            return (x - mu) * jax.lax.rsqrt(var + EPS) * gamma + beta
        return _gqa_forward(hidden_state, encoder_hidden_state, encoder_attention_mask, Wq, bq, Wk, bk, Wv, bv, Wo, bo, gamma, beta)

    def _L2_xattn_ref(x, state, i, ln1_w, ln1_b, ln2_w, ln2_b, maa_x, maa_w, maa_k, maa_v, maa_r, maa_g, maa_w1, maa_w2, time_decay, decay_w1, decay_w2, faaaa, Wr, Wk, Wv, Wg, Wo, gn_w, gn_b, fmaa_k, fmaa_r, fWk, fWr, fWv):
        import jax, jax.numpy as jnp
        import numpy as np
        N_HEAD = 32
        EPS = 1e-05

        def _ln(x, w, b):
            m = jnp.mean(x, axis=-1, keepdims=True)
            v = jnp.mean((x - m) ** 2, axis=-1, keepdims=True)
            return (x - m) * jax.lax.rsqrt(v + EPS) * w + b

        def _forward(x, state, i, ln1_w, ln1_b, ln2_w, ln2_b, maa_x, maa_w, maa_k, maa_v, maa_r, maa_g, maa_w1, maa_w2, time_decay, decay_w1, decay_w2, faaaa, Wr, Wk, Wv, Wg, Wo, gn_w, gn_b, fmaa_k, fmaa_r, fWk, fWr, fWv):
            B, L, C = x.shape
            H = N_HEAD
            S = C // H
            i0 = (2 + S) * i
            xa = _ln(x, ln1_w, ln1_b)
            sx = jnp.concatenate([state[:, i0 + 1][:, None], xa[:, :-1]], axis=1) - xa
            xxx = xa + sx * maa_x
            t = jnp.tanh(xxx @ maa_w1).reshape(B, L, 5, -1)
            m = jnp.einsum('blfd,fdc->blfc', t, maa_w2)
            mw, mk, mv, mr, mg = (m[:, :, j] for j in range(5))
            xw = xa + sx * (maa_w + mw)
            xk = xa + sx * (maa_k + mk)
            xv = xa + sx * (maa_v + mv)
            xr = xa + sx * (maa_r + mr)
            xg = xa + sx * (maa_g + mg)
            w = time_decay + jnp.tanh(xw @ decay_w1) @ decay_w2
            w = jnp.exp(-jnp.exp(w)).reshape(B, L, H, S)
            r = (xr @ Wr.T).reshape(B, L, H, S)
            k = (xk @ Wk.T).reshape(B, L, H, S)
            v = (xv @ Wv.T).reshape(B, L, H, S)
            g = jax.nn.silu(xg @ Wg.T)
            s0 = state[:, i0 + 2:i0 + 2 + S].reshape(B, H, S, S)

            def step(s, inp):
                k_l, v_l, w_l, r_l = inp
                a = k_l[..., :, None] * v_l[..., None, :]
                out = jnp.einsum('bhs,bhst->bht', r_l, faaaa * a + s)
                s_new = a + w_l[..., None] * s
                return (s_new, out)
            seq = tuple((z.transpose(1, 0, 2, 3) for z in (k, v, w, r)))
            _, outs = jax.lax.scan(step, s0, seq)
            y = outs.transpose(1, 0, 2, 3)
            gm = jnp.mean(y, axis=-1, keepdims=True)
            gv = jnp.mean((y - gm) ** 2, axis=-1, keepdims=True)
            y = ((y - gm) * jax.lax.rsqrt(gv + EPS)).reshape(B, L, C) * gn_w + gn_b
            x = x + y * g @ Wo.T
            xc = _ln(x, ln2_w, ln2_b)
            sxc = jnp.concatenate([state[:, i0][:, None], xc[:, :-1]], axis=1) - xc
            xk2 = xc + sxc * fmaa_k
            xr2 = xc + sxc * fmaa_r
            rr = jax.nn.sigmoid(xr2 @ fWr.T)
            kk = jnp.square(jax.nn.relu(xk2 @ fWk.T))
            x = x + rr * (kk @ fWv.T)
            return x
        return _forward(x, state, i, ln1_w, ln1_b, ln2_w, ln2_b, maa_x, maa_w, maa_k, maa_v, maa_r, maa_g, maa_w1, maa_w2, time_decay, decay_w1, decay_w2, faaaa, Wr, Wk, Wv, Wg, Wo, gn_w, gn_b, fmaa_k, fmaa_r, fWk, fWr, fWv)

    def _L3_xattn_ref(hidden_states, audio_kv, audio_attention_mask, Wq, Wk, Wv, Wo, ln_gamma, ln_beta, gate):
        import jax, jax.numpy as jnp
        import numpy as np
        HIDDEN = 256
        HEADS = 16
        HEAD_DIM = HIDDEN // HEADS
        LN_EPS = 1e-05
        GATE_INIT = 0.5

        def _layer_norm(x, gamma, beta):
            mu = jnp.mean(x, axis=-1, keepdims=True)
            var = jnp.mean(jnp.square(x - mu), axis=-1, keepdims=True)
            return (x - mu) * jax.lax.rsqrt(var + LN_EPS) * gamma + beta
        B, Tt, D = hidden_states.shape
        Ta = audio_kv.shape[1]
        scale = HEAD_DIM ** (-0.5)
        a = _layer_norm(audio_kv, ln_gamma, ln_beta)
        Q = (hidden_states @ Wq.T).reshape(B, Tt, HEADS, HEAD_DIM).transpose(0, 2, 1, 3)
        K = (a @ Wk.T).reshape(B, Ta, HEADS, HEAD_DIM).transpose(0, 2, 1, 3)
        V = (a @ Wv.T).reshape(B, Ta, HEADS, HEAD_DIM).transpose(0, 2, 1, 3)
        scores = jnp.einsum('bhtd,bhsd->bhts', Q, K) * scale
        mask = audio_attention_mask[:, None, None, :]
        scores = jnp.where(mask, scores, jnp.float32(-jnp.inf))
        attn = jax.nn.softmax(scores, axis=-1)
        out = jnp.einsum('bhts,bhsd->bhtd', attn, V)
        out = out.transpose(0, 2, 1, 3).reshape(B, Tt, D)
        out = out @ Wo.T
        return hidden_states + jnp.tanh(gate) * out
    x = _L0_xattn_ref(ctx_2048, x, mask_BxS2_ik0, L0_xattn_q_w, L0_xattn_q_b, L0_xattn_kv_w, L0_xattn_kv_b, L0_xattn_out_w, L0_xattn_out_b, L0_xattn_postnorm_w, L0_xattn_mlp_w1, L0_xattn_mlp_b1, L0_xattn_mlp_w2, L0_xattn_mlp_b2)
    x = _L1_xattn_ref(x, ctx_2048, mask_Bx1xSxS2_ff0, L1_xattn_Wq, L1_xattn_bq, L1_xattn_Wk, L1_xattn_bk, L1_xattn_Wv, L1_xattn_bv, L1_xattn_Wo, L1_xattn_bo, L1_xattn_gamma, L1_xattn_beta)
    x = _L2_xattn_ref(x, ctx_2048, 0, L2_xattn_ln1_w, L2_xattn_ln1_b, L2_xattn_ln2_w, L2_xattn_ln2_b, L2_xattn_maa_x, L2_xattn_maa_w, L2_xattn_maa_k, L2_xattn_maa_v, L2_xattn_maa_r, L2_xattn_maa_g, L2_xattn_maa_w1, L2_xattn_maa_w2, L2_xattn_time_decay, L2_xattn_decay_w1, L2_xattn_decay_w2, L2_xattn_faaaa, L2_xattn_Wr, L2_xattn_Wk, L2_xattn_Wv, L2_xattn_Wg, L2_xattn_Wo, L2_xattn_gn_w, L2_xattn_gn_b, L2_xattn_fmaa_k, L2_xattn_fmaa_r, L2_xattn_fWk, L2_xattn_fWr, L2_xattn_fWv)
    x = _L3_xattn_ref(x, ctx_2048, mask_BxS2_bf1, L3_xattn_Wq, L3_xattn_Wk, L3_xattn_Wv, L3_xattn_Wo, L3_xattn_ln_gamma, L3_xattn_ln_beta, L3_xattn_gate)
    return x

_drawn_inputs = setup_inputs


def setup_inputs(seed=0):
    import zlib

    import numpy as np

    out = dict(_drawn_inputs(seed))
    spreads = {'L0_xattn_q_b': (0.0, 0.8),
     'L0_xattn_kv_b': (0.0, 0.8),
     'L0_xattn_out_b': (0.0, 0.649),
     'L0_xattn_postnorm_w': (1.0, 0.6),
     'L0_xattn_mlp_b1': (0.0, 0.1),
     'L0_xattn_mlp_b2': (0.0, 0.1),
     'L1_xattn_bq': (0.0, 0.8),
     'L1_xattn_bk': (0.0, 2.0),
     'L1_xattn_bv': (0.0, 0.1),
     'L1_xattn_bo': (0.0, 0.1),
     'L1_xattn_gamma': (1.0, 0.2),
     'L1_xattn_beta': (0.0, 0.1),
     'L2_xattn_ln1_w': (1.0, 0.6),
     'L2_xattn_ln1_b': (0.0, 0.573),
     'L2_xattn_ln2_w': (1.0, 0.6),
     'L2_xattn_ln2_b': (0.0, 0.8),
     'L2_xattn_gn_w': (1.0, 0.6),
     'L2_xattn_gn_b': (0.0, 0.8),
     'L3_xattn_ln_gamma': (1.0, 0.6),
     'L3_xattn_ln_beta': (0.0, 2.0)}
    factors = {'L0_xattn_q_w': 8.0,
     'L0_xattn_kv_w': 8.0,
     'L0_xattn_out_w': 8.0,
     'L1_xattn_Wq': 8.0,
     'L1_xattn_Wk': 8.0,
     'L2_xattn_maa_x': 8.0,
     'L2_xattn_maa_w': 8.0,
     'L2_xattn_maa_w1': 8.0,
     'L2_xattn_maa_w2': 8.0,
     'L2_xattn_time_decay': 3.579,
     'L2_xattn_decay_w1': 8.0,
     'L2_xattn_decay_w2': 8.0,
     'L2_xattn_faaaa': 7.336,
     'L2_xattn_fmaa_k': 7.884,
     'L2_xattn_fmaa_r': 8.0,
     'L2_xattn_fWk': 4.447,
     'L2_xattn_fWr': 8.0,
     'L2_xattn_fWv': 4.106,
     'L3_xattn_Wq': 64.0,
     'L3_xattn_Wk': 64.0,
     'L3_xattn_Wv': 8.0,
     'L3_xattn_Wo': 8.0}
    for name, (base, spread) in spreads.items():
        noise = np.random.default_rng([zlib.crc32(name.encode()), seed]).standard_normal(out[name].shape)
        drawn = base * np.exp(spread * noise) if base else spread * noise
        out[name] = jnp.asarray(drawn.astype(out[name].dtype))
    for name, factor in factors.items():
        out[name] = (out[name] * factor).astype(out[name].dtype)
    return out
```

```python
from contextlib import ExitStack

import concourse.bass as bass
from concourse import mybir

F32 = mybir.dt.float32
I32 = mybir.dt.int32
U8 = mybir.dt.uint8
ALU = mybir.AluOpType
ACT = mybir.ActivationFunctionType
AX = mybir.AxisListType

P = 128
BATCH = 16
PAIR = 2
TURNS = BATCH // PAIR
C = 256
CT = C // P
T = PAIR * P
MLP = 4 * C
MT = MLP // P
LORA = 32
DECAY = 64
WEIGHTS_IN = 7 * 16
BIG = 1e30
HUGE = 3e38

W_L0 = dict(q=(CT, C), k=(CT, C), v=(CT, C), o=(CT, C), w1=(CT, MLP), w2=(MT, C))
W_L1 = dict(q=(CT, C), k=(CT, P), v=(CT, 64), o=(CT, C))
W_L2 = dict(m1=(CT, 5 * LORA), d1=(CT, DECAY), r=(CT, C), k=(CT, C), v=(CT, C), g=(CT, C), o=(CT, C),
            fr=(CT, C), fk=(CT, C), fv=(CT, C), m2=(1, C), m2g=(1, C), d2=(1, C))
W_L3 = dict(q=(CT, C), k=(CT, C), v=(CT, C), o=(CT, C))
COLS = ["q0_b", "k0_b", "b1_0", "b1_1", "b1_2", "b1_3", "post_w", "q1_b", "k1_b", "ln1_w", "ln1_b", "maa_x",
        "maa_w", "maa_k", "maa_v", "maa_r", "maa_g", "decay", "bonus", "gn_w", "gn_b", "ln2_w", "ln2_b",
        "fmaa_k", "fmaa_r", "ln3_w", "ln3_b"]
ROWS = ["v0_b", "o0_b", "b2", "o1_b", "gamma", "beta", "v1_b"]

JOBS = [("xT", "A"), ("cT", "D"), ("q0", "D"), ("k0c", "A"), ("k0l", "A"), ("v0c", "D"), ("v0l", "D"),
        ("aT", "A"), ("k3", "A"), ("v3", "D"),
        ("sum0", "A"), ("o0", "D"), ("nT", "D"), ("u0", "A"), ("u1", "A"), ("u2", "A"), ("u3", "A"), ("m2", "D"),
        ("x1T", "A"), ("q1", "D"), ("k1", "A"), ("v1", "D"),
        ("sum1", "A"), ("o1", "D"), ("xaT", "A"), ("t", "A"),
        ("mw", "D"), ("mk", "D"), ("mv", "D"), ("mr", "D"), ("mg", "D"), ("d1", "A"), ("d2", "A"),
        ("k2", "A"), ("v2", "D"), ("r2", "A"), ("g2", "A"), ("bonus", "D")] + \
       [(f"vr{n}", "D") for n in range(8)] + \
       [("yT", "A"), ("ynT", "A"), ("o2", "D"), ("xcT", "A"), ("fr", "A"), ("fk", "A"), ("fv", "D"),
        ("x4T", "A"), ("q3", "A"), ("sum3", "A"), ("o3", "D")]
BANKS = 3
NAMES = [n for n, _ in JOBS]
EVACS = {e: [n for n, by in JOBS if by == e] for e in "AD"}

NJ = {0: 16, 1: 16, 3: 8}
FIRST = {0: 0, 1: 16, 3: 32}
NJOBS = sum(NJ.values())


def attention_jobs(layer):
    if layer == 0:
        return [(ct, bb, j) for ct in range(CT) for bb in range(PAIR) for j in range(0, 8, 2)]
    if layer == 3:
        return [(ct, bb, j) for bb in range(PAIR) for ct in range(CT) for j in (0, 4)]
    return [(gp, bb, half * 8 + ct * 4) for bb in range(PAIR) for ct in range(CT)
            for gp in range(2) for half in range(2)]


PER_TURN = dict(
    x_in=16, c_in=16, m0_in=16, m1_in=16, m3_in=16, s0_in=32,
    product=len(JOBS), emptied_A=len(EVACS["A"]), emptied_D=len(EVACS["D"]),
    scores=NJOBS, masked=NJOBS, exps=NJOBS, turned=NJOBS, turned_D=NJOBS // 2, turned_A=NJOBS // 2,
    pv=NJOBS, summed=3, attn=3, mask_bias=3, keys0=16, keys1=16, keys3=16,
    stats3=1, stats1=1, stats2=1, stats4=1, rstd3=1, rstd0=1, rstd1=1, rstd2=1, rstd4=1, rstd_g=1,
    cn=1, xo=1, xb2=1, ssq=1, hn=1, xb1=1, n1=1, x2=1, n2=1,
    xxx=1, xf=5, w=1, ruk=1, seed=8, scan=8, z=8,
    gathered=8, y=1, yc=1, sq=1, gvar=1, yn=1, y2=1, n4=1, xk2=1, xr2=1, kk=1, x4=1, out_done=16,
    state_cols=1, halves=4, inverse=3, first_token=2, shift=2, gsum=1, veps=6, gamma=1)
NORMS = [3, 1, 2, 4]
POWERS = ["rstd3", "rstd0", "rstd1", "rstd2", "rstd_g", "rstd4"]
AHEAD = {"attn", "cn", "emptied_A", "emptied_D", "exps", "keys3", "mask_bias", "masked", "out_done", "pv",
         "seed", "turned", "turned_A", "turned_D", "xb2"}


def build(nc, x, ctx, m0, m1, m3, wl0, wl1, wl2, wl3, cols, rows, gate, out):
    x = x.rearrange("(n b) t c -> n t b c", b=PAIR)
    out = out.rearrange("(n b) t c -> n t b c", b=PAIR)
    ctx_in = ctx.rearrange("(n b) t c -> n t b c", b=PAIR)
    state_in = ctx.rearrange("(n b) t c -> n b (t c)", b=PAIR)[:, :, 2 * C:10 * C]\
        .rearrange("n b (k p j) -> n b p k j", k=CT, j=8)
    m0 = m0.rearrange("(n b) s -> n b s", b=PAIR)
    m3 = m3.rearrange("(n b) s -> n b s", b=PAIR)
    m1 = m1.rearrange("(n b) l s -> n l b s", b=PAIR)
    with ExitStack() as st:
        def sb(name, shape, dt=F32):
            return st.enter_context(nc.sbuf_tensor(name, [P] + shape, dt))

        def sem(name):
            return st.enter_context(nc.semaphore(name))

        def weights(prefix, table, total):
            tile = sb(prefix, [total])
            at, views = 0, {}
            for n, (kt, width) in table.items():
                views[n] = tile[:, at:at + kt * width].rearrange("p (k n) -> p k n", k=kt)
                at += kt * width
            assert at == total
            return tile, views

        def width(table):
            return sum(a * b for a, b in table.values())

        W0t, W0 = weights("w_l0", W_L0, width(W_L0))
        W1t, W1 = weights("w_l1", W_L1, width(W_L1))
        W2t, W2 = weights("w_l2", W_L2, width(W_L2))
        W3t, W3 = weights("w_l3", W_L3, width(W_L3))
        colt = sb("colt", [len(COLS), CT])
        rowt = sb("rowt", [len(ROWS), C])
        col = {n: [colt[:, k, ct:ct + 1] for ct in range(CT)] for k, n in enumerate(COLS)}
        row = {n: rowt[:, k, :] for k, n in enumerate(ROWS)}
        gate_t = sb("gate_t", [2])
        ident = sb("ident", [P])
        ones8 = sb("ones8", [P])
        head8 = sb("head8", [16])
        head16 = sb("head16", [2, 4])
        lane8 = sb("lane8", [8])
        spread = sb("spread", [8, P])
        gather = sb("gather", [8, P])
        minus_half = sb("minus_half", [64])

        slot = [sb(f"slot{n}", [512]) for n in range(1, 23)]

        def tm(n):
            return slot[n - 1][:, :].rearrange("p (b c) -> p b c", b=PAIR)

        def cm(n):
            return slot[n - 1][:, :].rearrange("p (k t) -> p k t", k=CT)

        X, CX = tm(1), tm(2)
        xT, cT, aT, CN = cm(3), cm(4), cm(5), tm(6)
        Q = cm(7)
        XO, XB2, H, HN, nT, X1, XB1 = tm(8), tm(9), tm(10), tm(11), cm(12), tm(13), tm(14)
        x1T, attnT, sumT, Y1, X2 = cm(3), cm(15), cm(16), tm(8), tm(9)
        sx, xxx, tT = cm(18), cm(12), cm(19)
        tmp = [cm(20), cm(21)]
        xf = [cm(3), cm(4), cm(5), cm(6), cm(10)]
        dT, w0 = cm(13), cm(12)
        rT, kT, vT, gT = cm(7), cm(14), cm(15), cm(16)
        ruk, Dv, y, yt, yc, sq, yn = cm(3), cm(4), cm(5), tm(6), tm(10), tm(20), tm(21)
        y2a, y2, X3, sxc, xk2, xr2 = cm(12), cm(13), tm(8), cm(18), cm(19), cm(20)
        rr, kk0, kk, tmpv, X4, x4T, OUT = tm(21), cm(10), cm(6), tm(5), tm(9), cm(3), tm(22)
        B16 = tm(20)
        EW = tm(11)
        shifted = sb("shifted", [CT, PAIR, P + 1])
        wP = sb("wP", [CT, PAIR, P + 1])
        state_cols = sb("state_cols", [CT, PAIR, 2])
        k0T = sb("k0T", [CT, PAIR, 2 * P])
        k1T = sb("k1T", [T])
        k3T = sb("k3T", [CT, T])
        keysA = sb("keysA", [4096])
        keysB = sb("keysB", [4096])
        hT = keysB[:, 0:MT * T].rearrange("p (m t) -> p m t", m=MT)
        V0 = sb("V0", [2, PAIR, 2, C])
        V1 = sb("V1", [PAIR, 4, C])
        V3 = sb("V3", [PAIR, 2, C])
        m0i = sb("m0i", [PAIR, P], I32)
        m3i = sb("m3i", [PAIR, P], U8)
        mb0 = sb("mb0", [PAIR, 2 * P])
        mb1 = sb("mb1", [PAIR, P])
        mb3 = sb("mb3", [PAIR, P])
        s0 = sb("s0", [PAIR, CT, 8])
        S = sb("S", [2, 512])
        E = sb("E", [2, 512])
        ET = sb("ET", [4, 4, P])
        nmax = sb("nmax", [4, 4])
        esum = {l: sb(f"esum{l}", [PAIR, 32]) for l in (0, 1, 3)}
        einv = {l: sb(f"einv{l}", [PAIR, 32]) for l in (0, 1, 3)}
        n_scan = 4 * PAIR * (P + 1)
        kv = keysA[:, 0:n_scan].rearrange("p (u a b t) -> p u a b t", u=2, a=2, b=PAIR)
        SS = keysA[:, n_scan:2 * n_scan].rearrange("p (u a b t) -> p u a b t", u=2, a=2, b=PAIR)
        Z = keysA[:, 2 * n_scan:2 * n_scan + 4 * T].rearrange("p (u a t) -> p u a t", u=2, a=2)
        bst = sb("bst", [PAIR, 6])
        mv = {n: sb(f"mv{n}", [PAIR, 2]) for n in (3, 1, 2, 4)}
        rs = {n: sb(f"rs{n}", [PAIR]) for n in (0, 3, 1, 2, 4)}
        veps = sb("veps", [64])
        ssq = sb("ssq", [PAIR])
        gsum = sb("gsum", [64])
        gvar = sb("gvar", [64])
        grs = sb("grs", [64])
        junk = tm(21)

        ring = [st.enter_context(nc.psum_tensor(f"ring{n}", [P, 512], F32)) for n in range(BANKS)]
        psS = [st.enter_context(nc.psum_tensor(f"psS{n}", [P, 512], F32)) for n in range(2)]
        psT = [st.enter_context(nc.psum_tensor(f"psT{n}", [P, 4, P], F32)) for n in range(2)]
        psO = st.enter_context(nc.psum_tensor("psO", [P, CT, T], F32))

        sems = {n: sem("s_" + n) for n in PER_TURN}
        s_w = sem("weights_in")
        s_const = sem("s_const")
        s_setup = sem("s_setup")
        s_setup_d = sem("s_setup_d")
        waited_in, i_reg = {}, {}

        def turn(i, name, k=None):
            return i * PER_TURN[name] + (PER_TURN[name] if k is None else k) + (name in AHEAD)

        def before(i, name):
            assert name in AHEAD
            return i * PER_TURN[name] + 1

        def bank(name):
            return ring[NAMES.index(name) % BANKS][:, :].rearrange("p (a b) -> p a b", a=2)

        def made(i, name):
            return turn(i, "product", NAMES.index(name) + 1)

        def leaves(name):
            return sems["emptied_" + dict(JOBS)[name]]

        def left(i, name):
            by = dict(JOBS)[name]
            return turn(i, "emptied_" + by, EVACS[by].index(name) + 1)

        def count_of(name):
            by = dict(JOBS)[name]
            return "emptied_" + by, EVACS[by].index(name) + 1

        def counted(eng, *signals):
            for (n, k), reg in zip(signals, waited_in[eng]):
                eng.reg_mul(reg, i_reg[eng], PER_TURN[n])
                eng.reg_add(reg, reg, (PER_TURN[n] if k is None else k) + (n in AHEAD))
            return waited_in[eng]

        block = st.enter_context(nc.Block())

        @block.sync
        def _(sp):
            sp.dma_start(W0t[:, :], wl0).then_inc(s_w, 16)
            sp.dma_start(colt[:, :, :], cols).then_inc(s_w, 16)
            sp.dma_start(rowt[:, :, :], rows.partition_broadcast(P)).then_inc(s_w, 16)
            sp.dma_start(gate_t[:, 0:1], gate.partition_broadcast(P)).then_inc(s_w, 16)
            sp.dma_start(W3t[:, :], wl3).then_inc(s_w, 16)
            sp.dma_start(W1t[:, :], wl1).then_inc(s_w, 16)
            sp.dma_start(W2t[:, :], wl2).then_inc(s_w, 16)
            with sp.Fori(0, TURNS) as i:
                sp.wait_ge(sems["xb2"], before(i, "xb2"))
                sp.dma_start(X, x[i]).then_inc(sems["x_in"], 16)
                sp.wait_ge(sems["cn"], before(i, "cn"))
                sp.dma_start(CX, ctx_in[i]).then_inc(sems["c_in"], 16)
                sp.wait_ge(sems["mask_bias"], before(i, "mask_bias"))
                sp.dma_start(m0i[:, :, :], m0[i].partition_broadcast(P)).then_inc(sems["m0_in"], 16)
                sp.dma_start(m3i[:, :, :], m3[i].partition_broadcast(P)).then_inc(sems["m3_in"], 16)
                sp.wait_ge(sems["masked"], before(i, "masked"))
                sp.dma_start(mb1[:, :, :], m1[i]).then_inc(sems["m1_in"], 16)
                sp.wait_ge(sems["seed"], before(i, "seed"))
                for bb in range(PAIR):
                    sp.dma_start(s0[:, bb, :, :], state_in[i][bb]).then_inc(sems["s0_in"], 16)
                sp.wait_ge(leaves("o3"), left(i, "o3"))
                sp.dma_start(out[i], OUT).then_inc(sems["out_done"], 16)
            sp.wait_ge(sems["out_done"], TURNS * 16 + 1)

        @block.tensor
        def _(pe):
            pe.wait_ge(s_setup_d, 4)
            pe.wait_ge(s_w, WEIGHTS_IN)

            with pe.Fori(0, TURNS) as i:
                def start(name):
                    n = NAMES.index(name)
                    if n >= BANKS:
                        pe.wait_ge(leaves(NAMES[n - BANKS]), left(i, NAMES[n - BANKS]))
                    else:
                        pe.wait_ge(sems["emptied_A"], before(i, "emptied_A"))
                        pe.wait_ge(sems["emptied_D"], before(i, "emptied_D"))
                    return bank(name)

                def transposes(name, src):
                    b = start(name)
                    for a in range(2):
                        for c in range(2):
                            m = pe.transpose(b[:, c, a * P:(a + 1) * P], src[:, a, c * P:(c + 1) * P], ident[:, :])
                    m.then_inc(sems["product"], 1)

                def channel_major(name, w, src, tiles=2, m0=0):
                    b = start(name)
                    kt = w.shape[1]
                    for a in range(tiles):
                        for k in range(kt):
                            m = pe.matmul(b[:, a, :], w[:, k, m0 + a * P:m0 + (a + 1) * P], src[:, k, :],
                                          start=(k == 0), stop=(k == kt - 1))
                    m.then_inc(sems["product"], 1)

                def token_major(name, src, w):
                    b = start(name)
                    kt, n = w.shape[1], w.shape[2]
                    for bb in range(PAIR):
                        for k in range(kt):
                            m = pe.matmul(b[:, bb, 0:n], src[:, k, bb * P:(bb + 1) * P], w[:, k, :],
                                          start=(k == 0), stop=(k == kt - 1))
                    m.then_inc(sems["product"], 1)

                def attention(layer, keys, V):
                    jobs = attention_jobs(layer)
                    f = FIRST[layer]

                    def scores(n):
                        t, bb, j = jobs[n]
                        if f + n >= 2:
                            pe.wait_ge(sems["masked"], turn(i, "masked", f + n - 1))
                        else:
                            pe.wait_ge(sems["masked"], before(i, "masked"))
                        if layer == 0:
                            pe.wait_ge(sems["keys0"], turn(i, "keys0", t * 8 + j + 2))
                            rhs = keys[t][:, j:j + 2, bb, :]
                        else:
                            pe.wait_ge(sems[f"keys{layer}"], turn(i, f"keys{layer}", j + 4 if layer == 1 else t * 8 + j + 4))
                            rhs = keys[t][:, j:j + 4, bb * P:(bb + 1) * P]
                        pe.matmul(psS[(f + n) % 2][:, :], Q[:, t, bb * P:(bb + 1) * P], rhs,
                                       start=True, stop=True).then_inc(sems["scores"], 1)

                    def turn_over(n):
                        g = f + n
                        pe.wait_ge(sems["exps"], turn(i, "exps", g + 1))
                        if g >= 2:
                            pe.wait_ge(sems["turned_D" if g % 2 == 0 else "turned_A"], turn(i, "turned_D" if g % 2 == 0 else "turned_A", g // 2))
                        else:
                            pe.wait_ge(sems["turned_D" if g % 2 == 0 else "turned_A"], before(i, "turned_D" if g % 2 == 0 else "turned_A"))
                        for k in range(4):
                            m = pe.transpose(psT[g % 2][:, k, :], E[:, g % 2, k * P:(k + 1) * P], ident[:, :])
                        m.then_inc(sems["turned"], 1)

                    def weigh(n):
                        g = f + n
                        t, bb, j = jobs[n]
                        cols_ = slice(bb * P, (bb + 1) * P)
                        if layer == 0 and n % 2 == 0:
                            return
                        pe.wait_ge(sems["turned_D"], turn(i, "turned_D", (g + 2) // 2))
                        pe.wait_ge(sems["turned_A"], turn(i, "turned_A", (g + 1) // 2))
                        if layer == 0:
                            par = j // 4
                            for sblk in range(2):
                                for s in range(4):
                                    e = ET[:, (g - 1 + s // 2) % 4, (s % 2) * 2 + sblk, :]
                                    m = pe.matmul(psO[32 * s:32 * s + 32, t, cols_],
                                                  V[:, sblk, bb, par, t * P + 32 * s:t * P + 32 * s + 32], e,
                                                  start=(par == 0 and sblk == 0), stop=(par == 1 and sblk == 1),
                                                  skip_group_check=True)
                            m.then_inc(sems["pv"], 2)
                            return
                        if layer == 3:
                            ct, kept, last = t, j // 4, 1
                        else:
                            ct, kept, last = (j % 8) // 4, 2 * t + j // 8, 3
                        for s in range(4):
                            m = pe.matmul(psO[32 * s:32 * s + 32, ct, cols_],
                                          V[:, bb, kept, ct * P + 32 * s:ct * P + 32 * s + 32],
                                          ET[:, g % 4, s, :], start=(kept == 0), stop=(kept == last),
                                          skip_group_check=True)
                        m.then_inc(sems["pv"], 1)

                    if layer == 0:
                        pe.wait_ge(sems["attn"], before(i, "attn"))
                    else:
                        pe.wait_ge(sems["attn"], turn(i, "attn", 1 if layer == 1 else 2))
                    for n in range(len(jobs) + 4):
                        if n < len(jobs):
                            scores(n)
                        if 0 <= n - 2 < len(jobs):
                            turn_over(n - 2)
                        if 0 <= n - 4 < len(jobs):
                            weigh(n - 4)
                    b = start(f"sum{layer}")
                    pe.wait_ge(sems["summed"], turn(i, "summed", {0: 1, 1: 2, 3: 3}[layer]))
                    for bb in range(PAIR):
                        for ct in range(CT):
                            m = pe.transpose(b[:, ct, bb * P:(bb + 1) * P], EW[:, bb, ct * P:(ct + 1) * P],
                                             ident[:, :])
                    m.then_inc(sems["product"], 1)

                pe.wait_ge(sems["x_in"], turn(i, "x_in"))
                transposes("xT", X)
                pe.wait_ge(sems["c_in"], turn(i, "c_in"))
                transposes("cT", CX)
                pe.wait_ge(leaves("xT"), left(i, "xT"))
                channel_major("q0", W0["q"], xT)
                pe.wait_ge(leaves("cT"), left(i, "cT"))
                channel_major("k0c", W0["k"], cT)
                channel_major("k0l", W0["k"], xT)
                token_major("v0c", cT, W0["v"])
                token_major("v0l", xT, W0["v"])
                pe.wait_ge(sems["cn"], turn(i, "cn"))
                transposes("aT", CN)
                pe.wait_ge(leaves("aT"), left(i, "aT"))
                channel_major("k3", W3["k"], aT)
                token_major("v3", aT, W3["v"])
                pe.wait_ge(leaves("q0"), left(i, "q0"))
                pe.wait_ge(leaves("v0l"), left(i, "v0l"))
                attention(0, [kA[:, :].rearrange("p (j b s) -> p j b s", j=8, b=PAIR) for kA in (keysA, keysB)], V0)
                pe.wait_ge(sems["attn"], turn(i, "attn", 1))
                token_major("o0", attnT, W0["o"])
                pe.wait_ge(sems["hn"], turn(i, "hn"))
                transposes("nT", HN)
                pe.wait_ge(leaves("nT"), left(i, "nT"))
                for u in range(4):
                    channel_major(f"u{u}", W0["w1"], nT, m0=u * C)
                pe.wait_ge(leaves("u3"), left(i, "u3"))
                token_major("m2", hT, W0["w2"])
                pe.wait_ge(leaves("m2"), left(i, "m2"))
                transposes("x1T", X1)
                pe.wait_ge(leaves("x1T"), left(i, "x1T"))
                channel_major("q1", W1["q"], x1T)
                channel_major("k1", W1["k"], cT, tiles=1)
                token_major("v1", cT, W1["v"])
                pe.wait_ge(leaves("q1"), left(i, "q1"))
                pe.wait_ge(leaves("v1"), left(i, "v1"))
                attention(1, [keysA[:, :].rearrange("p (j s) -> p j s", j=16)] * 2, V1)
                pe.wait_ge(sems["attn"], turn(i, "attn", 2))
                token_major("o1", attnT, W1["o"])
                pe.wait_ge(sems["n2"], turn(i, "n2"))
                transposes("xaT", HN)
                pe.wait_ge(sems["xxx"], turn(i, "xxx"))
                b = start("t")
                for a, n in ((0, P), (1, LORA)):
                    for k in range(CT):
                        m = pe.matmul(b[0:n, a, :], W2["m1"][:, k, a * P:a * P + n], xxx[:, k, :],
                                      start=(k == 0), stop=(k == CT - 1))
                m.then_inc(sems["product"], 1)
                pe.wait_ge(leaves("t"), left(i, "t"))
                for f, name in enumerate(("mw", "mk", "mv", "mr", "mg")):
                    b = start(name)
                    r0 = 32 * (f % 4)
                    lora = W2["m2"] if f < 4 else W2["m2g"]
                    for a in range(CT):
                        m = pe.matmul(b[:, a, :], lora[r0:r0 + 32, 0, a * P:(a + 1) * P],
                                      tT[r0:r0 + 32, f // 4, :], start=True, stop=True)
                    m.then_inc(sems["product"], 1)
                pe.wait_ge(sems["xf"], turn(i, "xf", 1))
                b = start("d1")
                for k in range(CT):
                    m = pe.matmul(b[0:DECAY, 0, :], W2["d1"][:, k, :], xf[0][:, k, :],
                                  start=(k == 0), stop=(k == CT - 1))
                m.then_inc(sems["product"], 1)
                pe.wait_ge(leaves("d1"), left(i, "d1"))
                b = start("d2")
                for a in range(CT):
                    m = pe.matmul(b[:, a, :], W2["d2"][0:DECAY, 0, a * P:(a + 1) * P], dT[0:DECAY, 0, :],
                                  start=True, stop=True)
                m.then_inc(sems["product"], 1)
                for f, name in ((1, "k"), (2, "v"), (3, "r"), (4, "g")):
                    pe.wait_ge(sems["xf"], turn(i, "xf", f + 1))
                    channel_major(name + "2", W2[name], xf[f])
                pe.wait_ge(sems["ruk"], turn(i, "ruk"))
                b = start("bonus")
                for a in range(CT):
                    m = pe.matmul(b[:, a, :], ones8[:, :], ruk[:, a, :], start=True, stop=True)
                m.then_inc(sems["product"], 1)
                pe.wait_ge(leaves("v2"), left(i, "v2"))

                def spread_v(u):
                    ct, j = u // 4, 2 * (u % 4)
                    b = start(f"vr{u}")
                    for a in range(2):
                        m = pe.matmul(b[:, a, :], spread[:, j + a, :], vT[:, ct, :], start=True, stop=True)
                    m.then_inc(sems["product"], 1)

                def gather_y(u):
                    ct, j = u // 4, 2 * (u % 4)
                    pe.wait_ge(sems["z"], turn(i, "z", u + 1))
                    for a in range(2):
                        m = pe.matmul(psO[:, ct, :], gather[:, j + a, :], Z[:, u % 2, a, :],
                                      start=(j + a == 0), stop=(j + a == 7), skip_group_check=True)
                    m.then_inc(sems["gathered"], 1)

                for u in range(9):
                    if u < 8:
                        spread_v(u)
                    if u >= 1:
                        gather_y(u - 1)
                pe.wait_ge(sems["y"], turn(i, "y"))
                transposes("yT", y)
                pe.wait_ge(sems["yn"], turn(i, "yn"))
                transposes("ynT", yn)
                pe.wait_ge(sems["y2"], turn(i, "y2"))
                token_major("o2", y2, W2["o"])
                pe.wait_ge(sems["n4"], turn(i, "n4"))
                transposes("xcT", HN)
                pe.wait_ge(sems["xr2"], turn(i, "xr2"))
                token_major("fr", xr2, W2["fr"])
                pe.wait_ge(sems["xk2"], turn(i, "xk2"))
                channel_major("fk", W2["fk"], xk2)
                pe.wait_ge(sems["kk"], turn(i, "kk"))
                token_major("fv", kk, W2["fv"])
                pe.wait_ge(sems["x4"], turn(i, "x4"))
                transposes("x4T", X4)
                pe.wait_ge(leaves("x4T"), left(i, "x4T"))
                channel_major("q3", W3["q"], x4T)
                pe.wait_ge(leaves("q3"), left(i, "q3"))
                pe.wait_ge(leaves("v3"), left(i, "v3"))
                attention(3, [keysB[:, c * 2048:(c + 1) * 2048].rearrange("p (j s) -> p j s", j=8)
                              for c in range(CT)], V3)
                pe.wait_ge(sems["attn"], turn(i, "attn", 3))
                token_major("o3", attnT, W3["o"])

        @block.scalar
        def _(act):
            act.wait_ge(s_w, WEIGHTS_IN)
            act.activation(gate_t[:, 1:2], gate_t[:, 0:1], ACT.Tanh).then_inc(s_setup, 1)
            with act.Fori(0, TURNS) as i:
                def copy_out(name, dst):
                    act.wait_ge(sems["product"], made(i, name))
                    act.activation(dst, bank(name), ACT.Copy).then_inc(sems["emptied_A"], 1)

                def affine(name, dsts, scale, bias, func=ACT.Identity):
                    act.wait_ge(sems["product"], made(i, name))
                    for a, d in enumerate(dsts):
                        kw = {}
                        if bias is not None:
                            kw["bias"] = bias[a]
                        if scale is not None:
                            kw["scale"] = scale[a]
                        ins = act.activation(d, bank(name)[:, a, :] if len(d.shape) == 2 else
                                             bank(name)[:, a, :].rearrange("p (b t) -> p b t", b=PAIR), func, **kw)
                    ins.then_inc(sems["emptied_A"], 1)

                def attention(layer):
                    jobs = attention_jobs(layer)
                    f = FIRST[layer]

                    def exps(n):
                        g = f + n
                        t, bb, j = jobs[n]
                        act.wait_ge(sems["masked"], turn(i, "masked", g + 1))
                        if g >= 2:
                            act.wait_ge(sems["turned"], turn(i, "turned", g - 1))
                        else:
                            act.wait_ge(sems["turned"], before(i, "turned"))
                        heads = 2 if layer == 0 else 4
                        w = 512 // heads
                        for h in range(heads):
                            jj = j + h
                            if layer == 1:
                                at = (jj % 8) * 4 + 2 * t + jj // 8
                            else:
                                at = t * 8 + (jj % 4) * 2 + jj // 4
                            ins = act.activation(E[:, g % 2, h * w:(h + 1) * w], S[:, g % 2, h * w:(h + 1) * w],
                                                 ACT.Exp, bias=nmax[:, g % 4, h:h + 1], scale=-1.0,
                                                 accum_out=esum[layer][:, bb, at:at + 1])
                        ins.then_inc(sems["exps"], 1)

                    def unturn(n):
                        g = f + n
                        if g % 2 == 0:
                            return
                        act.wait_ge(sems["turned"], turn(i, "turned", g + 1))
                        if g >= 4:
                            act.wait_ge(sems["pv"], turn(i, "pv", g - 3))
                        else:
                            act.wait_ge(sems["pv"], before(i, "pv"))
                        act.activation(ET[:, g % 4, :, :], psT[g % 2][:, :, :], ACT.Copy).then_inc(sems["turned_A"], 1)

                    for n in range(len(jobs) + 3):
                        if n < len(jobs):
                            exps(n)
                        if 0 <= n - 3 < len(jobs):
                            unturn(n - 3)
                    copy_out(f"sum{layer}", sumT)

                copy_out("xT", xT)
                affine("k0c", [k0T[:, a, :, 0:P] for a in range(CT)], None, col["k0_b"])
                affine("k0l", [k0T[:, a, :, P:2 * P] for a in range(CT)], None, col["k0_b"])
                affine("aT", [aT[:, a, :] for a in range(CT)], col["ln3_w"], col["ln3_b"])
                act.wait_ge(sems["keys3"], before(i, "keys3"))
                copy_out("k3", k3T[:, :, :])
                attention(0)
                act.wait_ge(leaves("o0"), left(i, "o0"))
                for bb in range(PAIR):
                    ins = act.activation(junk[:, bb, :], H[:, bb, :], ACT.Square, accum_out=ssq[:, bb:bb + 1])
                ins.then_inc(sems["ssq"], 1)
                act.wait_ge(sems["rstd0"], turn(i, "rstd0"))
                for bb in range(PAIR):
                    ins = act.activation(HN[:, bb, :], H[:, bb, :], ACT.Copy, scale=rs[0][:, bb:bb + 1])
                ins.then_inc(sems["hn"], 1)
                for u in range(4):
                    affine(f"u{u}", [hT[:, 2 * u + a, :] for a in range(2)], None, col[f"b1_{u}"],
                           ACT.Gelu_apprx_tanh)
                copy_out("x1T", x1T)
                act.wait_ge(sems["product"], made(i, "k1"))
                act.activation(k1T[:, :], bank("k1")[:, 0, :], ACT.Identity, bias=col["k1_b"][0]).then_inc(sems["emptied_A"], 1)
                attention(1)
                affine("xaT", [shifted[:, a, :, 1:P + 1] for a in range(CT)], col["ln1_w"], col["ln1_b"])
                act.wait_ge(sems["product"], made(i, "t"))
                act.activation(tT[:, 0, :], bank("t")[:, 0, :], ACT.Tanh)
                act.activation(tT[0:LORA, 1, :], bank("t")[0:LORA, 1, :], ACT.Tanh).then_inc(sems["emptied_A"], 1)
                act.wait_ge(sems["product"], made(i, "d1"))
                act.activation(dT[0:DECAY, 0, :], bank("d1")[0:DECAY, 0, :], ACT.Tanh).then_inc(sems["emptied_A"], 1)
                affine("d2", [w0[:, a, :] for a in range(CT)], None, col["decay"], ACT.Exp)
                act.wait_ge(sems["emptied_A"], turn(i, "emptied_A", EVACS["A"].index("d2") + 1))
                for a in range(CT):
                    ins = act.activation(wP[:, a, :, 1:P + 1], w0[:, a, :].rearrange("p (b t) -> p b t", b=PAIR),
                                         ACT.Exp, scale=-1.0)
                ins.then_inc(sems["w"], 1)
                copy_out("k2", kT)
                copy_out("r2", rT)
                act.wait_ge(sems["product"], made(i, "g2"))
                act.activation(gT, bank("g2"), ACT.Silu).then_inc(sems["emptied_A"], 1)
                copy_out("yT", yt)
                act.wait_ge(sems["yc"], turn(i, "yc"))
                act.activation(sq, yc, ACT.Square).then_inc(sems["sq"], 1)
                affine("ynT", [y2a[:, a, :] for a in range(CT)], col["gn_w"], col["gn_b"])
                affine("xcT", [shifted[:, a, :, 1:P + 1] for a in range(CT)], col["ln2_w"], col["ln2_b"])
                act.wait_ge(sems["product"], made(i, "fr"))
                act.activation(rr, bank("fr"), ACT.Sigmoid).then_inc(sems["emptied_A"], 1)
                act.wait_ge(sems["product"], made(i, "fk"))
                act.activation(kk0, bank("fk"), ACT.Relu).then_inc(sems["emptied_A"], 1)
                act.wait_ge(leaves("fk"), left(i, "fk"))
                act.activation(kk, kk0, ACT.Square).then_inc(sems["kk"], 1)
                copy_out("x4T", x4T)
                act.wait_ge(sems["product"], made(i, "q3"))
                act.activation(Q, bank("q3"), ACT.Copy, scale=0.25).then_inc(sems["emptied_A"], 1)
                attention(3)

        @block.vector
        def _(dve):
            dve.wait_ge(s_const, 3)
            dve.tensor_reduce(head8[:, :], ident[:, :].rearrange("p (a b) -> p a b", b=8), AX.X, ALU.add)\
                .then_inc(s_setup_d, 1)
            dve.tensor_reduce(head16[:, :, :], ident[:, :].rearrange("p (s r d) -> p r s d", r=2, d=16), AX.X,
                              ALU.add).then_inc(s_setup_d, 1)
            dve.tensor_reduce(lane8[:, :], ident[:, :].rearrange("p (a b) -> p b a", b=8), AX.X, ALU.add)\
                .then_inc(s_setup_d, 1)
            dve.wait_ge(s_setup_d, 3)
            dve.tensor_copy(ones8[:, :].rearrange("p (a b) -> p a b", b=8),
                            head8[:, :].unsqueeze(2).to_broadcast([P, 16, 8]))
            for j in range(8):
                dve.tensor_scalar(spread[:, j, :].rearrange("p (a b) -> p a b", b=8),
                                  head8[:, :].unsqueeze(2).to_broadcast([P, 16, 8]), lane8[:, j:j + 1], None,
                                  ALU.mult)
            for j in range(8):
                ins = dve.tensor_copy(gather[:, j, :].rearrange("p (a b) -> p a b", b=8)[:, :, j], head8[:, :])
            ins.then_inc(s_setup_d, 1)
            dve.wait_ge(s_w, WEIGHTS_IN)
            dve.wait_ge(s_setup, 1)

            waited_in[dve] = [dve.alloc_register(f"count{n}_dve") for n in range(3)]
            i_reg[dve] = dve.alloc_register("turn_dve")
            dve.reg_mov(i_reg[dve], 0)
            with dve.Fori(0, TURNS) as i:
                def norm_stats(src, n):
                    for bb in range(PAIR):
                        ins = dve.bn_stats(bst[:, bb, :], src[:, bb, :])
                    ins.then_inc(sems["halves"], 1)
                    at = counted(dve, ("halves", NORMS.index(n) + 1))
                    dve.wait_ge(s_w, WEIGHTS_IN)
                    dve.wait_ge(sems["halves"], at[0])
                    for bb in range(PAIR):
                        ins = dve.bn_aggr(mv[n][:, bb, :], bst[:, bb, :])
                    ins.then_inc(sems[f"stats{n}"], 1)

                def normalise(dst, src, n, name):
                    dve.wait_ge(sems[f"stats{n}"], turn(i, f"stats{n}"))
                    dve.wait_ge(sems[f"rstd{n}"], turn(i, f"rstd{n}"))
                    for bb in range(PAIR):
                        ins = dve.tensor_scalar(dst[:, bb, :], src[:, bb, :], mv[n][:, bb, 0:1],
                                                rs[n][:, bb:bb + 1], ALU.subtract, ALU.mult)
                    ins.then_inc(sems[name], 1)

                def add_out(name, dst, add, sig):
                    dve.wait_ge(sems["product"], made(i, name))
                    dve.tensor_tensor(dst, bank(name), add, ALU.add).then_inc(sems["emptied_D"], 1)

                def attention(layer, bias):
                    jobs = attention_jobs(layer)
                    f = FIRST[layer]

                    def mask(n):
                        g = f + n
                        t, bb, j = jobs[n]
                        at = counted(dve, ("scores", g + 1), ("exps", g - 1 if g >= 2 else 0))
                        dve.wait_ge(s_w, WEIGHTS_IN)
                        dve.wait_ge(sems["scores"], at[0])
                        dve.wait_ge(sems["exps"], at[1])
                        heads = 2 if layer == 0 else 4
                        w = 512 // heads
                        for h in range(heads):
                            ins = dve.tensor_tensor_reduce(S[:, g % 2, h * w:(h + 1) * w],
                                                           psS[g % 2][:, h * w:(h + 1) * w], bias[:, bb, :],
                                                           -1.0, HUGE, ALU.add, ALU.min,
                                                           nmax[:, g % 4, h:h + 1])
                        ins.then_inc(sems["masked"], 1)

                    def unturn(n):
                        g = f + n
                        if g % 2 == 1:
                            return
                        dve.wait_ge(sems["turned"], turn(i, "turned", g + 1))
                        if g >= 4:
                            dve.wait_ge(sems["pv"], turn(i, "pv", g - 3))
                        else:
                            dve.wait_ge(sems["pv"], before(i, "pv"))
                        dve.tensor_copy(ET[:, g % 4, :, :], psT[g % 2][:, :, :]).then_inc(sems["turned_D"], 1)

                    for n in range(len(jobs) + 3):
                        if n < len(jobs):
                            mask(n)
                        if 0 <= n - 3 < len(jobs):
                            unturn(n - 3)
                    dve.wait_ge(sems["exps"], turn(i, "exps", f + len(jobs)))
                    heads = 16 if layer != 1 else 32
                    inv = einv[layer][:, :, 0:heads]
                    dve.reciprocal(inv, esum[layer][:, :, 0:heads]).then_inc(sems["inverse"], 1)
                    dve.wait_ge(sems["inverse"], turn(i, "inverse", {0: 1, 1: 2, 3: 3}[layer]))
                    dve.tensor_copy(EW.rearrange("p b (h d) -> p b h d", h=heads),
                                         inv.unsqueeze(3).to_broadcast([P, PAIR, heads, C // heads])).then_inc(sems["summed"], 1)
                    dve.wait_ge(leaves(f"sum{layer}"), left(i, f"sum{layer}"))
                    dve.wait_ge(sems["pv"], turn(i, "pv", f + len(jobs)))
                    dve.tensor_tensor(attnT, psO[:, :, :], sumT, ALU.mult).then_inc(sems["attn"], 1)

                dve.wait_ge(sems["c_in"], turn(i, "c_in"))
                norm_stats(CX, 3)
                dve.wait_ge(sems["product"], made(i, "cT"))
                dve.tensor_copy(cT, bank("cT")).then_inc(sems["emptied_D"], 1)
                dve.wait_ge(sems["product"], made(i, "q0"))
                for a in range(CT):
                    ins = dve.tensor_scalar(Q[:, a, :], bank("q0")[:, a, :], col["q0_b"][a], 1.0 / 16, ALU.add,
                                            ALU.mult)
                ins.then_inc(sems["emptied_D"], 1)
                normalise(CN, CX, 3, "cn")
                dve.wait_ge(sems["masked"], before(i, "masked"))
                dve.wait_ge(sems["m0_in"], turn(i, "m0_in"))
                dve.tensor_scalar(mb0[:, :, 0:P], m0i[:, :, :], 0.0, -BIG, ALU.is_equal, ALU.mult).then_inc(sems["mask_bias"], 1)
                dve.memset(mb0[:, :, P:2 * P], 0.0).then_inc(sems["mask_bias"], 1)
                dve.wait_ge(sems["m3_in"], turn(i, "m3_in"))
                dve.tensor_scalar(mb3[:, :, :], m3i[:, :, :], 0.0, -BIG, ALU.is_equal, ALU.mult).then_inc(sems["mask_bias"], 1)

                def values16(name, dst):
                    dve.wait_ge(sems["product"], made(i, name))
                    for par in range(2):
                        d = dst[:, :, par, :].rearrange("p b (s r d) -> p b s r d", r=2, d=16)[:, :, :, par, :]
                        v = bank(name).rearrange("p b (s r d) -> p b s r d", r=2, d=16)[:, :, :, par, :]
                        if name == "v3":
                            ins = dve.tensor_copy(d, v)
                        else:
                            bias = row["v0_b"].rearrange("p (s r d) -> p s r d", r=2, d=16)[:, :, par, :]
                            ins = dve.tensor_tensor(d, v, bias.unsqueeze(1).to_broadcast([P, PAIR, 8, 16]), ALU.add)
                    ins.then_inc(sems["emptied_D"], 1)

                values16("v0c", V0[:, 0, :, :, :])
                values16("v0l", V0[:, 1, :, :, :])
                values16("v3", V3[:, :, :, :])
                dve.wait_ge(leaves("cT"), left(i, "cT"))
                dve.tensor_copy(state_cols[:, :, :, :],
                                     cT.rearrange("p k (b t) -> p k b t", b=PAIR)[:, :, :, 0:2]).then_inc(sems["state_cols"], 1)
                dve.wait_ge(sems["mask_bias"], turn(i, "mask_bias"))
                attention(0, mb0[:, :, :])
                dve.wait_ge(sems["xo"], turn(i, "xo"))
                dve.wait_ge(sems["product"], made(i, "o0"))
                dve.tensor_tensor(H, bank("o0"), XO, ALU.add).then_inc(sems["emptied_D"], 1)
                dve.wait_ge(sems["product"], made(i, "nT"))
                for a in range(CT):
                    ins = dve.tensor_scalar(nT[:, a, :], bank("nT")[:, a, :], col["post_w"][a], None, ALU.mult)
                ins.then_inc(sems["emptied_D"], 1)
                dve.wait_ge(sems["xb2"], turn(i, "xb2"))
                dve.wait_ge(sems["product"], made(i, "m2"))
                dve.tensor_tensor(X1, bank("m2"), XB2, ALU.add).then_inc(sems["emptied_D"], 1)
                dve.wait_ge(sems["product"], made(i, "q1"))
                for a in range(CT):
                    ins = dve.tensor_scalar(Q[:, a, :], bank("q1")[:, a, :], col["q1_b"][a], 8.0 ** -0.5, ALU.add,
                                            ALU.mult)
                ins.then_inc(sems["emptied_D"], 1)
                dve.wait_ge(sems["product"], made(i, "v1"))
                for g in range(4):
                    d = V1[:, :, g, :].rearrange("p b (k g d) -> p b k g d", g=4, d=8)[:, :, :, g, :]
                    v = bank("v1")[:, :, 0:64].rearrange("p b (k d) -> p b k d", d=8)
                    bias = row["v1_b"][:, 0:64].rearrange("p (k d) -> p k d", d=8)
                    ins = dve.tensor_tensor(d, v, bias.unsqueeze(1).to_broadcast([P, PAIR, 8, 8]), ALU.add)
                ins.then_inc(sems["emptied_D"], 1)
                dve.wait_ge(sems["m1_in"], turn(i, "m1_in"))
                attention(1, mb1[:, :, :])
                dve.wait_ge(sems["xb1"], turn(i, "xb1"))
                dve.wait_ge(sems["product"], made(i, "o1"))
                dve.tensor_tensor(Y1, bank("o1"), XB1, ALU.add).then_inc(sems["emptied_D"], 1)
                dve.wait_ge(leaves("o1"), left(i, "o1"))
                norm_stats(Y1, 1)
                normalise(HN, Y1, 1, "n1")
                dve.wait_ge(sems["x2"], turn(i, "x2"))
                norm_stats(X2, 2)
                normalise(HN, X2, 2, "n2")

                def token_shift(state_col, dst):
                    n = 2 - state_col
                    dve.tensor_copy(shifted[:, :, :, 0:1], state_cols[:, :, :, state_col:state_col + 1])\
                        .then_inc(sems["first_token"], 1)
                    dve.wait_ge(sems["first_token"], turn(i, "first_token", n))
                    dve.tensor_tensor(dst.rearrange("p k (b t) -> p k b t", b=PAIR), shifted[:, :, :, 0:P],
                                      shifted[:, :, :, 1:P + 1], ALU.subtract).then_inc(sems["shift"], 1)
                    dve.wait_ge(sems["shift"], turn(i, "shift", n))

                def now(a):
                    return shifted[:, a, :, 1:P + 1]

                def halves(ap):
                    return ap.rearrange("p (b t) -> p b t", b=PAIR)

                dve.wait_ge(leaves("xaT"), left(i, "xaT"))
                token_shift(1, sx)
                for a in range(CT):
                    ins = dve.scalar_tensor_tensor(halves(xxx[:, a, :]), halves(sx[:, a, :]), col["maa_x"][a], now(a),
                                                   ALU.mult, ALU.add)
                ins.then_inc(sems["xxx"], 1)
                for f, name in enumerate(("mw", "mk", "mv", "mr", "mg")):
                    dve.wait_ge(sems["product"], made(i, name))
                    if f >= 2:
                        dve.wait_ge(sems["xf"], turn(i, "xf", f - 1))
                    for a in range(CT):
                        ins = dve.scalar_tensor_tensor(tmp[f % 2][:, a, :], bank(name)[:, a, :],
                                                       col["maa_" + name[1]][a], sx[:, a, :], ALU.add, ALU.mult)
                    ins.then_inc(sems["emptied_D"], 1)
                dve.wait_ge(sems["product"], made(i, "v2"))
                dve.tensor_copy(vT, bank("v2")).then_inc(sems["emptied_D"], 1)
                dve.wait_ge(leaves("r2"), left(i, "r2"))
                for a in range(CT):
                    ins = dve.scalar_tensor_tensor(ruk[:, a, :], rT[:, a, :], col["bonus"][a], kT[:, a, :],
                                                   ALU.mult, ALU.mult)
                ins.then_inc(sems["ruk"], 1)
                dve.wait_ge(sems["product"], made(i, "bonus"))
                dve.wait_ge(leaves("v2"), left(i, "v2"))
                dve.tensor_tensor(Dv, bank("bonus"), vT, ALU.mult).then_inc(sems["emptied_D"], 1)
                dve.wait_ge(sems["w"], turn(i, "w"))
                for u in range(8):
                    ct = u // 4
                    dve.wait_ge(sems["product"], made(i, f"vr{u}"))
                    if u >= 2:
                        dve.wait_ge(sems["scan"], turn(i, "scan", u - 1))
                    dve.wait_ge(sems["seed"], turn(i, "seed", u + 1))
                    k_ = kT[:, ct, :].rearrange("p (b t) -> p b t", b=PAIR).unsqueeze(1)\
                        .to_broadcast([P, 2, PAIR, P])
                    dve.tensor_tensor(kv[:, u % 2, :, :, 1:P + 1],
                                           bank(f"vr{u}").rearrange("p a (b t) -> p a b t", b=PAIR), k_,
                                           ALU.mult).then_inc(sems["emptied_D"], 1)
                    dve.wait_ge(leaves(f"vr{u}"), left(i, f"vr{u}"))
                    if u >= 2:
                        dve.wait_ge(sems["z"], turn(i, "z", u - 1))
                    for a in range(2):
                        ins = dve.tensor_tensor_scan(SS[:, u % 2, a, :, :].rearrange("p b t -> p (b t)"),
                                                     wP[:, ct, :, :].rearrange("p b t -> p (b t)"),
                                                     kv[:, u % 2, a, :, :].rearrange("p b t -> p (b t)"),
                                                     0.0, ALU.mult, ALU.add)
                    ins.then_inc(sems["scan"], 1)
                dve.wait_ge(sems["gathered"], turn(i, "gathered"))
                dve.tensor_tensor(y, psO[:, :, :], Dv, ALU.add).then_inc(sems["y"], 1)
                dve.wait_ge(leaves("yT"), left(i, "yT"))
                groups = yt.rearrange("p b (h d) -> p (b h) d", d=8)
                yc_g = yc.rearrange("p b (h d) -> p (b h) d", d=8)
                dve.tensor_reduce(gsum[:, :], groups, AX.X, ALU.add).then_inc(sems["gsum"], 1)
                dve.wait_ge(sems["gsum"], turn(i, "gsum"))
                dve.scalar_tensor_tensor(yc_g, gsum[:, :].unsqueeze(2).to_broadcast([P, 64, 8]), -1.0 / 8,
                                              groups, ALU.mult, ALU.add).then_inc(sems["yc"], 1)
                dve.wait_ge(sems["sq"], turn(i, "sq"))
                dve.tensor_reduce(gvar[:, :], sq.rearrange("p b (h d) -> p (b h) d", d=8), AX.X, ALU.add).then_inc(sems["gvar"], 1)
                dve.wait_ge(sems["rstd_g"], turn(i, "rstd_g"))
                dve.tensor_tensor(yn.rearrange("p b (h d) -> p (b h) d", d=8), yc_g,
                                       grs[:, :].unsqueeze(2).to_broadcast([P, 64, 8]), ALU.mult).then_inc(sems["yn"], 1)
                dve.wait_ge(sems["product"], made(i, "o2"))
                dve.tensor_tensor(X3, bank("o2"), X2, ALU.add).then_inc(sems["emptied_D"], 1)
                dve.wait_ge(leaves("o2"), left(i, "o2"))
                norm_stats(X3, 4)
                normalise(HN, X3, 4, "n4")
                dve.wait_ge(leaves("xcT"), left(i, "xcT"))
                token_shift(0, sxc)
                for name, dst in (("fmaa_r", xr2), ("fmaa_k", xk2)):
                    for a in range(CT):
                        ins = dve.scalar_tensor_tensor(halves(dst[:, a, :]), halves(sxc[:, a, :]), col[name][a],
                                                       now(a), ALU.mult, ALU.add)
                    ins.then_inc(sems["xr2" if name == "fmaa_r" else "xk2"], 1)
                dve.wait_ge(sems["product"], made(i, "fv"))
                dve.wait_ge(leaves("fr"), left(i, "fr"))
                dve.tensor_tensor(tmpv, bank("fv"), rr, ALU.mult).then_inc(sems["emptied_D"], 1)
                dve.wait_ge(leaves("fv"), left(i, "fv"))
                dve.tensor_tensor(X4, tmpv, X3, ALU.add).then_inc(sems["x4"], 1)
                attention(3, mb3[:, :, :])
                dve.wait_ge(sems["product"], made(i, "o3"))
                dve.wait_ge(sems["x4"], turn(i, "x4"))
                dve.wait_ge(sems["out_done"], before(i, "out_done"))
                dve.scalar_tensor_tensor(OUT, bank("o3"), gate_t[:, 1:2], X4, ALU.mult, ALU.add).then_inc(sems["emptied_D"], 1)
                dve.reg_add(i_reg[dve], i_reg[dve], 1)

        @block.gpsimd
        def _(pool):
            for name in sorted(AHEAD):
                pool.sem_inc(sems[name], 1)
            pool.memset(ident[:, :], 0.0).then_inc(s_const, 1)
            pool.wait_ge(s_const, 1)
            pool.affine_select(out=ident[:, :], in_=ident[:, :], compare_op=ALU.not_equal, fill=1.0, base=0,
                               pattern=[[-1, P]], channel_multiplier=1).then_inc(s_const, 1)
            for buf in (gather, V0, V1, V3, wP):
                shape = buf.shape
                flat = buf[tuple(slice(None) for _ in shape)]
                pool.memset(flat, 0.0)
            pool.memset(minus_half[:, :], -0.5).then_inc(s_const, 1)
            pool.wait_ge(s_w, WEIGHTS_IN)
            pool.wait_ge(s_setup_d, 3)

            waited_in[pool] = [pool.alloc_register(f"count{n}_pool") for n in range(3)]
            i_reg[pool] = pool.alloc_register("turn_pool")
            pool.reg_mov(i_reg[pool], 0)
            with pool.Fori(0, TURNS) as i:
                def power(dst, var, scale, eps, name):
                    n = dst.shape[1]
                    pool.tensor_scalar(veps[:, 0:n], var, scale, eps, ALU.mult, ALU.add).then_inc(sems["veps"], 1)
                    pool.wait_ge(sems["veps"], turn(i, "veps", POWERS.index(name) + 1))
                    pool.tensor_tensor(dst, veps[:, 0:n], minus_half[:, 0:n], ALU.pow).then_inc(sems[name], 1)

                at = counted(pool, ("stats3", None))
                pool.wait_ge(s_w, WEIGHTS_IN)
                pool.wait_ge(sems["stats3"], at[0])
                power(rs[3][:, :], mv[3][:, :, 1], 1.0, 1e-5, "rstd3")
                pool.wait_ge(sems["x_in"], turn(i, "x_in"))
                pool.tensor_tensor(XO, X, row["o0_b"].unsqueeze(1).to_broadcast([P, PAIR, C]), ALU.add).then_inc(sems["xo"], 1)
                pool.tensor_tensor(XB2, X, row["b2"].unsqueeze(1).to_broadcast([P, PAIR, C]), ALU.add).then_inc(sems["xb2"], 1)
                at = counted(pool, count_of("k0l"))
                pool.wait_ge(s_w, WEIGHTS_IN)
                pool.wait_ge(leaves("k0l"), at[0])
                for ct, keys in ((0, keysA), (1, keysB)):
                    for j in range(8):
                        pool.tensor_scalar(keys[:, j * 512:(j + 1) * 512],
                                                k0T[:, ct, :, :].rearrange("p b s -> p (b s)"),
                                                head16[:, j // 4, j % 4:j % 4 + 1], None, ALU.mult).then_inc(sems["keys0"], 1)
                at = counted(pool, ("ssq", None))
                pool.wait_ge(s_w, WEIGHTS_IN)
                pool.wait_ge(sems["ssq"], at[0])
                power(rs[0][:, :], ssq[:, :], 1.0 / C, 1e-6, "rstd0")
                pool.wait_ge(leaves("m2"), left(i, "m2"))
                pool.tensor_tensor(XB1, X1, row["o1_b"].unsqueeze(1).to_broadcast([P, PAIR, C]), ALU.add).then_inc(sems["xb1"], 1)
                at = counted(pool, count_of("k1"))
                pool.wait_ge(s_w, WEIGHTS_IN)
                pool.wait_ge(leaves("k1"), at[0])
                for j in range(16):
                    pool.tensor_scalar(keysA[:, j * T:(j + 1) * T], k1T[:, :], head8[:, j:j + 1], None,
                                            ALU.mult).then_inc(sems["keys1"], 1)
                at = counted(pool, count_of("k3"), ("product", NAMES.index("m2") + 1))
                pool.wait_ge(s_w, WEIGHTS_IN)
                pool.wait_ge(leaves("k3"), at[0])
                pool.wait_ge(sems["product"], at[1])
                for ct in range(CT):
                    for j in range(8):
                        pool.tensor_scalar(keysB[:, (ct * 8 + j) * T:(ct * 8 + j + 1) * T], k3T[:, ct, :],
                                                head16[:, j // 4, j % 4:j % 4 + 1], None, ALU.mult).then_inc(sems["keys3"], 1)
                at = counted(pool, ("stats1", None))
                pool.wait_ge(s_w, WEIGHTS_IN)
                pool.wait_ge(sems["stats1"], at[0])
                power(rs[1][:, :], mv[1][:, :, 1], 1.0, 1e-6, "rstd1")
                pool.wait_ge(sems["n1"], turn(i, "n1"))
                pool.tensor_tensor(B16, HN, row["gamma"].unsqueeze(1).to_broadcast([P, PAIR, C]), ALU.mult)\
                    .then_inc(sems["gamma"], 1)
                pool.wait_ge(sems["gamma"], turn(i, "gamma"))
                pool.tensor_tensor(X2, B16, row["beta"].unsqueeze(1).to_broadcast([P, PAIR, C]), ALU.add).then_inc(sems["x2"], 1)
                at = counted(pool, ("stats2", None))
                pool.wait_ge(s_w, WEIGHTS_IN)
                pool.wait_ge(sems["stats2"], at[0])
                power(rs[2][:, :], mv[2][:, :, 1], 1.0, 1e-5, "rstd2")
                for f in range(5):
                    pool.wait_ge(leaves(("mw", "mk", "mv", "mr", "mg")[f]), left(i, ("mw", "mk", "mv", "mr", "mg")[f]))
                    for a in range(CT):
                        ins = pool.tensor_tensor(xf[f][:, a, :].rearrange("p (b t) -> p b t", b=PAIR),
                                                 tmp[f % 2][:, a, :].rearrange("p (b t) -> p b t", b=PAIR),
                                                 shifted[:, a, :, 1:P + 1], ALU.add)
                    ins.then_inc(sems["xf"], 1)
                pool.wait_ge(sems["s0_in"], turn(i, "s0_in"))
                pool.wait_ge(leaves("r2"), left(i, "r2"))
                for u in range(9):
                    if u < 8:
                        if u >= 2:
                            pool.wait_ge(sems["scan"], turn(i, "scan", u - 1))
                        ct, j = u // 4, 2 * (u % 4)
                        pool.tensor_tensor(kv[:, u % 2, :, :, 0],
                                                s0[:, :, ct, j:j + 2].rearrange("p b j -> p j b"),
                                                wP[:, :, :, 0], ALU.add).then_inc(sems["seed"], 1)
                    if u >= 1:
                        v = u - 1
                        ct = v // 4
                        pool.wait_ge(sems["scan"], turn(i, "scan", v + 1))
                        if v >= 2:
                            pool.wait_ge(sems["gathered"], turn(i, "gathered", v - 1))
                        for a in range(2):
                            ins = pool.tensor_tensor(Z[:, v % 2, a, :].rearrange("p (b t) -> p b t", b=PAIR),
                                                     SS[:, v % 2, a, :, 0:P],
                                                     rT[:, ct, :].rearrange("p (b t) -> p b t", b=PAIR), ALU.mult)
                        ins.then_inc(sems["z"], 1)
                at = counted(pool, ("gvar", None))
                pool.wait_ge(s_w, WEIGHTS_IN)
                pool.wait_ge(sems["gvar"], at[0])
                power(grs[:, :], gvar[:, :], 1.0 / 8, 1e-5, "rstd_g")
                pool.wait_ge(leaves("ynT"), left(i, "ynT"))
                pool.tensor_tensor(y2, y2a, gT, ALU.mult).then_inc(sems["y2"], 1)
                at = counted(pool, ("stats4", None))
                pool.wait_ge(s_w, WEIGHTS_IN)
                pool.wait_ge(sems["stats4"], at[0])
                power(rs[4][:, :], mv[4][:, :, 1], 1.0, 1e-5, "rstd4")
                pool.reg_add(i_reg[pool], i_reg[pool], 1)


def kernel(**inputs):
    import numpy as np
    import concourse.bacc as bacc
    from concourse.bass_utils import run_bass_kernel_spmd

    a = {k: np.ascontiguousarray(v) for k, v in inputs.items()}

    def l(n, k):
        return a[f"L{n}_xattn_{k}"]

    def tiles(w):
        return w.reshape(-1, P, w.shape[1]).transpose(1, 0, 2).reshape(P, -1)

    def pad(w):
        return np.concatenate([w, np.zeros((P - w.shape[0], w.shape[1]), w.dtype)], 0) if w.shape[0] < P else w

    def column(v):
        return v.reshape(-1, P).T

    kvw = l(0, "kv_w").reshape(C, C, 2)
    kvb = l(0, "kv_b").reshape(C, 2)
    wl0 = dict(q=l(0, "q_w"), k=kvw[:, :, 0], v=kvw[:, :, 1], o=l(0, "out_w"), w1=l(0, "mlp_w1"), w2=l(0, "mlp_w2"))
    def by_group(w):
        return w.reshape(-1, 8, 4, 8).transpose(0, 2, 1, 3).reshape(-1, C)

    wl1 = dict(q=by_group(l(1, "Wq")), k=np.concatenate([l(1, "Wk")] * 2, 1), v=l(1, "Wv"), o=l(1, "Wo"))
    m2 = l(2, "maa_w2")
    wl2 = dict(m1=l(2, "maa_w1"), d1=l(2, "decay_w1"), r=l(2, "Wr").T, k=l(2, "Wk").T, v=l(2, "Wv").T,
               g=l(2, "Wg").T, o=l(2, "Wo").T, fr=l(2, "fWr").T, fk=l(2, "fWk").T, fv=l(2, "fWv").T,
               m2=m2[0:4].reshape(P, C), m2g=pad(m2[4]), d2=pad(l(2, "decay_w2")))
    wl3 = {k: l(3, "W" + k).T for k in "qkvo"}
    b1 = l(0, "mlp_b1").reshape(4, C)
    cols = dict(q0_b=l(0, "q_b"), k0_b=kvb[:, 0], b1_0=b1[0], b1_1=b1[1], b1_2=b1[2], b1_3=b1[3],
                post_w=l(0, "postnorm_w"), q1_b=by_group(l(1, "bq"))[0], k1_b=np.concatenate([l(1, "bk")] * 4),
                ln1_w=l(2, "ln1_w"), ln1_b=l(2, "ln1_b"), maa_x=l(2, "maa_x"), maa_w=l(2, "maa_w"),
                maa_k=l(2, "maa_k"), maa_v=l(2, "maa_v"), maa_r=l(2, "maa_r"), maa_g=l(2, "maa_g"),
                decay=l(2, "time_decay"), bonus=l(2, "faaaa").reshape(C), gn_w=l(2, "gn_w"), gn_b=l(2, "gn_b"),
                ln2_w=l(2, "ln2_w"), ln2_b=l(2, "ln2_b"), fmaa_k=l(2, "fmaa_k"), fmaa_r=l(2, "fmaa_r"),
                ln3_w=l(3, "ln_gamma"), ln3_b=l(3, "ln_beta"))
    rows = dict(v0_b=kvb[:, 1], o0_b=l(0, "out_b"), b2=l(0, "mlp_b2"), o1_b=l(1, "bo"), gamma=l(1, "gamma"),
                beta=l(1, "beta"), v1_b=np.concatenate([l(1, "bv")] * 4))
    arrays = dict(
        x=a["x"], ctx=a["ctx_2048"], m0=a["mask_BxS2_ik0"], m1=a["mask_Bx1xSxS2_ff0"].reshape(BATCH, P, P),
        m3=a["mask_BxS2_bf1"].view(np.uint8),
        wl0=np.concatenate([tiles(wl0[k]) for k in W_L0], 1), wl1=np.concatenate([tiles(wl1[k]) for k in W_L1], 1),
        wl2=np.concatenate([tiles(wl2[k]) for k in W_L2], 1), wl3=np.concatenate([tiles(wl3[k]) for k in W_L3], 1),
        cols=np.stack([column(cols[k]) for k in COLS], 1), rows=np.stack([rows[k] for k in ROWS])[None],
        gate=l(3, "gate").reshape(1, 1))
    nc = bacc.Bacc("TRN2", target_bir_lowering=False, num_devices=1)
    arrays = {f"in_{k}": np.ascontiguousarray(v) for k, v in arrays.items()}
    args = [nc.dram_tensor(k, v.shape, mybir.dt.from_np(v.dtype), kind="ExternalInput").ap()
            for k, v in arrays.items()]
    out = nc.dram_tensor("out", (BATCH, P, C), F32, kind="ExternalOutput").ap()
    build(nc, *args, out)
    return run_bass_kernel_spmd(nc, [arrays], core_ids=[0]).results[0]["out"]
```

```python
from contextlib import ExitStack

import concourse.bass as bass
from concourse import mybir

F32 = mybir.dt.float32
I32 = mybir.dt.int32
U8 = mybir.dt.uint8
ALU = mybir.AluOpType
ACT = mybir.ActivationFunctionType
AX = mybir.AxisListType

P = 128
BATCH = 16
PAIR = 2
TURNS = BATCH // PAIR
C = 256
CT = C // P
T = PAIR * P
MLP = 4 * C
MT = MLP // P
LORA = 32
DECAY = 64
WEIGHTS_IN = 7 * 16
BIG = 1e30
HUGE = 3e38

W_L0 = dict(q=(CT, C), k=(CT, C), v=(CT, C), o=(CT, C), w1=(CT, MLP), w2=(MT, C))
W_L1 = dict(q=(CT, C), k=(CT, P), v=(CT, 64), o=(CT, C))
W_L2 = dict(m1=(CT, 5 * LORA), d1=(CT, DECAY), r=(CT, C), k=(CT, C), v=(CT, C), g=(CT, C), o=(CT, C),
            fr=(CT, C), fk=(CT, C), fv=(CT, C), m2=(1, C), m2g=(1, C), d2=(1, C))
W_L3 = dict(q=(CT, C), k=(CT, C), v=(CT, C), o=(CT, C))
COLS = ["q0_b", "k0_b", "b1_0", "b1_1", "b1_2", "b1_3", "post_w", "q1_b", "k1_b", "ln1_w", "ln1_b", "maa_x",
        "maa_w", "maa_k", "maa_v", "maa_r", "maa_g", "decay", "bonus", "gn_w", "gn_b", "ln2_w", "ln2_b",
        "fmaa_k", "fmaa_r", "ln3_w", "ln3_b"]
ROWS = ["v0_b", "o0_b", "b2", "o1_b", "gamma", "beta", "v1_b"]

NJ = {0: 16, 1: 16, 3: 8}
DRAIN = 4
BANKS = 3
RING_K, RING_S, RING_E = 4, 2, 4


def jobs(layer, first, end):
    return [("job", layer, n) for n in range(first, end)]


def spread(steps, between):
    merged, done = [], 0
    for n, s in enumerate(steps):
        merged.append(s)
        upto = (n + 1) * len(between) // len(steps)
        merged += between[done:upto]
        done = upto
    return merged


FRONT_IN = ["xT", "cT", "q0", "k0c", "k0l", "norm3", "v0c", "v0l"]
SCHEDULE = (
    ["xaT", "xT", "shift1", "cT", "t", "q0", "k0c", "mw", "k0l", "mk", "norm3"]
    + spread(jobs(0, 0, 16), ["v0c", "v0l", "mv", "d1", "mr", "d2", "k2", "decay", "mg", "v2", "r2", "k1", "ruk",
                              "g2", "v1", "bonus", "aT", "vr0"])
    + spread(jobs(0, 16, 16 + DRAIN), ["vr1"])
    + ["sum0", "o0", ("gather", 0), "vr2", "hn", ("gather", 1), "nT", "vr3", ("gather", 2), "u0", "u1", "vr4", ("gather", 3), "u2", "vr5",
       ("gather", 4), "u3", "vr6", ("gather", 5), "vr7", ("gather", 6), "m2", ("gather", 7), "yT", "x1T", "group", "q1", "yn"]
    + spread(jobs(1, 0, 16), ["ynT", "y2", "o2", "norm4", "xcT", "shift0", "fr", "fk", "fv", "x4T"])
    + ["q3"] + spread(jobs(1, 16, 16 + DRAIN), jobs(3, 0, 3))
    + ["sum1", "o1"] + jobs(3, 3, 4) + ["norm1"] + jobs(3, 4, 7) + ["norm2"] + jobs(3, 7, 8 + DRAIN)
    + ["k3", "sum3", "v3", "o3"])
FRONT = {"xT", "cT", "q0", "k0c", "k0l", "norm3", "v0c", "v0l", "aT", "k1", "v1", "sum0", "o0", "hn", "nT", "u0", "u1",
         "u2", "u3", "m2", "x1T", "q1", "sum1", "o1", "norm1", "norm2", "k3", "v3"}


def is_front(step):
    return step in FRONT or (step[0] == "job" and step[1] != 3)


def steps_of(phase):
    return [s for s in SCHEDULE if phase == "steady" or is_front(s) == (phase == "first")]


EMPTIES = dict(
    xT="A", cT="D", q0="D", k0c="A", k0l="A", v0c="D", v0l="D", k1="A", v1="D", aT="A", k3="A", v3="D",
    sum0="A", o0="D", nT="D", u0="A", u1="A", u2="A", u3="A", m2="D", x1T="A", q1="D", sum1="A", o1="D",
    xaT="A", t="A", mw="D", mk="D", mv="D", mr="D", mg="D", d1="A", d2="A", k2="A", v2="D", r2="A", g2="D",
    bonus="D", yT="A", ynT="A", o2="D", xcT="A", fr="A", fk="A", fv="D", x4T="A", q3="A", sum3="A", o3="D",
    **{f"vr{u}": "D" for u in range(8)})
PHASES = ("first", "steady", "last")
PRODUCTS = {p: [s for s in steps_of(p) if s in EMPTIES] for p in PHASES}
EMPTIED = {p: {e: [s for s in PRODUCTS[p] if EMPTIES[s] == e] for e in "AD"} for p in PHASES}
assert len(PRODUCTS["steady"]) == len(EMPTIES) and len(EMPTIES) % BANKS == 0
IN_ORDER = {"first": [0, 1], "steady": [0, 1, 3], "last": [3]}
FIRST = {p: {layer: sum(NJ[m] for m in IN_ORDER[p][:k]) for k, layer in enumerate(IN_ORDER[p])} for p in PHASES}
ALL_JOBS = {p: [(layer, n) for layer in IN_ORDER[p] for n in range(NJ[layer])] for p in PHASES}


def attention_jobs(layer):
    if layer == 0:
        return [(ct, bb, j) for ct in range(CT) for bb in range(PAIR) for j in range(0, 8, 2)]
    if layer == 3:
        return [(ct, bb, j) for bb in range(PAIR) for ct in range(CT) for j in (0, 4)]
    return [(gp, bb, half * 8 + ct * 4) for bb in range(PAIR) for ct in range(CT)
            for gp in range(2) for half in range(2)]


def both(front, back):
    return front, back


PER_TURN = dict(
    product=both(len(PRODUCTS["first"]), len(PRODUCTS["last"])),
    emptied_A=both(len(EMPTIED["first"]["A"]), len(EMPTIED["last"]["A"])),
    emptied_D=both(len(EMPTIED["first"]["D"]), len(EMPTIED["last"]["D"])),
    **{n: both(NJ[0] + NJ[1], NJ[3]) for n in ("keys", "scores", "masked", "exps", "turned", "pv")},
    **{n: both((NJ[0] + NJ[1]) // 2, NJ[3] // 2) for n in ("turned_D", "turned_A")},
    **{n: both(16, 0) for n in ("x_in", "c_in", "m0_in", "m1_in")},
    **{n: both(1, 0) for n in (
        "halves3", "halves1", "halves2", "stats3", "stats1", "stats2", "rstd3", "rstd1", "rstd2", "rstd0",
        "veps3", "veps1", "veps2", "veps0", "cn", "xo",
        "xb2", "ssq", "hn", "xb1", "n1", "gamma", "x2", "n2", "new_cols", "state_cols", "inverse0", "inverse1",
        "summed0", "summed1", "attn0", "attn1")},
    mask_bias0=both(2, 0), mask_bias3=both(0, 1), m3_in=both(0, 16), s0_in=both(0, 32), out_done=both(0, 16),
    xf=both(0, 5), seed=both(0, 8), scan=both(0, 8), z=both(0, 8), gathered=both(0, 8), first_token=both(0, 2),
    shift=both(0, 2),
    **{n: both(0, 1) for n in (
        "halves4", "stats4", "veps4", "rstd4", "rstd_g", "gdev", "xxx", "w", "ruk", "gate_tanh", "y", "gsum", "yc", "sq", "gvar", "yn",
        "y2", "n4", "xk2", "xr2", "kk", "tmpv", "x4", "inverse3", "summed3", "attn3")})
AHEAD = {"attn3", "out_done", "mask_bias3", "seed"}


def build(nc, x, ctx, m0, m1, m3, wl0, wl1, wl2, wl3, cols, rows, gate, out):
    x = x.rearrange("(n b) t c -> n t b c", b=PAIR)
    out = out.rearrange("(n b) t c -> n t b c", b=PAIR)
    ctx_in = ctx.rearrange("(n b) t c -> n t b c", b=PAIR)
    state_in = ctx.rearrange("(n b) t c -> n b (t c)", b=PAIR)[:, :, 2 * C:10 * C]\
        .rearrange("n b (k p j) -> n b p k j", k=CT, j=8)
    m0 = m0.rearrange("(n b) s -> n b s", b=PAIR)
    m3 = m3.rearrange("(n b) s -> n b s", b=PAIR)
    m1 = m1.rearrange("(n b) l s -> n l b s", b=PAIR)
    with ExitStack() as st:
        def sb(name, shape, dt=F32):
            return st.enter_context(nc.sbuf_tensor(name, [P] + shape, dt))

        def sem(name):
            return st.enter_context(nc.semaphore(name))

        def weights(prefix, table, total):
            tile = sb(prefix, [total])
            at, views = 0, {}
            for n, (kt, width) in table.items():
                views[n] = tile[:, at:at + kt * width].rearrange("p (k n) -> p k n", k=kt)
                at += kt * width
            assert at == total
            return tile, views

        def width(table):
            return sum(a * b for a, b in table.values())

        W0t, W0 = weights("w_l0", W_L0, width(W_L0))
        W1t, W1 = weights("w_l1", W_L1, width(W_L1))
        W2t, W2 = weights("w_l2", W_L2, width(W_L2))
        W3t, W3 = weights("w_l3", W_L3, width(W_L3))
        colt = sb("colt", [len(COLS), CT])
        rowt = sb("rowt", [len(ROWS), C])
        col = {n: [colt[:, k, ct:ct + 1] for ct in range(CT)] for k, n in enumerate(COLS)}
        row = {n: rowt[:, k, :] for k, n in enumerate(ROWS)}
        gate_t = sb("gate_t", [2])
        ident = sb("ident", [P])
        ones8 = sb("ones8", [P])
        head8 = sb("head8", [16])
        head16 = sb("head16", [2, 4])
        lane8 = sb("lane8", [8])
        spread_j = sb("spread", [8, P])
        gather_j = sb("gather", [8, P])

        minus_half = sb("minus_half", [PAIR])
        eps_g = sb("eps_g", [1])

        slot = [sb(f"slot{n}", [512]) for n in range(1, 22)]

        def tm(n):
            return slot[n - 1][:, :].rearrange("p (b c) -> p b c", b=PAIR)

        def cm(n):
            return slot[n - 1][:, :].rearrange("p (k t) -> p k t", k=CT)

        X, XB2, X1 = tm(1), tm(1), tm(1)
        CX = tm(2)
        xT, junk, nT, x1T = cm(3), tm(3), cm(3), cm(3)
        cT, aT = cm(4), cm(5)
        CN, XO, H, HN, XB1, Y1, N1, B16 = (tm(6) for _ in range(8))
        Q = cm(7)
        sumT, attnT = cm(8), cm(8)
        EW = tm(9)
        X2 = tm(10)
        N2, dT, N4 = tm(11), cm(11), tm(11)
        sx, y, sxc = cm(12), cm(12), cm(12)
        xxx, w0, y2a, y2 = cm(13), cm(13), cm(13), cm(13)
        tT, yt, yn = cm(14), tm(14), tm(14)
        xf = [cm(15 + f % 3) for f in range(5)]
        Dv, yc, ruk, sq = cm(15), tm(16), cm(17), tm(17)
        xr2, xk2, rr = cm(15), cm(16), tm(17)
        rT, X3, OUT = cm(18), tm(18), tm(18)
        kT, kk = cm(19), cm(19)
        vT, tmpv, X4 = cm(20), tm(20), tm(20)
        gT, x4T = cm(21), cm(21)
        shifted = sb("shifted", [CT, PAIR, P + 1])
        wP = sb("wP", [CT, PAIR, P + 1])
        new_cols = sb("new_cols", [CT, PAIR, 2])
        state_cols = sb("state_cols", [CT, PAIR, 2])
        k0T = sb("k0T", [CT, PAIR, 2 * P])
        k1T = sb("k1T", [T])
        k3T = sb("k3T", [CT, T])
        keys = sb("keys", [RING_K, 512])
        hT = sb("hT", [MT, T])
        V0 = sb("V0", [2, PAIR, 2, C])
        V1 = sb("V1", [PAIR, 4, C])
        V3 = sb("V3", [PAIR, 2, C])
        m0i = sb("m0i", [PAIR, P], I32)
        m3i = sb("m3i", [PAIR, P], U8)
        mb0 = sb("mb0", [PAIR, 2 * P])
        mb1 = sb("mb1", [PAIR, P])
        mb3 = sb("mb3", [PAIR, P])
        s0 = sb("s0", [PAIR, CT, 8])
        S = sb("S", [RING_S, 512])
        E = sb("E", [RING_E, 512])
        ET = sb("ET", [4, 4, P])
        nmax = sb("nmax", [4, 4])
        esum = {l: sb(f"esum{l}", [PAIR, 32]) for l in (0, 1, 3)}
        einv = {l: sb(f"einv{l}", [PAIR, 32]) for l in (0, 1, 3)}
        kv = sb("kv", [2, 2, PAIR, P + 1])
        SS = sb("SS", [2, 2, PAIR, P + 1])
        Z = sb("Z", [2, 2, T])
        bst = {n: sb(f"bst{n}", [PAIR, 6]) for n in (3, 1, 2, 4)}
        mv = {n: sb(f"mv{n}", [PAIR, 2]) for n in (3, 1, 2, 4)}
        rs = {n: sb(f"rs{n}", [PAIR]) for n in (0, 3, 1, 2, 4)}
        veps = {n: sb(f"veps{n}", [PAIR]) for n in (0, 3, 1, 2, 4)}
        ssq = sb("ssq", [PAIR])
        gsum = sb("gsum", [64])
        gvar = sb("gvar", [64])
        gdev = sb("gdev", [64])
        grs = sb("grs", [64])

        ring = [st.enter_context(nc.psum_tensor(f"ring{n}", [P, 512], F32)) for n in range(BANKS)]
        psS = [st.enter_context(nc.psum_tensor(f"psS{n}", [P, 512], F32)) for n in range(2)]
        psT = [st.enter_context(nc.psum_tensor(f"psT{n}", [P, 4, P], F32)) for n in range(2)]
        psO = st.enter_context(nc.psum_tensor("psO", [P, CT, T], F32))

        sems = {n: sem("s_" + n) for n in PER_TURN}
        s_w = sem("weights_in")
        s_const = sem("s_const")
        s_setup = sem("s_setup")
        s_setup_d = sem("s_setup_d")
        waited_in, i_reg = {}, {}

        def counts(phase, i):
            def per(name):
                return sum(PER_TURN[name])

            def here(name):
                front, back = PER_TURN[name]
                return {"first": front, "steady": front + back, "last": back}[phase]

            def upto(name, k):
                front = PER_TURN[name][0]
                k = k + (name in AHEAD)
                if phase == "first":
                    return k
                if phase == "last":
                    return front + (TURNS - 1) * per(name) + k
                return i * per(name) + (front + k)

            def turn(name, k=None):
                return upto(name, here(name) if k is None else k)

            def before(name):
                assert phase != "first" and (PER_TURN[name][0] or name in AHEAD)
                return upto(name, 0)

            def product(name):
                return turn("product", PRODUCTS[phase].index(name) + 1)

            def left(name):
                return turn("emptied_" + EMPTIES[name], EMPTIED[phase][EMPTIES[name]].index(name) + 1)

            return turn, before, product, left

        def bank(phase, name):
            front = len(PRODUCTS["first"]) if phase != "first" else 0
            return ring[(front + PRODUCTS[phase].index(name)) % BANKS][:, :].rearrange("p (a b) -> p a b", a=2)

        def leaves(name):
            return sems["emptied_" + EMPTIES[name]]

        def counted(eng, phase, turn, *signals):
            if phase != "steady":
                return [turn(name, k) for name, k in signals]
            for (name, k), reg in zip(signals, waited_in[eng]):
                front, back = PER_TURN[name]
                eng.reg_mul(reg, i_reg[eng], front + back)
                eng.reg_add(reg, reg, front + (front + back if k is None else k) + (name in AHEAD))
            return waited_in[eng]

        block = st.enter_context(nc.Block())

        @block.sync
        def _(sp):
            sp.dma_start(W0t[:, :], wl0).then_inc(s_w, 16)
            sp.dma_start(colt[:, :, :], cols).then_inc(s_w, 16)
            sp.dma_start(rowt[:, :, :], rows.partition_broadcast(P)).then_inc(s_w, 16)
            sp.dma_start(gate_t[:, 0:1], gate.partition_broadcast(P)).then_inc(s_w, 16)
            sp.dma_start(W3t[:, :], wl3).then_inc(s_w, 16)
            sp.dma_start(W1t[:, :], wl1).then_inc(s_w, 16)
            sp.dma_start(W2t[:, :], wl2).then_inc(s_w, 16)

            waited_in[sp] = [sp.alloc_register("count0_sp")]
            i_reg[sp] = sp.alloc_register("turn_sp")
            sp.reg_mov(i_reg[sp], 0)

            def program(phase, i):
                turn, before, product, left = counts(phase, i)
                if phase != "last":
                    ahead = 0 if phase == "first" else i
                    skip = 0 if phase == "first" else 1
                    if phase == "steady":
                        sp.wait_ge(sems["xb1"], before("xb1"))
                    sp.dma_start(X, x[skip:][ahead]).then_inc(sems["x_in"], 16)
                    if phase == "steady":
                        sp.wait_ge(sems["cn"], before("cn"))
                    sp.dma_start(CX, ctx_in[skip:][ahead]).then_inc(sems["c_in"], 16)
                    if phase == "steady":
                        sp.wait_ge(sems["mask_bias0"], before("mask_bias0"))
                    sp.dma_start(m0i[:, :, :], m0[skip:][ahead].partition_broadcast(P)).then_inc(sems["m0_in"], 16)
                if phase != "first":
                    pair = TURNS - 1 if phase == "last" else i
                    sp.wait_ge(sems["mask_bias3"], before("mask_bias3"))
                    sp.dma_start(m3i[:, :, :], m3[pair].partition_broadcast(P)).then_inc(sems["m3_in"], 16)
                    sp.wait_ge(sems["seed"], before("seed"))
                    for bb in range(PAIR):
                        sp.dma_start(s0[:, bb, :, :], state_in[pair][bb]).then_inc(sems["s0_in"], 16)
                if phase != "last":
                    if phase == "steady":
                        sp.wait_ge(sems["masked"], before("masked"))
                    sp.dma_start(mb1[:, :, :], m1[skip:][ahead]).then_inc(sems["m1_in"], 16)
                if phase != "first":
                    emptied = "emptied_D", EMPTIED[phase]["D"].index("o3") + 1
                    at = counted(sp, phase, turn, emptied)
                    sp.wait_ge(s_w, WEIGHTS_IN)
                    sp.wait_ge(leaves("o3"), at[0])
                    sp.dma_start(out[pair], OUT).then_inc(sems["out_done"], 16)
                if phase == "steady":
                    sp.reg_add(i_reg[sp], i_reg[sp], 1)

            program("first", None)
            with sp.Fori(0, TURNS - 1) as i:
                program("steady", i)
            program("last", None)
            sp.wait_ge(sems["out_done"], TURNS * 16 + 1)

        @block.tensor
        def _(pe):
            pe.wait_ge(s_setup_d, 4)
            pe.wait_ge(s_w, WEIGHTS_IN)

            def program(phase, i):
                turn, before, product, left = counts(phase, i)
                first_job = FIRST[phase]

                def start(name):
                    n = PRODUCTS[phase].index(name)
                    if n >= BANKS:
                        last = PRODUCTS[phase][n - BANKS]
                        pe.wait_ge(leaves(last), left(last))
                    elif phase != "first":
                        pe.wait_ge(sems["emptied_A"], before("emptied_A"))
                        pe.wait_ge(sems["emptied_D"], before("emptied_D"))
                    return bank(phase, name)

                def transposes(name, src):
                    b = start(name)
                    for a in range(2):
                        for c in range(2):
                            m = pe.transpose(b[:, c, a * P:(a + 1) * P], src[:, a, c * P:(c + 1) * P], ident[:, :])
                    m.then_inc(sems["product"], 1)

                def channel_major(name, w, src, tiles=2, m0=0):
                    b = start(name)
                    kt = w.shape[1]
                    for a in range(tiles):
                        for k in range(kt):
                            m = pe.matmul(b[:, a, :], w[:, k, m0 + a * P:m0 + (a + 1) * P], src[:, k, :],
                                          start=(k == 0), stop=(k == kt - 1))
                    m.then_inc(sems["product"], 1)

                def token_major(name, src, w):
                    b = start(name)
                    kt, n = w.shape[1], w.shape[2]
                    for bb in range(PAIR):
                        for k in range(kt):
                            m = pe.matmul(b[:, bb, 0:n], src[:, k, bb * P:(bb + 1) * P], w[:, k, :],
                                          start=(k == 0), stop=(k == kt - 1))
                    m.then_inc(sems["product"], 1)

                def scores(layer, n):
                    g = first_job[layer] + n
                    t, bb, _ = attention_jobs(layer)[n]
                    if n == 0:
                        q = {0: "q0", 1: "q1", 3: "q3"}[layer]
                        pe.wait_ge(leaves(q), left(q))
                    if g >= 2:
                        pe.wait_ge(sems["masked"], turn("masked", g - 1))
                    elif phase != "first":
                        pe.wait_ge(sems["masked"], before("masked"))
                    pe.wait_ge(sems["keys"], turn("keys", g + 1))
                    pe.matmul(psS[g % 2][:, :], Q[:, t, bb * P:(bb + 1) * P], keys[:, g % RING_K, :],
                              start=True, stop=True).then_inc(sems["scores"], 1)

                def turn_over(layer, n):
                    g = first_job[layer] + n
                    copied = "turned_D" if g % 2 == 0 else "turned_A"
                    pe.wait_ge(sems["exps"], turn("exps", g + 1))
                    if g >= 2:
                        pe.wait_ge(sems[copied], turn(copied, g // 2))
                    elif phase != "first":
                        pe.wait_ge(sems[copied], before(copied))
                    for k in range(4):
                        m = pe.transpose(psT[g % 2][:, k, :], E[:, g % RING_E, k * P:(k + 1) * P], ident[:, :])
                    m.then_inc(sems["turned"], 1)

                def weigh(layer, n):
                    g = first_job[layer] + n
                    t, bb, j = attention_jobs(layer)[n]
                    cols_ = slice(bb * P, (bb + 1) * P)
                    if layer == 0 and n == 1 and phase == "steady":
                        pe.wait_ge(sems["attn3"], before("attn3"))
                    if layer == 1 and n == 0:
                        if phase == "first":
                            pe.wait_ge(sems["attn0"], turn("attn0"))
                        else:
                            pe.wait_ge(sems["y"], turn("y"))
                    if layer == 3 and n == 0:
                        if phase == "steady":
                            pe.wait_ge(sems["attn1"], turn("attn1"))
                        else:
                            pe.wait_ge(sems["y"], turn("y"))
                    if n <= 1:
                        for v in {0: ("v0c", "v0l"), 1: ("v1",), 3: ()}[layer]:
                            pe.wait_ge(leaves(v), left(v))
                    if layer == 0 and n % 2 == 0:
                        return
                    pe.wait_ge(sems["turned_D"], turn("turned_D", (g + 2) // 2))
                    pe.wait_ge(sems["turned_A"], turn("turned_A", (g + 1) // 2))
                    if layer == 0:
                        par = j // 4
                        for sblk in range(2):
                            for s in range(4):
                                e = ET[:, (g - 1 + s // 2) % 4, (s % 2) * 2 + sblk, :]
                                m = pe.matmul(psO[32 * s:32 * s + 32, t, cols_],
                                              V0[:, sblk, bb, par, t * P + 32 * s:t * P + 32 * s + 32], e,
                                              start=(par == 0 and sblk == 0), stop=(par == 1 and sblk == 1),
                                              skip_group_check=True)
                        m.then_inc(sems["pv"], 2)
                        return
                    if layer == 3:
                        V, ct, kept, last = V3, t, j // 4, 1
                    else:
                        V, ct, kept, last = V1, (j % 8) // 4, 2 * t + j // 8, 3
                    for s in range(4):
                        m = pe.matmul(psO[32 * s:32 * s + 32, ct, cols_],
                                      V[:, bb, kept, ct * P + 32 * s:ct * P + 32 * s + 32],
                                      ET[:, g % 4, s, :], start=(kept == 0), stop=(kept == last),
                                      skip_group_check=True)
                    m.then_inc(sems["pv"], 1)

                def spread_v(u):
                    ct, j = u // 4, 2 * (u % 4)
                    b = start(f"vr{u}")
                    for a in range(2):
                        m = pe.matmul(b[:, a, :], spread_j[:, j + a, :], vT[:, ct, :], start=True, stop=True)
                    m.then_inc(sems["product"], 1)

                def gather_y(u):
                    ct, j = u // 4, 2 * (u % 4)
                    if u == 0:
                        if phase == "steady":
                            pe.wait_ge(sems["attn0"], turn("attn0"))
                        else:
                            pe.wait_ge(sems["attn3"], before("attn3"))
                    pe.wait_ge(sems["z"], turn("z", u + 1))
                    for a in range(2):
                        m = pe.matmul(psO[:, ct, :], gather_j[:, j + a, :], Z[:, u % 2, a, :],
                                      start=(j + a == 0), stop=(j + a == 7), skip_group_check=True)
                    m.then_inc(sems["gathered"], 1)

                for step in steps_of(phase):
                    if step[0] == "job":
                        _, layer, n = step
                        if n < NJ[layer]:
                            scores(layer, n)
                        if 0 <= n - 2 < NJ[layer]:
                            turn_over(layer, n - 2)
                        if 0 <= n - 4 < NJ[layer]:
                            weigh(layer, n - 4)
                    elif step in ("sum0", "sum1", "sum3"):
                        pe.wait_ge(sems["summed" + step[3]], turn("summed" + step[3]))
                        transposes(step, EW)
                    elif step == "xT":
                        pe.wait_ge(sems["x_in"], turn("x_in"))
                        transposes("xT", X)
                    elif step == "cT":
                        pe.wait_ge(sems["c_in"], turn("c_in"))
                        transposes("cT", CX)
                    elif step == "q0":
                        pe.wait_ge(leaves("xT"), left("xT"))
                        channel_major("q0", W0["q"], xT)
                    elif step == "k0c":
                        pe.wait_ge(leaves("cT"), left("cT"))
                        channel_major("k0c", W0["k"], cT)
                    elif step == "k0l":
                        channel_major("k0l", W0["k"], xT)
                    elif step == "v0c":
                        token_major("v0c", cT, W0["v"])
                    elif step == "v0l":
                        token_major("v0l", xT, W0["v"])
                    elif step == "o0":
                        pe.wait_ge(sems["attn0"], turn("attn0"))
                        token_major("o0", attnT, W0["o"])
                    elif step == "nT":
                        pe.wait_ge(sems["hn"], turn("hn"))
                        transposes("nT", HN)
                    elif step in ("u0", "u1", "u2", "u3"):
                        pe.wait_ge(leaves("nT"), left("nT"))
                        channel_major(step, W0["w1"], nT, m0=int(step[1]) * C)
                    elif step == "m2":
                        pe.wait_ge(leaves("u3"), left("u3"))
                        token_major("m2", hT, W0["w2"])
                    elif step == "k1":
                        channel_major("k1", W1["k"], cT, tiles=1)
                    elif step == "v1":
                        token_major("v1", cT, W1["v"])
                    elif step == "x1T":
                        pe.wait_ge(leaves("m2"), left("m2"))
                        transposes("x1T", X1)
                    elif step == "q1":
                        pe.wait_ge(leaves("x1T"), left("x1T"))
                        channel_major("q1", W1["q"], x1T)
                    elif step == "o1":
                        pe.wait_ge(sems["attn1"], turn("attn1"))
                        token_major("o1", attnT, W1["o"])
                    elif step == "xaT":
                        pe.wait_ge(sems["n2"], before("n2"))
                        transposes("xaT", N2)
                    elif step == "t":
                        pe.wait_ge(sems["xxx"], turn("xxx"))
                        b = start("t")
                        for a, n in ((0, P), (1, LORA)):
                            for k in range(CT):
                                m = pe.matmul(b[0:n, a, :], W2["m1"][:, k, a * P:a * P + n], xxx[:, k, :],
                                              start=(k == 0), stop=(k == CT - 1))
                        m.then_inc(sems["product"], 1)
                    elif step in ("mw", "mk", "mv", "mr", "mg"):
                        f = ("mw", "mk", "mv", "mr", "mg").index(step)
                        pe.wait_ge(leaves("t"), left("t"))
                        b = start(step)
                        r0 = 32 * (f % 4)
                        lora = W2["m2"] if f < 4 else W2["m2g"]
                        for a in range(CT):
                            m = pe.matmul(b[:, a, :], lora[r0:r0 + 32, 0, a * P:(a + 1) * P],
                                          tT[r0:r0 + 32, f // 4, :], start=True, stop=True)
                        m.then_inc(sems["product"], 1)
                    elif step == "d1":
                        pe.wait_ge(sems["xf"], turn("xf", 1))
                        b = start("d1")
                        for k in range(CT):
                            m = pe.matmul(b[0:DECAY, 0, :], W2["d1"][:, k, :], xf[0][:, k, :],
                                          start=(k == 0), stop=(k == CT - 1))
                        m.then_inc(sems["product"], 1)
                    elif step == "d2":
                        pe.wait_ge(leaves("d1"), left("d1"))
                        b = start("d2")
                        for a in range(CT):
                            m = pe.matmul(b[:, a, :], W2["d2"][0:DECAY, 0, a * P:(a + 1) * P], dT[0:DECAY, 0, :],
                                          start=True, stop=True)
                        m.then_inc(sems["product"], 1)
                    elif step in ("k2", "v2", "r2", "g2"):
                        f = {"k2": 1, "v2": 2, "r2": 3, "g2": 4}[step]
                        pe.wait_ge(sems["xf"], turn("xf", f + 1))
                        channel_major(step, W2[step[0]], xf[f])
                    elif step == "bonus":
                        pe.wait_ge(sems["ruk"], turn("ruk"))
                        b = start("bonus")
                        for a in range(CT):
                            m = pe.matmul(b[:, a, :], ones8[:, :], ruk[:, a, :], start=True, stop=True)
                        m.then_inc(sems["product"], 1)
                    elif step[0:2] == "vr":
                        pe.wait_ge(leaves("v2"), left("v2"))
                        spread_v(int(step[2]))
                    elif step[0] == "gather":
                        gather_y(step[1])
                    elif step == "yT":
                        pe.wait_ge(sems["y"], turn("y"))
                        transposes("yT", y)
                    elif step == "ynT":
                        pe.wait_ge(sems["yn"], turn("yn"))
                        transposes("ynT", yn)
                    elif step == "o2":
                        pe.wait_ge(sems["y2"], turn("y2"))
                        token_major("o2", y2, W2["o"])
                    elif step == "xcT":
                        pe.wait_ge(sems["n4"], turn("n4"))
                        transposes("xcT", N4)
                    elif step == "fr":
                        pe.wait_ge(sems["xr2"], turn("xr2"))
                        token_major("fr", xr2, W2["fr"])
                    elif step == "fk":
                        pe.wait_ge(sems["xk2"], turn("xk2"))
                        channel_major("fk", W2["fk"], xk2)
                    elif step == "fv":
                        pe.wait_ge(sems["kk"], turn("kk"))
                        token_major("fv", kk, W2["fv"])
                    elif step == "aT":
                        pe.wait_ge(sems["cn"], turn("cn"))
                        transposes("aT", CN)
                    elif step == "k3":
                        pe.wait_ge(leaves("aT"), left("aT"))
                        channel_major("k3", W3["k"], aT)
                    elif step == "v3":
                        token_major("v3", aT, W3["v"])
                    elif step == "x4T":
                        pe.wait_ge(sems["x4"], turn("x4"))
                        transposes("x4T", X4)
                    elif step == "q3":
                        pe.wait_ge(leaves("x4T"), left("x4T"))
                        channel_major("q3", W3["q"], x4T)
                    elif step == "o3":
                        pe.wait_ge(sems["attn3"], turn("attn3"))
                        token_major("o3", attnT, W3["o"])

            program("first", None)
            with pe.Fori(0, TURNS - 1) as i:
                program("steady", i)
            program("last", None)

        @block.scalar
        def _(act):
            act.wait_ge(s_w, WEIGHTS_IN)
            act.wait_ge(s_const, 3)
            act.activation(gate_t[:, 1:2], gate_t[:, 0:1], ACT.Tanh).then_inc(s_setup, 1)

            def program(phase, i):
                turn, before, product, left = counts(phase, i)
                first_job = FIRST[phase]

                def copy_out(name, dst, scale=1.0):
                    act.wait_ge(sems["product"], product(name))
                    act.activation(dst, bank(phase, name), ACT.Copy, scale=scale).then_inc(sems["emptied_A"], 1)

                def affine(name, dsts, scale, bias, func=ACT.Identity):
                    act.wait_ge(sems["product"], product(name))
                    for a, d in enumerate(dsts):
                        kw = {}
                        if bias is not None:
                            kw["bias"] = bias[a]
                        if scale is not None:
                            kw["scale"] = scale[a]
                        ins = act.activation(d, bank(phase, name)[:, a, :] if len(d.shape) == 2 else
                                             bank(phase, name)[:, a, :].rearrange("p (b t) -> p b t", b=PAIR), func,
                                             **kw)
                    ins.then_inc(sems["emptied_A"], 1)

                def exps(layer, n):
                    g = first_job[layer] + n
                    t, bb, j = attention_jobs(layer)[n]
                    act.wait_ge(sems["masked"], turn("masked", g + 1))
                    if g >= RING_E:
                        act.wait_ge(sems["turned"], turn("turned", g - RING_E + 1))
                    elif phase != "first":
                        act.wait_ge(sems["turned"], before("turned"))
                    heads = 2 if layer == 0 else 4
                    w = 512 // heads
                    for h in range(heads):
                        jj = j + h
                        if layer == 1:
                            at = (jj % 8) * 4 + 2 * t + jj // 8
                        else:
                            at = t * 8 + (jj % 4) * 2 + jj // 4
                        ins = act.activation(E[:, g % RING_E, h * w:(h + 1) * w], S[:, g % RING_S, h * w:(h + 1) * w],
                                             ACT.Exp, bias=nmax[:, g % 4, h:h + 1], scale=-1.0,
                                             accum_out=esum[layer][:, bb, at:at + 1])
                    ins.then_inc(sems["exps"], 1)

                def unturn(layer, n):
                    g = first_job[layer] + n
                    if g % 2 == 0:
                        return
                    act.wait_ge(sems["turned"], turn("turned", g + 1))
                    if g >= 4:
                        act.wait_ge(sems["pv"], turn("pv", g - 3))
                    elif phase != "first":
                        act.wait_ge(sems["pv"], before("pv"))
                    act.activation(ET[:, g % 4, :, :], psT[g % 2][:, :, :], ACT.Copy).then_inc(sems["turned_A"], 1)

                for step in steps_of(phase):
                    if step[0] == "job":
                        _, layer, n = step
                        if n < NJ[layer]:
                            exps(layer, n)
                        if 0 <= n - 3 < NJ[layer]:
                            unturn(layer, n - 3)
                    elif step in ("sum0", "sum1", "sum3"):
                        copy_out(step, sumT)
                    elif step == "xT":
                        copy_out("xT", xT)
                    elif step in ("k0c", "k0l"):
                        if step == "k0c" and phase == "steady":
                            act.wait_ge(sems["keys"], before("keys"))
                        at = 0 if step == "k0c" else P
                        affine(step, [k0T[:, a, :, at:at + P] for a in range(CT)], None, col["k0_b"])
                    elif step == "aT":
                        affine("aT", [aT[:, a, :] for a in range(CT)], col["ln3_w"], col["ln3_b"])
                    elif step == "k3":
                        if phase == "steady":
                            act.wait_ge(sems["keys"], turn("keys"))
                        copy_out("k3", k3T[:, :, :])
                    elif step == "hn":
                        act.wait_ge(leaves("o0"), left("o0"))
                        for bb in range(PAIR):
                            ins = act.activation(junk[:, bb, :], H[:, bb, :], ACT.Square, scale=C ** -0.5,
                                                 accum_out=ssq[:, bb:bb + 1])
                        ins.then_inc(sems["ssq"], 1)
                        act.wait_ge(sems["rstd0"], turn("rstd0"))
                        for bb in range(PAIR):
                            ins = act.activation(HN[:, bb, :], H[:, bb, :], ACT.Copy, scale=rs[0][:, bb:bb + 1])
                        ins.then_inc(sems["hn"], 1)
                    elif step in ("u0", "u1", "u2", "u3"):
                        u = int(step[1])
                        affine(step, [hT[:, 2 * u + a, :] for a in range(2)], None, col[f"b1_{u}"],
                               ACT.Gelu_apprx_tanh)
                    elif step == "x1T":
                        copy_out("x1T", x1T)
                    elif step == "k1":
                        act.wait_ge(sems["product"], product("k1"))
                        act.activation(k1T[:, :], bank(phase, "k1")[:, 0, :], ACT.Identity,
                                       bias=col["k1_b"][0]).then_inc(sems["emptied_A"], 1)
                    elif step == "xaT":
                        affine("xaT", [shifted[:, a, :, 1:P + 1] for a in range(CT)], col["ln1_w"], col["ln1_b"])
                    elif step == "t":
                        act.wait_ge(sems["product"], product("t"))
                        act.activation(tT[:, 0, :], bank(phase, "t")[:, 0, :], ACT.Tanh)
                        act.activation(tT[0:LORA, 1, :], bank(phase, "t")[0:LORA, 1, :], ACT.Tanh)\
                            .then_inc(sems["emptied_A"], 1)
                    elif step == "d1":
                        act.wait_ge(sems["product"], product("d1"))
                        act.activation(dT[0:DECAY, 0, :], bank(phase, "d1")[0:DECAY, 0, :], ACT.Tanh)\
                            .then_inc(sems["emptied_A"], 1)
                    elif step == "d2":
                        affine("d2", [w0[:, a, :] for a in range(CT)], None, col["decay"], ACT.Exp)
                    elif step == "decay":
                        act.wait_ge(leaves("d2"), left("d2"))
                        for a in range(CT):
                            ins = act.activation(wP[:, a, :, 1:P + 1], w0[:, a, :].rearrange("p (b t) -> p b t", b=PAIR),
                                                 ACT.Exp, scale=-1.0)
                        ins.then_inc(sems["w"], 1)
                    elif step == "k2":
                        copy_out("k2", kT)
                    elif step == "r2":
                        act.wait_ge(sems["out_done"], before("out_done"))
                        copy_out("r2", rT)
                    elif step == "g2":
                        act.wait_ge(sems["product"], product("g2"))
                        act.activation(gT, bank(phase, "g2"), ACT.Tanh, scale=0.5).then_inc(sems["gate_tanh"], 1)
                    elif step == "yT":
                        copy_out("yT", yt)
                    elif step == "group":
                        act.wait_ge(sems["yc"], turn("yc"))
                        act.activation(sq, yc, ACT.Square).then_inc(sems["sq"], 1)
                    elif step == "yn":
                        act.wait_ge(sems["gvar"], turn("gvar"))
                        act.activation(gdev[:, :], gvar[:, :], ACT.Sqrt, scale=1.0 / 8, bias=eps_g[:, :])\
                            .then_inc(sems["gdev"], 1)
                    elif step == "ynT":
                        affine("ynT", [y2a[:, a, :] for a in range(CT)], col["gn_w"], col["gn_b"])
                    elif step == "xcT":
                        affine("xcT", [shifted[:, a, :, 1:P + 1] for a in range(CT)], col["ln2_w"], col["ln2_b"])
                    elif step == "fr":
                        act.wait_ge(sems["product"], product("fr"))
                        act.activation(rr, bank(phase, "fr"), ACT.Tanh, scale=0.5).then_inc(sems["emptied_A"], 1)
                    elif step == "fk":
                        act.wait_ge(sems["product"], product("fk"))
                        act.activation(kk, bank(phase, "fk"), ACT.Relu).then_inc(sems["emptied_A"], 1)
                        act.wait_ge(leaves("fk"), left("fk"))
                        act.activation(kk, kk, ACT.Square).then_inc(sems["kk"], 1)
                    elif step == "x4T":
                        copy_out("x4T", x4T)
                    elif step == "q3":
                        copy_out("q3", Q, 0.25)

            program("first", None)
            with act.Fori(0, TURNS - 1) as i:
                program("steady", i)
            program("last", None)

        @block.vector
        def _(dve):
            dve.wait_ge(s_const, 3)
            dve.tensor_reduce(head8[:, :], ident[:, :].rearrange("p (a b) -> p a b", b=8), AX.X, ALU.add)\
                .then_inc(s_setup_d, 1)
            dve.tensor_reduce(head16[:, :, :], ident[:, :].rearrange("p (s r d) -> p r s d", r=2, d=16), AX.X,
                              ALU.add).then_inc(s_setup_d, 1)
            dve.tensor_reduce(lane8[:, :], ident[:, :].rearrange("p (a b) -> p b a", b=8), AX.X, ALU.add)\
                .then_inc(s_setup_d, 1)
            dve.wait_ge(s_setup_d, 3)
            dve.tensor_copy(ones8[:, :].rearrange("p (a b) -> p a b", b=8),
                            head8[:, :].unsqueeze(2).to_broadcast([P, 16, 8]))
            for j in range(8):
                dve.tensor_scalar(spread_j[:, j, :].rearrange("p (a b) -> p a b", b=8),
                                  head8[:, :].unsqueeze(2).to_broadcast([P, 16, 8]), lane8[:, j:j + 1], None,
                                  ALU.mult)
            for j in range(8):
                ins = dve.tensor_copy(gather_j[:, j, :].rearrange("p (a b) -> p a b", b=8)[:, :, j], head8[:, :])
            ins.then_inc(s_setup_d, 1)
            dve.wait_ge(s_w, WEIGHTS_IN)
            dve.wait_ge(s_setup, 1)

            waited_in[dve] = [dve.alloc_register(f"count{n}_dve") for n in range(3)]
            i_reg[dve] = dve.alloc_register("turn_dve")
            dve.reg_mov(i_reg[dve], 0)

            def program(phase, i):
                turn, before, product, left = counts(phase, i)
                first_job = FIRST[phase]

                def norm_stats(src, n):
                    for bb in range(PAIR):
                        ins = dve.bn_stats(bst[n][:, bb, :], src[:, bb, :])
                    ins.then_inc(sems[f"halves{n}"], 1)
                    at = counted(dve, phase, turn, (f"halves{n}", None))
                    dve.wait_ge(s_w, WEIGHTS_IN)
                    dve.wait_ge(sems[f"halves{n}"], at[0])
                    for bb in range(PAIR):
                        ins = dve.bn_aggr(mv[n][:, bb, :], bst[n][:, bb, :])
                    ins.then_inc(sems[f"stats{n}"], 1)

                def normalise(dst, src, n, name):
                    dve.wait_ge(sems[f"stats{n}"], turn(f"stats{n}"))
                    dve.wait_ge(sems[f"rstd{n}"], turn(f"rstd{n}"))
                    for bb in range(PAIR):
                        ins = dve.tensor_scalar(dst[:, bb, :], src[:, bb, :], mv[n][:, bb, 0:1],
                                                rs[n][:, bb:bb + 1], ALU.subtract, ALU.mult)
                    ins.then_inc(sems[name], 1)

                def mask(layer, n):
                    g = first_job[layer] + n
                    _, bb, _ = attention_jobs(layer)[n]
                    bias = {0: mb0, 1: mb1, 3: mb3}[layer]
                    if n == 0:
                        if layer == 0:
                            dve.wait_ge(sems["mask_bias0"], turn("mask_bias0"))
                        elif layer == 3:
                            dve.wait_ge(sems["mask_bias3"], turn("mask_bias3"))
                        else:
                            dve.wait_ge(sems["m1_in"], turn("m1_in"))
                    held = max(g - RING_S + 1, 0)
                    at = counted(dve, phase, turn, ("scores", g + 1), ("exps", held))
                    dve.wait_ge(s_w, WEIGHTS_IN)
                    dve.wait_ge(sems["scores"], at[0])
                    if held > 0 or phase != "first":
                        dve.wait_ge(sems["exps"], at[1])
                    heads = 2 if layer == 0 else 4
                    w = 512 // heads
                    for h in range(heads):
                        ins = dve.tensor_tensor_reduce(S[:, g % RING_S, h * w:(h + 1) * w],
                                                       psS[g % 2][:, h * w:(h + 1) * w], bias[:, bb, :],
                                                       -1.0, HUGE, ALU.add, ALU.min,
                                                       nmax[:, g % 4, h:h + 1])
                    ins.then_inc(sems["masked"], 1)

                def unturn(layer, n):
                    g = first_job[layer] + n
                    if g % 2 == 1:
                        return
                    dve.wait_ge(sems["turned"], turn("turned", g + 1))
                    if g >= 4:
                        dve.wait_ge(sems["pv"], turn("pv", g - 3))
                    elif phase != "first":
                        dve.wait_ge(sems["pv"], before("pv"))
                    dve.tensor_copy(ET[:, g % 4, :, :], psT[g % 2][:, :, :]).then_inc(sems["turned_D"], 1)

                def inverse_sums(layer):
                    dve.wait_ge(sems["exps"], turn("exps", first_job[layer] + NJ[layer]))
                    heads = 16 if layer != 1 else 32
                    inv = einv[layer][:, :, 0:heads]
                    dve.reciprocal(inv, esum[layer][:, :, 0:heads]).then_inc(sems[f"inverse{layer}"], 1)
                    dve.wait_ge(sems[f"inverse{layer}"], turn(f"inverse{layer}"))
                    dve.tensor_copy(EW.rearrange("p b (h d) -> p b h d", h=heads),
                                    inv.unsqueeze(3).to_broadcast([P, PAIR, heads, C // heads]))\
                        .then_inc(sems[f"summed{layer}"], 1)

                def attended(layer):
                    dve.wait_ge(leaves(f"sum{layer}"), left(f"sum{layer}"))
                    dve.wait_ge(sems["pv"], turn("pv", first_job[layer] + NJ[layer]))
                    dve.tensor_tensor(attnT, psO[:, :, :], sumT, ALU.mult).then_inc(sems[f"attn{layer}"], 1)

                def values16(name, dst):
                    dve.wait_ge(sems["product"], product(name))
                    for par in range(2):
                        d = dst[:, :, par, :].rearrange("p b (s r d) -> p b s r d", r=2, d=16)[:, :, :, par, :]
                        v = bank(phase, name).rearrange("p b (s r d) -> p b s r d", r=2, d=16)[:, :, :, par, :]
                        if name == "v3":
                            ins = dve.tensor_copy(d, v)
                        else:
                            bias = row["v0_b"].rearrange("p (s r d) -> p s r d", r=2, d=16)[:, :, par, :]
                            ins = dve.tensor_tensor(d, v, bias.unsqueeze(1).to_broadcast([P, PAIR, 8, 16]), ALU.add)
                    ins.then_inc(sems["emptied_D"], 1)

                def now(a):
                    return shifted[:, a, :, 1:P + 1]

                def halves(ap):
                    return ap.rearrange("p (b t) -> p b t", b=PAIR)

                def token_shift(state_col, dst):
                    n = 2 - state_col
                    dve.tensor_copy(shifted[:, :, :, 0:1], state_cols[:, :, :, state_col:state_col + 1])\
                        .then_inc(sems["first_token"], 1)
                    dve.wait_ge(sems["first_token"], turn("first_token", n))
                    dve.tensor_tensor(dst.rearrange("p k (b t) -> p k b t", b=PAIR), shifted[:, :, :, 0:P],
                                      shifted[:, :, :, 1:P + 1], ALU.subtract).then_inc(sems["shift"], 1)
                    dve.wait_ge(sems["shift"], turn("shift", n))

                for step in steps_of(phase):
                    if step[0] == "job":
                        _, layer, n = step
                        if n < NJ[layer]:
                            mask(layer, n)
                        if 0 <= n - 3 < NJ[layer]:
                            unturn(layer, n - 3)
                    elif step in ("sum0", "sum1", "sum3"):
                        inverse_sums(int(step[3]))
                        attended(int(step[3]))
                    elif step == "cT":
                        dve.wait_ge(sems["product"], product("cT"))
                        dve.tensor_copy(cT, bank(phase, "cT")).then_inc(sems["emptied_D"], 1)
                        dve.wait_ge(sems["m0_in"], turn("m0_in"))
                        dve.tensor_scalar(mb0[:, :, 0:P], m0i[:, :, :], 0.0, -BIG, ALU.is_equal, ALU.mult)\
                            .then_inc(sems["mask_bias0"], 1)
                        dve.memset(mb0[:, :, P:2 * P], 0.0).then_inc(sems["mask_bias0"], 1)
                    elif step == "q0":
                        dve.wait_ge(sems["product"], product("q0"))
                        for a in range(CT):
                            ins = dve.tensor_scalar(Q[:, a, :], bank(phase, "q0")[:, a, :], col["q0_b"][a], 1.0 / 16,
                                                    ALU.add, ALU.mult)
                        ins.then_inc(sems["emptied_D"], 1)
                    elif step == "norm3":
                        norm_stats(CX, 3)
                        if phase == "steady":
                            dve.wait_ge(sems["x2"], before("x2"))
                        normalise(CN, CX, 3, "cn")
                        dve.wait_ge(leaves("cT"), left("cT"))
                        dve.tensor_copy(new_cols[:, :, :, :], cT.rearrange("p k (b t) -> p k b t", b=PAIR)[:, :, :, 0:2])\
                            .then_inc(sems["new_cols"], 1)
                    elif step == "v0c":
                        values16("v0c", V0[:, 0, :, :, :])
                    elif step == "v0l":
                        values16("v0l", V0[:, 1, :, :, :])
                    elif step == "o0":
                        dve.wait_ge(sems["xo"], turn("xo"))
                        dve.wait_ge(sems["product"], product("o0"))
                        dve.tensor_tensor(H, bank(phase, "o0"), XO, ALU.add).then_inc(sems["emptied_D"], 1)
                    elif step == "nT":
                        dve.wait_ge(sems["product"], product("nT"))
                        for a in range(CT):
                            ins = dve.tensor_scalar(nT[:, a, :], bank(phase, "nT")[:, a, :], col["post_w"][a], None,
                                                    ALU.mult)
                        ins.then_inc(sems["emptied_D"], 1)
                    elif step == "m2":
                        dve.wait_ge(sems["xb2"], turn("xb2"))
                        dve.wait_ge(sems["product"], product("m2"))
                        dve.tensor_tensor(X1, bank(phase, "m2"), XB2, ALU.add).then_inc(sems["emptied_D"], 1)
                    elif step == "v1":
                        dve.wait_ge(sems["product"], product("v1"))
                        for g in range(4):
                            d = V1[:, :, g, :].rearrange("p b (k g d) -> p b k g d", g=4, d=8)[:, :, :, g, :]
                            v = bank(phase, "v1")[:, :, 0:64].rearrange("p b (k d) -> p b k d", d=8)
                            bias = row["v1_b"][:, 0:64].rearrange("p (k d) -> p k d", d=8)
                            ins = dve.tensor_tensor(d, v, bias.unsqueeze(1).to_broadcast([P, PAIR, 8, 8]), ALU.add)
                        ins.then_inc(sems["emptied_D"], 1)
                    elif step == "q1":
                        dve.wait_ge(sems["product"], product("q1"))
                        for a in range(CT):
                            ins = dve.tensor_scalar(Q[:, a, :], bank(phase, "q1")[:, a, :], col["q1_b"][a], 8.0 ** -0.5,
                                                    ALU.add, ALU.mult)
                        ins.then_inc(sems["emptied_D"], 1)
                    elif step == "o1":
                        dve.wait_ge(sems["xb1"], turn("xb1"))
                        dve.wait_ge(sems["product"], product("o1"))
                        dve.tensor_tensor(Y1, bank(phase, "o1"), XB1, ALU.add).then_inc(sems["emptied_D"], 1)
                    elif step == "norm1":
                        dve.wait_ge(leaves("o1"), left("o1"))
                        norm_stats(Y1, 1)
                        normalise(N1, Y1, 1, "n1")
                    elif step == "norm2":
                        dve.wait_ge(sems["x2"], turn("x2"))
                        norm_stats(X2, 2)
                        normalise(N2, X2, 2, "n2")
                        dve.wait_ge(sems["new_cols"], turn("new_cols"))
                        dve.tensor_copy(state_cols[:, :, :, :], new_cols[:, :, :, :]).then_inc(sems["state_cols"], 1)
                    elif step == "shift1":
                        dve.wait_ge(sems["state_cols"], before("state_cols"))
                        dve.wait_ge(leaves("xaT"), left("xaT"))
                        token_shift(1, sx)
                        for a in range(CT):
                            ins = dve.scalar_tensor_tensor(halves(xxx[:, a, :]), halves(sx[:, a, :]), col["maa_x"][a],
                                                           now(a), ALU.mult, ALU.add)
                        ins.then_inc(sems["xxx"], 1)
                    elif step in ("mw", "mk", "mv", "mr", "mg"):
                        f = ("mw", "mk", "mv", "mr", "mg").index(step)
                        dve.wait_ge(sems["product"], product(step))
                        if f >= 3:
                            dve.wait_ge(sems["product"], product(("d1", "k2")[f - 3]))
                        for a in range(CT):
                            ins = dve.scalar_tensor_tensor(xf[f][:, a, :], bank(phase, step)[:, a, :],
                                                           col["maa_" + step[1]][a], sx[:, a, :], ALU.add, ALU.mult)
                        ins.then_inc(sems["emptied_D"], 1)
                    elif step == "v2":
                        dve.wait_ge(sems["product"], product("v2"))
                        dve.tensor_copy(vT, bank(phase, "v2")).then_inc(sems["emptied_D"], 1)
                    elif step == "ruk":
                        dve.wait_ge(leaves("r2"), left("r2"))
                        for a in range(CT):
                            ins = dve.scalar_tensor_tensor(ruk[:, a, :], rT[:, a, :], col["bonus"][a], kT[:, a, :],
                                                           ALU.mult, ALU.mult)
                        ins.then_inc(sems["ruk"], 1)
                    elif step == "g2":
                        dve.wait_ge(sems["gate_tanh"], turn("gate_tanh"))
                        dve.scalar_tensor_tensor(gT, gT, 1.0, bank(phase, "g2"), ALU.add, ALU.mult)\
                            .then_inc(sems["emptied_D"], 1)
                    elif step == "bonus":
                        dve.wait_ge(sems["product"], product("bonus"))
                        dve.wait_ge(leaves("v2"), left("v2"))
                        dve.tensor_tensor(Dv, bank(phase, "bonus"), vT, ALU.mult).then_inc(sems["emptied_D"], 1)
                    elif step[0:2] == "vr":
                        u = int(step[2])
                        ct = u // 4
                        if u == 0:
                            dve.wait_ge(sems["w"], turn("w"))
                        dve.wait_ge(sems["product"], product(step))
                        if u >= 2:
                            dve.wait_ge(sems["scan"], turn("scan", u - 1))
                        dve.wait_ge(sems["seed"], turn("seed", u + 1))
                        k_ = kT[:, ct, :].rearrange("p (b t) -> p b t", b=PAIR).unsqueeze(1)\
                            .to_broadcast([P, 2, PAIR, P])
                        dve.tensor_tensor(kv[:, u % 2, :, :, 1:P + 1],
                                          bank(phase, step).rearrange("p a (b t) -> p a b t", b=PAIR), k_,
                                          ALU.mult).then_inc(sems["emptied_D"], 1)
                        dve.wait_ge(leaves(step), left(step))
                        if u >= 2:
                            dve.wait_ge(sems["z"], turn("z", u - 1))
                        for a in range(2):
                            ins = dve.tensor_tensor_scan(SS[:, u % 2, a, :, :].rearrange("p b t -> p (b t)"),
                                                         wP[:, ct, :, :].rearrange("p b t -> p (b t)"),
                                                         kv[:, u % 2, a, :, :].rearrange("p b t -> p (b t)"),
                                                         0.0, ALU.mult, ALU.add)
                        ins.then_inc(sems["scan"], 1)
                    elif step == "yT":
                        dve.wait_ge(sems["gathered"], turn("gathered"))
                        dve.tensor_tensor(y, psO[:, :, :], Dv, ALU.add).then_inc(sems["y"], 1)
                    elif step == "group":
                        dve.wait_ge(leaves("yT"), left("yT"))
                        groups = yt.rearrange("p b (h d) -> p (b h) d", d=8)
                        dve.tensor_reduce(gsum[:, :], groups, AX.X, ALU.add).then_inc(sems["gsum"], 1)
                        dve.wait_ge(sems["gsum"], turn("gsum"))
                        dve.scalar_tensor_tensor(yc.rearrange("p b (h d) -> p (b h) d", d=8),
                                                 gsum[:, :].unsqueeze(2).to_broadcast([P, 64, 8]), -1.0 / 8,
                                                 groups, ALU.mult, ALU.add).then_inc(sems["yc"], 1)
                    elif step == "yn":
                        dve.wait_ge(sems["sq"], turn("sq"))
                        dve.tensor_reduce(gvar[:, :], sq.rearrange("p b (h d) -> p (b h) d", d=8), AX.X, ALU.add)\
                            .then_inc(sems["gvar"], 1)
                        dve.wait_ge(sems["gdev"], turn("gdev"))
                        dve.reciprocal(grs[:, :], gdev[:, :]).then_inc(sems["rstd_g"], 1)
                        dve.wait_ge(sems["rstd_g"], turn("rstd_g"))
                        dve.tensor_tensor(yn.rearrange("p b (h d) -> p (b h) d", d=8),
                                          yc.rearrange("p b (h d) -> p (b h) d", d=8),
                                          grs[:, :].unsqueeze(2).to_broadcast([P, 64, 8]), ALU.mult)\
                            .then_inc(sems["yn"], 1)
                    elif step == "y2":
                        dve.wait_ge(leaves("ynT"), left("ynT"))
                        dve.scalar_tensor_tensor(y2, y2a, 0.5, gT, ALU.mult, ALU.mult).then_inc(sems["y2"], 1)
                    elif step == "o2":
                        dve.wait_ge(sems["product"], product("o2"))
                        dve.tensor_tensor(X3, bank(phase, "o2"), X2, ALU.add).then_inc(sems["emptied_D"], 1)
                    elif step == "norm4":
                        dve.wait_ge(leaves("o2"), left("o2"))
                        norm_stats(X3, 4)
                        normalise(N4, X3, 4, "n4")
                    elif step == "shift0":
                        dve.wait_ge(leaves("xcT"), left("xcT"))
                        token_shift(0, sxc)
                        for name, dst in (("fmaa_r", xr2), ("fmaa_k", xk2)):
                            for a in range(CT):
                                ins = dve.scalar_tensor_tensor(halves(dst[:, a, :]), halves(sxc[:, a, :]), col[name][a],
                                                               now(a), ALU.mult, ALU.add)
                            ins.then_inc(sems["xr2" if name == "fmaa_r" else "xk2"], 1)
                    elif step == "fv":
                        dve.wait_ge(sems["product"], product("fv"))
                        dve.wait_ge(leaves("fr"), left("fr"))
                        dve.scalar_tensor_tensor(tmpv, rr, 1.0, bank(phase, "fv"), ALU.add, ALU.mult)\
                            .then_inc(sems["emptied_D"], 1)
                        dve.wait_ge(leaves("fv"), left("fv"))
                        dve.scalar_tensor_tensor(X4, tmpv, 0.5, X3, ALU.mult, ALU.add).then_inc(sems["x4"], 1)
                        dve.wait_ge(sems["m3_in"], turn("m3_in"))
                        dve.tensor_scalar(mb3[:, :, :], m3i[:, :, :], 0.0, -BIG, ALU.is_equal, ALU.mult)\
                            .then_inc(sems["mask_bias3"], 1)
                    elif step == "v3":
                        values16("v3", V3[:, :, :, :])
                    elif step == "o3":
                        dve.wait_ge(sems["product"], product("o3"))
                        dve.wait_ge(sems["x4"], turn("x4"))
                        dve.scalar_tensor_tensor(OUT, bank(phase, "o3"), gate_t[:, 1:2], X4, ALU.mult, ALU.add)\
                            .then_inc(sems["emptied_D"], 1)
                if phase == "steady":
                    dve.reg_add(i_reg[dve], i_reg[dve], 1)

            program("first", None)
            with dve.Fori(0, TURNS - 1) as i:
                program("steady", i)
            program("last", None)

        @block.gpsimd
        def _(pool):
            for name in sorted(AHEAD):
                pool.sem_inc(sems[name], 1)
            pool.memset(ident[:, :], 0.0).then_inc(s_const, 1)
            pool.wait_ge(s_const, 1)
            pool.affine_select(out=ident[:, :], in_=ident[:, :], compare_op=ALU.not_equal, fill=1.0, base=0,
                               pattern=[[-1, P]], channel_multiplier=1).then_inc(s_const, 1)
            for buf in (gather_j, V0, V1, V3, wP):
                shape = buf.shape
                pool.memset(buf[tuple(slice(None) for _ in shape)], 0.0)
            pool.memset(minus_half[:, :], -0.5)
            pool.memset(eps_g[:, :], 1e-5).then_inc(s_const, 1)
            pool.wait_ge(s_w, WEIGHTS_IN)
            pool.wait_ge(s_setup_d, 3)

            waited_in[pool] = [pool.alloc_register(f"count{n}_pool") for n in range(3)]
            i_reg[pool] = pool.alloc_register("turn_pool")
            pool.reg_mov(i_reg[pool], 0)

            def program(phase, i):
                turn, before, product, left = counts(phase, i)

                def masked_keys(g):
                    layer, n = ALL_JOBS[phase][g]
                    t, bb, j = attention_jobs(layer)[n]
                    if n == 0:
                        if layer == 3:
                            pool.wait_ge(sems["emptied_A"], before("emptied_A"))
                        else:
                            last = ("k0l", "k1")[layer]
                            pool.wait_ge(leaves(last), left(last))
                    if g >= RING_K:
                        pool.wait_ge(sems["scores"], turn("scores", g - RING_K + 1))
                    elif phase != "first":
                        pool.wait_ge(sems["scores"], before("scores"))
                    if layer == 0:
                        k_, head, heads = k0T[:, t, bb, :], head16[:, j // 4, j % 4:j % 4 + 2], 2
                    elif layer == 1:
                        k_, head, heads = k1T[:, bb * P:(bb + 1) * P], head8[:, j:j + 4], 4
                    else:
                        k_, head, heads = k3T[:, t, bb * P:(bb + 1) * P], head16[:, j // 4, 0:4], 4
                    shape = [P, heads, 512 // heads]
                    pool.tensor_tensor(keys[:, g % RING_K, :].rearrange("p (h s) -> p h s", h=heads),
                                       k_.unsqueeze(1).to_broadcast(shape), head.unsqueeze(2).to_broadcast(shape),
                                       ALU.mult).then_inc(sems["keys"], 1)

                def states_by_r(v):
                    ct = v // 4
                    pool.wait_ge(sems["scan"], turn("scan", v + 1))
                    if v >= 2:
                        pool.wait_ge(sems["gathered"], turn("gathered", v - 1))
                    for a in range(2):
                        ins = pool.tensor_tensor(Z[:, v % 2, a, :].rearrange("p (b t) -> p b t", b=PAIR),
                                                 SS[:, v % 2, a, :, 0:P],
                                                 rT[:, ct, :].rearrange("p (b t) -> p b t", b=PAIR), ALU.mult)
                    ins.then_inc(sems["z"], 1)

                def seed(u):
                    if u == 0:
                        pool.wait_ge(sems["s0_in"], turn("s0_in"))
                    if u >= 2:
                        pool.wait_ge(sems["scan"], turn("scan", u - 1))
                    ct, j = u // 4, 2 * (u % 4)
                    pool.tensor_tensor(kv[:, u % 2, :, :, 0], s0[:, :, ct, j:j + 2].rearrange("p b j -> p j b"),
                                       wP[:, :, :, 0], ALU.add).then_inc(sems["seed"], 1)

                def inverse_root(var, eps, n):
                    await_ = "ssq" if n == 0 else f"stats{n}"
                    at = counted(pool, phase, turn, (await_, None))
                    pool.wait_ge(s_w, WEIGHTS_IN)
                    pool.wait_ge(sems[await_], at[0])
                    pool.tensor_scalar(veps[n][:, :], var, eps, None, ALU.add).then_inc(sems[f"veps{n}"], 1)
                    pool.wait_ge(sems[f"veps{n}"], turn(f"veps{n}"))
                    pool.tensor_tensor(rs[n][:, :], veps[n][:, :], minus_half[:, :], ALU.pow)\
                        .then_inc(sems[f"rstd{n}"], 1)

                for step in steps_of(phase):
                    if step[0] == "job":
                        _, layer, n = step
                        if n < NJ[layer]:
                            g = FIRST[phase][layer] + n
                            for later in range(RING_K) if g == 0 else (g + RING_K - 1,):
                                if later < len(ALL_JOBS[phase]):
                                    masked_keys(later)
                    elif step == "sum0":
                        pool.wait_ge(leaves("aT"), left("aT"))
                        pool.tensor_tensor(XO, X, row["o0_b"].unsqueeze(1).to_broadcast([P, PAIR, C]), ALU.add)\
                            .then_inc(sems["xo"], 1)
                        pool.tensor_tensor(XB2, X, row["b2"].unsqueeze(1).to_broadcast([P, PAIR, C]), ALU.add)\
                            .then_inc(sems["xb2"], 1)
                    elif step == "x1T":
                        pool.wait_ge(leaves("m2"), left("m2"))
                        pool.wait_ge(leaves("x1T"), left("x1T"))
                        pool.tensor_tensor(XB1, X1, row["o1_b"].unsqueeze(1).to_broadcast([P, PAIR, C]), ALU.add)\
                            .then_inc(sems["xb1"], 1)
                    elif step == "hn":
                        inverse_root(ssq[:, :], 1e-6, 0)
                    elif step in ("norm3", "norm2", "norm4"):
                        n = int(step[4])
                        inverse_root(mv[n][:, :, 1], 1e-5, n)
                    elif step == "norm1":
                        inverse_root(mv[1][:, :, 1], 1e-6, 1)
                        pool.wait_ge(sems["n1"], turn("n1"))
                        pool.tensor_tensor(B16, N1, row["gamma"].unsqueeze(1).to_broadcast([P, PAIR, C]), ALU.mult)\
                            .then_inc(sems["gamma"], 1)
                        if phase == "steady":
                            pool.wait_ge(leaves("o2"), left("o2"))
                        pool.wait_ge(sems["gamma"], turn("gamma"))
                        pool.tensor_tensor(X2, B16, row["beta"].unsqueeze(1).to_broadcast([P, PAIR, C]), ALU.add)\
                            .then_inc(sems["x2"], 1)
                    elif step in ("mw", "mk", "mv", "mr", "mg"):
                        f = ("mw", "mk", "mv", "mr", "mg").index(step)
                        pool.wait_ge(leaves(step), left(step))
                        for a in range(CT):
                            ins = pool.tensor_tensor(xf[f][:, a, :].rearrange("p (b t) -> p b t", b=PAIR),
                                                     xf[f][:, a, :].rearrange("p (b t) -> p b t", b=PAIR),
                                                     shifted[:, a, :, 1:P + 1], ALU.add)
                        ins.then_inc(sems["xf"], 1)
                    elif step[0:2] == "vr":
                        u = int(step[2])
                        if u == 0:
                            pool.wait_ge(leaves("r2"), left("r2"))
                        seed(u)
                    elif step[0] == "gather":
                        states_by_r(step[1])
                if phase == "steady":
                    pool.reg_add(i_reg[pool], i_reg[pool], 1)

            program("first", None)
            with pool.Fori(0, TURNS - 1) as i:
                program("steady", i)
            program("last", None)


def kernel(**inputs):
    import numpy as np
    import concourse.bacc as bacc
    from concourse.bass_utils import run_bass_kernel_spmd

    a = {k: np.ascontiguousarray(v) for k, v in inputs.items()}

    def l(n, k):
        return a[f"L{n}_xattn_{k}"]

    def tiles(w):
        return w.reshape(-1, P, w.shape[1]).transpose(1, 0, 2).reshape(P, -1)

    def pad(w):
        return np.concatenate([w, np.zeros((P - w.shape[0], w.shape[1]), w.dtype)], 0) if w.shape[0] < P else w

    def column(v):
        return v.reshape(-1, P).T

    kvw = l(0, "kv_w").reshape(C, C, 2)
    kvb = l(0, "kv_b").reshape(C, 2)
    wl0 = dict(q=l(0, "q_w"), k=kvw[:, :, 0], v=kvw[:, :, 1], o=l(0, "out_w"), w1=l(0, "mlp_w1"), w2=l(0, "mlp_w2"))
    def by_group(w):
        return w.reshape(-1, 8, 4, 8).transpose(0, 2, 1, 3).reshape(-1, C)

    wl1 = dict(q=by_group(l(1, "Wq")), k=np.concatenate([l(1, "Wk")] * 2, 1), v=l(1, "Wv"), o=l(1, "Wo"))
    m2 = l(2, "maa_w2")
    wl2 = dict(m1=l(2, "maa_w1"), d1=l(2, "decay_w1"), r=l(2, "Wr").T, k=l(2, "Wk").T, v=l(2, "Wv").T,
               g=l(2, "Wg").T, o=l(2, "Wo").T, fr=l(2, "fWr").T, fk=l(2, "fWk").T, fv=l(2, "fWv").T,
               m2=m2[0:4].reshape(P, C), m2g=pad(m2[4]), d2=pad(l(2, "decay_w2")))
    wl3 = {k: l(3, "W" + k).T for k in "qkvo"}
    b1 = l(0, "mlp_b1").reshape(4, C)
    cols = dict(q0_b=l(0, "q_b"), k0_b=kvb[:, 0], b1_0=b1[0], b1_1=b1[1], b1_2=b1[2], b1_3=b1[3],
                post_w=l(0, "postnorm_w"), q1_b=by_group(l(1, "bq"))[0], k1_b=np.concatenate([l(1, "bk")] * 4),
                ln1_w=l(2, "ln1_w"), ln1_b=l(2, "ln1_b"), maa_x=l(2, "maa_x"), maa_w=l(2, "maa_w"),
                maa_k=l(2, "maa_k"), maa_v=l(2, "maa_v"), maa_r=l(2, "maa_r"), maa_g=l(2, "maa_g"),
                decay=l(2, "time_decay"), bonus=l(2, "faaaa").reshape(C), gn_w=l(2, "gn_w"), gn_b=l(2, "gn_b"),
                ln2_w=l(2, "ln2_w"), ln2_b=l(2, "ln2_b"), fmaa_k=l(2, "fmaa_k"), fmaa_r=l(2, "fmaa_r"),
                ln3_w=l(3, "ln_gamma"), ln3_b=l(3, "ln_beta"))
    rows = dict(v0_b=kvb[:, 1], o0_b=l(0, "out_b"), b2=l(0, "mlp_b2"), o1_b=l(1, "bo"), gamma=l(1, "gamma"),
                beta=l(1, "beta"), v1_b=np.concatenate([l(1, "bv")] * 4))
    arrays = dict(
        x=a["x"], ctx=a["ctx_2048"], m0=a["mask_BxS2_ik0"], m1=a["mask_Bx1xSxS2_ff0"].reshape(BATCH, P, P),
        m3=a["mask_BxS2_bf1"].view(np.uint8),
        wl0=np.concatenate([tiles(wl0[k]) for k in W_L0], 1), wl1=np.concatenate([tiles(wl1[k]) for k in W_L1], 1),
        wl2=np.concatenate([tiles(wl2[k]) for k in W_L2], 1), wl3=np.concatenate([tiles(wl3[k]) for k in W_L3], 1),
        cols=np.stack([column(cols[k]) for k in COLS], 1), rows=np.stack([rows[k] for k in ROWS])[None],
        gate=l(3, "gate").reshape(1, 1))
    nc = bacc.Bacc("TRN2", target_bir_lowering=False, num_devices=1)
    arrays = {f"in_{k}": np.ascontiguousarray(v) for k, v in arrays.items()}
    args = [nc.dram_tensor(k, v.shape, mybir.dt.from_np(v.dtype), kind="ExternalInput").ap()
            for k, v in arrays.items()]
    out = nc.dram_tensor("out", (BATCH, P, C), F32, kind="ExternalOutput").ap()
    build(nc, *args, out)
    return run_bass_kernel_spmd(nc, [arrays], core_ids=[0]).results[0]["out"]
```

```python
from contextlib import ExitStack

import concourse.bass as bass
from concourse import mybir

F32 = mybir.dt.float32
I32 = mybir.dt.int32
U8 = mybir.dt.uint8
ALU = mybir.AluOpType
ACT = mybir.ActivationFunctionType
AX = mybir.AxisListType

P = 128
BATCH = 16
PAIR = 2
TURNS = BATCH // PAIR
C = 256
CT = C // P
T = PAIR * P
MLP = 4 * C
MT = MLP // P
LORA = 32
DECAY = 64
WEIGHTS_IN = 4 * 16
BIG = 1e30
HUGE = 3e38

W_L0 = dict(q=(CT, C), k=(CT, C), v=(CT, C), o=(CT, C), w1=(CT, MLP), w2=(MT, C))
W_L1 = dict(q=(CT, C), k=(CT, P), v=(CT, 64), o=(CT, C))
W_L2 = dict(m1=(CT, 5 * LORA), d1=(CT, DECAY), r=(CT, C), k=(CT, C), v=(CT, C), g=(CT, C), o=(CT, C),
            fr=(CT, C), fk=(CT, C), fv=(CT, C), m2=(1, C), m2g=(1, C), d2=(1, C))
W_L3 = dict(q=(CT, C), k=(CT, C), v=(CT, C), o=(CT, C))
COLS = ["q0_b", "k0_b", "b1_0", "b1_1", "b1_2", "b1_3", "post_w", "q1_b", "k1_b", "ln1_w", "ln1_b", "maa_x",
        "maa_w", "maa_k", "maa_v", "maa_r", "maa_g", "decay", "bonus", "gn_w", "gn_b", "ln2_w", "ln2_b",
        "fmaa_k", "fmaa_r", "ln3_w", "ln3_b"]
ROWS = ["v0_b", "o0_b", "b2", "o1_b", "gamma", "beta", "v1_b"]

NJ = {0: 16, 1: 16, 3: 8}
DRAIN = 4
BANKS = 3
RING_K, RING_S, RING_E = 4, 2, 2


def jobs(layer, first, end):
    return [("job", layer, n) for n in range(first, end)]


SCHEDULE = [
    "norm3", "xaT", "shift1", "t", "mask0", "cols", *jobs(0, 0, 1), "mw", "mk", "mv", *jobs(0, 1, 3), "k2",
    *jobs(0, 3, 4), "apply3", "d1", *jobs(0, 4, 5), "mr", *jobs(0, 5, 6), "d2", *jobs(0, 6, 9), "v2", "mg",
    *jobs(0, 9, 10), "r2", *jobs(0, 10, 12), "ruk", *jobs(0, 12, 15), "decay", *jobs(0, 15, 16), "vr0",
    *jobs(0, 16, 17), "inv0", *jobs(0, 17, 19), "aT", "vr1", "g2", "bonus", "sum0", *jobs(0, 19, 20), "vr2",
    "o0", ("gather", 0), "vr3", ("gather", 1), "nT", "hn", "apply0", "vr4", ("gather", 2), "u0", "u1", "u2",
    "vr5", ("gather", 3), "vr6", ("gather", 4), "u3", "vr7", ("gather", 5), ("gather", 6), "m2",
    ("gather", 7), "yT", "x1T", "group", "q1", "yn", *jobs(1, 0, 1), "ynT", *jobs(1, 1, 3), "y2",
    *jobs(1, 3, 5), "o2", *jobs(1, 5, 6), "norm4", *jobs(1, 6, 8), "apply4", *jobs(1, 8, 9), "xcT",
    *jobs(1, 9, 11), "shift0", *jobs(1, 11, 13), "fr", "fk", *jobs(1, 13, 15), "fv", *jobs(1, 15, 16), "x4T",
    "q3", *jobs(1, 16, 18), *jobs(3, 0, 1), *jobs(1, 18, 19), "inv1", "sum1", *jobs(1, 19, 20),
    *jobs(3, 1, 3), "xT", "o1", "cT", *jobs(3, 3, 4), "norm1", *jobs(3, 4, 5), "q0", "k0l", "k0c", "apply1",
    *jobs(3, 5, 8), "k3", *jobs(3, 8, 9), "norm2", *jobs(3, 9, 10), "v0c", *jobs(3, 10, 11), "inv3", "v0l",
    "sum3", *jobs(3, 11, 12), "v3", "apply2", "k1", "o3", "v1"]
FIRST_ORDER = [
    "norm3", "mask0", "cols", *jobs(0, 0, 2), "apply3", *jobs(0, 2, 17), "inv0", *jobs(0, 17, 19), "aT",
    "sum0", *jobs(0, 19, 20), "o0", "nT", "hn", "apply0", "u0", "u1", "u2", "u3", "m2", "x1T", "q1",
    *jobs(1, 0, 19), "inv1", "sum1", *jobs(1, 19, 20), "xT", "o1", "cT", "norm1", "q0", "apply1", "k0l",
    "k0c", "norm2", "v0c", "v1", "k3", "v0l", "v3", "apply2", "k1"]
LAST_ORDER = [
    "xaT", "shift1", "t", "mw", "mk", "mv", "d1", "k2", "mr", "d2", "v2", "mg", "r2", "ruk", "vr0", "vr1",
    "decay", "vr2", "g2", "bonus", ("gather", 0), "vr3", ("gather", 1), "vr4", ("gather", 2), "vr5",
    ("gather", 3), "vr6", ("gather", 4), "vr7", ("gather", 5), ("gather", 6), ("gather", 7), "yT", "group",
    "yn", "ynT", "y2", "o2", "norm4", "apply4", "xcT", "fr", "fk", "shift0", "fv", "x4T", "q3",
    *jobs(3, 0, 12), "inv3", "sum3", "o3"]
ENTRY = {"xT", "cT", "q0", "k0c", "k0l", "v0c", "v0l", "k1", "v1"}
FRONT = {"mask0", "cols", "norm3", "apply3", "aT", "inv0", "sum0", "o0", "hn", "apply0", "nT", "u0", "u1", "u2", "u3",
         "m2", "x1T", "q1", "inv1", "sum1", "o1", "norm1", "apply1", "norm2", "apply2", "k3", "v3"}


def stream(step):
    if step[0] == "job":
        return 2 if step[1] == 3 else 1
    return 0 if step in ENTRY else 1 if step in FRONT else 2


HAS = {"start": (0,), "first": (0, 1), "steady": (0, 1, 2), "closing": (1, 2), "last": (2,)}
TIMES = {"start": 1, "first": 1, "steady": TURNS - 2, "closing": 1, "last": 1}
PHASES = tuple(HAS)


def steps_of(phase):
    order = {"first": FIRST_ORDER, "last": LAST_ORDER}.get(phase, SCHEDULE)
    return [s for s in order if stream(s) in HAS[phase]]


EMPTIES = dict(
    xT="A", cT="D", q0="D", k0c="A", k0l="A", v0c="D", v0l="D", k1="A", v1="D", aT="A", k3="A", v3="D",
    sum0="A", o0="D", nT="D", u0="A", u1="A", u2="A", u3="A", m2="D", x1T="A", q1="D", sum1="A", o1="D",
    xaT="A", t="A", mw="D", mk="D", mv="D", mr="D", mg="D", d1="A", d2="A", k2="A", v2="D", r2="A", g2="D",
    bonus="D", yT="A", ynT="A", o2="D", xcT="A", fr="A", fk="A", fv="D", x4T="A", q3="A", sum3="A", o3="D",
    **{f"vr{u}": "D" for u in range(8)})
PRODUCTS = {p: [s for s in steps_of(p) if s in EMPTIES] for p in PHASES}
EMPTIED = {p: {e: [s for s in PRODUCTS[p] if EMPTIES[s] == e] for e in "AD"} for p in PHASES}
assert len(PRODUCTS["steady"]) == len(EMPTIES) and len(EMPTIES) % BANKS == 0
IN_ORDER = {"start": [], "first": [0, 1], "steady": [0, 1, 3], "closing": [0, 1, 3], "last": [3]}
FIRST = {p: {layer: sum(NJ[m] for m in IN_ORDER[p][:k]) for k, layer in enumerate(IN_ORDER[p])} for p in PHASES}
ALL_JOBS = {p: [(layer, n) for layer in IN_ORDER[p] for n in range(NJ[layer])] for p in PHASES}


def attention_jobs(layer):
    if layer == 0:
        return [(ct, bb, j) for ct in range(CT) for bb in range(PAIR) for j in range(0, 8, 2)]
    if layer == 3:
        return [(ct, bb, j) for bb in range(PAIR) for ct in range(CT) for j in (0, 4)]
    return [(gp, bb, half * 8 + ct * 4) for bb in range(PAIR) for ct in range(CT)
            for gp in range(2) for half in range(2)]


def by_stream(steps):
    return tuple(sum(stream(s) == n for s in steps) for n in range(3))


PER_TURN = dict(
    product=by_stream(EMPTIES),
    emptied_A=by_stream([s for s in EMPTIES if EMPTIES[s] == "A"]),
    emptied_D=by_stream([s for s in EMPTIES if EMPTIES[s] == "D"]),
    **{n: (0, NJ[0] + NJ[1], NJ[3]) for n in ("keys", "scores", "masked", "exps", "turned", "copied", "pv")},
    **{n: (16, 0, 0) for n in ("x_in", "c_in")},
    **{n: (0, 16, 0) for n in ("m0_in", "m1_in")},
    **{n: (0, 1, 0) for n in (
        "halves3", "halves1", "halves2", "stats3", "stats1", "stats2", "rstd3", "rstd1", "rstd2", "rstd0", "veps3",
        "veps1", "veps2", "veps0", "cn", "xo", "xb2", "ssq", "hn", "xb1", "n1", "gamma", "x2", "n2", "new_cols",
        "state_cols", "inverse0", "inverse1", "summed0", "summed1", "attn0", "attn1")},
    mask_bias0=(0, 2, 0), mask_bias3=(0, 0, 1), m3_in=(0, 0, 16), s0_in=(0, 0, 32), out_done=(0, 0, 16),
    xf=(0, 0, 5), seed=(0, 0, 8), scan=(0, 0, 8), z=(0, 0, 8), gathered=(0, 0, 8), first_token=(0, 0, 2),
    shift=(0, 0, 2),
    **{n: (0, 0, 1) for n in (
        "halves4", "stats4", "veps4", "rstd4", "rstd_g", "gdev", "xxx", "w", "ruk", "gate_tanh", "y", "gsum", "yc",
        "sq", "gvar", "yn", "y2", "n4", "xk2", "xr2", "kk", "x4", "inverse3", "summed3", "attn3")})


def per_turn(phase, name):
    return sum(PER_TURN[name][n] for n in HAS[phase])


def ahead_of(phase, name):
    earlier = PHASES[:PHASES.index(phase)]
    return sum(TIMES[p] * per_turn(p, name) for p in earlier) + (name in AHEAD)


AHEAD = {"attn3", "out_done", "mask_bias3", "seed"}


def build(nc, x, ctx, m0, m1, m3, wl0, wl1, wl2, wl3, cols, rows, gate, out):
    x = x.rearrange("(n b) t c -> n t b c", b=PAIR)
    out = out.rearrange("(n b) t c -> n t b c", b=PAIR)
    ctx_in = ctx.rearrange("(n b) t c -> n t b c", b=PAIR)
    state_in = ctx.rearrange("(n b) t c -> n b (t c)", b=PAIR)[:, :, 2 * C:10 * C]\
        .rearrange("n b (k p j) -> n b p k j", k=CT, j=8)
    m0 = m0.rearrange("(n b) s -> n b s", b=PAIR)
    m3 = m3.rearrange("(n b) s -> n b s", b=PAIR)
    m1 = m1.rearrange("(n b) l s -> n l b s", b=PAIR)
    with ExitStack() as st:
        def sb(name, shape, dt=F32):
            return st.enter_context(nc.sbuf_tensor(name, [P] + shape, dt))

        def sem(name):
            return st.enter_context(nc.semaphore(name))

        def weights(prefix, table, total):
            tile = sb(prefix, [total])
            at, views = 0, {}
            for n, (kt, width) in table.items():
                views[n] = tile[:, at:at + kt * width].rearrange("p (k n) -> p k n", k=kt)
                at += kt * width
            assert at == total
            return tile, views

        def width(table):
            return sum(a * b for a, b in table.values())

        W0t, W0 = weights("w_l0", W_L0, width(W_L0))
        W1t, W1 = weights("w_l1", W_L1, width(W_L1))
        W2t, W2 = weights("w_l2", W_L2, width(W_L2))
        W3t, W3 = weights("w_l3", W_L3, width(W_L3))
        colt = sb("colt", [len(COLS), CT])
        rowt = sb("rowt", [len(ROWS), C])
        col = {n: [colt[:, k, ct:ct + 1] for ct in range(CT)] for k, n in enumerate(COLS)}
        row = {n: rowt[:, k, :] for k, n in enumerate(ROWS)}
        gate_t = sb("gate_t", [2])
        ident = sb("ident", [P])
        ones8 = sb("ones8", [P])
        head8 = sb("head8", [16])
        head16 = sb("head16", [2, 4])
        lane8 = sb("lane8", [8])
        spread_j = sb("spread", [8, P])
        gather_j = sb("gather", [8, P])
        minus_half = sb("minus_half", [PAIR])
        eps_g = sb("eps_g", [1])

        slot = [sb(f"slot{n}", [512]) for n in range(1, 23)]

        def tm(n):
            return slot[n - 1][:, :].rearrange("p (b c) -> p b c", b=PAIR)

        def cm(n):
            return slot[n - 1][:, :].rearrange("p (k t) -> p k t", k=CT)

        X, XB2, X1 = tm(1), tm(1), tm(1)
        CX, CN = tm(2), tm(2)
        xT, junk, nT, x1T = cm(3), tm(3), cm(3), cm(3)
        cT, aT = cm(4), cm(5)
        XO, H, HN, XB1, Y1, N1, B16 = (tm(6) for _ in range(7))
        Q0, Q = cm(22), cm(7)
        sumT, attnT = cm(8), cm(8)
        EW = tm(9)
        X2 = tm(10)
        N2, dT, N4 = tm(11), cm(11), tm(11)
        sx, y, sxc = cm(12), cm(12), cm(12)
        xxx, w0, y2a, y2 = cm(13), cm(13), cm(13), cm(13)
        tT, yt, yn = cm(14), tm(14), tm(14)
        xf = [cm(15 + f % 3) for f in range(5)]
        Dv, yc, ruk, sq = cm(15), tm(16), cm(17), tm(17)
        xr2, xk2, rr = cm(15), cm(16), tm(17)
        rT, X3, OUT = cm(18), tm(18), tm(18)
        kT, kk = cm(19), cm(19)
        vT, tmpv, X4 = cm(20), tm(20), tm(20)
        gT, x4T = cm(21), cm(21)
        shifted = sb("shifted", [CT, PAIR, P + 1])
        wP = sb("wP", [CT, PAIR, P + 1])
        new_cols = sb("new_cols", [CT, PAIR, 2])
        state_cols = sb("state_cols", [CT, PAIR, 2])
        k0T = sb("k0T", [CT, PAIR, 2 * P])
        k1T = sb("k1T", [T])
        k3T = sb("k3T", [CT, T])
        keys = sb("keys", [RING_K, 512])
        hT = sb("hT", [MT, T])
        V0 = sb("V0", [2, PAIR, 2, C])
        V1 = sb("V1", [PAIR, 4, C])
        V3 = sb("V3", [PAIR, 2, C])
        m0i = sb("m0i", [PAIR, P], I32)
        m3i = sb("m3i", [PAIR, P], U8)
        mb0 = sb("mb0", [PAIR, 2 * P])
        mb1 = sb("mb1", [PAIR, P])
        mb3 = sb("mb3", [PAIR, P])
        s0 = sb("s0", [PAIR, CT, 8])
        S = sb("S", [RING_S, 512])
        E = sb("E", [RING_E, 512])
        ET = sb("ET", [4, 4, P])
        nmax = sb("nmax", [4, 4])
        esum = {l: sb(f"esum{l}", [PAIR, 32]) for l in (0, 1, 3)}
        einv = {l: sb(f"einv{l}", [PAIR, 32]) for l in (0, 1, 3)}
        kv = sb("kv", [2, 2, PAIR, P + 1])
        SS = sb("SS", [2, 2, PAIR, P + 1])
        Z = sb("Z", [2, 2, T])
        bst = {n: sb(f"bst{n}", [PAIR, 6]) for n in (3, 1, 2, 4)}
        mv = {n: sb(f"mv{n}", [PAIR, 2]) for n in (3, 1, 2, 4)}
        rs = {n: sb(f"rs{n}", [PAIR]) for n in (0, 3, 1, 2, 4)}
        veps = {n: sb(f"veps{n}", [PAIR]) for n in (0, 3, 1, 2, 4)}
        ssq = sb("ssq", [PAIR])
        gsum = sb("gsum", [64])
        gvar = sb("gvar", [64])
        gdev = sb("gdev", [64])
        grs = sb("grs", [64])

        ring = [st.enter_context(nc.psum_tensor(f"ring{n}", [P, 512], F32)) for n in range(BANKS)]
        psS = [st.enter_context(nc.psum_tensor(f"psS{n}", [P, 512], F32)) for n in range(2)]
        psT = [st.enter_context(nc.psum_tensor(f"psT{n}", [P, 4, P], F32)) for n in range(2)]
        psO = st.enter_context(nc.psum_tensor("psO", [P, CT, T], F32))

        sems = {n: sem("s_" + n) for n in PER_TURN}
        s_w = sem("weights_in")
        qkv = 3 * CT * C
        s_w0, s_w1, s_w3, s_w2 = (sem(f"weights{n}_in") for n in (0, 1, 3, 2))
        s_const = sem("s_const")
        s_setup = sem("s_setup")
        s_setup_d = sem("s_setup_d")
        waited_in, i_reg = {}, {}

        def counts(phase, i):
            def turn(name, k=None):
                k = ahead_of(phase, name) + (per_turn(phase, name) if k is None else k)
                return i * per_turn(phase, name) + k if phase == "steady" else k

            def before(name):
                assert ahead_of(phase, name) > 0
                return turn(name, 0)

            def product(name):
                return turn("product", PRODUCTS[phase].index(name) + 1)

            def left(name):
                return turn("emptied_" + EMPTIES[name], EMPTIED[phase][EMPTIES[name]].index(name) + 1)

            return turn, before, product, left

        def bank(phase, name):
            made_before = ahead_of(phase, "product") + PRODUCTS[phase].index(name)
            return ring[made_before % BANKS][:, :].rearrange("p (a b) -> p a b", a=2)

        def leaves(name):
            return sems["emptied_" + EMPTIES[name]]

        def counted(eng, phase, turn, *signals):
            if phase != "steady":
                return [turn(name, k) for name, k in signals]
            for (name, k), reg in zip(signals, waited_in[eng]):
                eng.reg_mul(reg, i_reg[eng], per_turn(phase, name))
                eng.reg_add(reg, reg, ahead_of(phase, name) + (per_turn(phase, name) if k is None else k))
            return waited_in[eng]

        block = st.enter_context(nc.Block())

        @block.sync
        def _(sp):
            sp.dma_start(W0t[:, 0:qkv], wl0[:, 0:qkv]).then_inc(s_w, 16)
            sp.dma_start(colt[:, :, :], cols).then_inc(s_w, 16)
            sp.dma_start(rowt[:, :, :], rows.partition_broadcast(P)).then_inc(s_w, 16)
            sp.dma_start(gate_t[:, 0:1], gate.partition_broadcast(P)).then_inc(s_w, 16)

            waited_in[sp] = [sp.alloc_register("count0_sp")]
            i_reg[sp] = sp.alloc_register("turn_sp")
            sp.reg_mov(i_reg[sp], 0)

            def program(phase, i):
                turn, before, product, left = counts(phase, i)
                entry = {"start": 0, "first": 1, "steady": i}.get(phase)
                front = {"first": 0, "steady": i, "closing": TURNS - 1}.get(phase)
                back = {"steady": i, "closing": TURNS - 2, "last": TURNS - 1}.get(phase)
                streams = HAS[phase]
                if 1 in streams:
                    shift = 1 if phase == "steady" else 0
                    if phase != "first":
                        sp.wait_ge(sems["mask_bias0"], before("mask_bias0"))
                    sp.dma_start(m0i[:, :, :], m0[shift:][front].partition_broadcast(P)).then_inc(sems["m0_in"], 16)
                if 2 in streams:
                    sp.wait_ge(sems["mask_bias3"], before("mask_bias3"))
                    sp.dma_start(m3i[:, :, :], m3[back].partition_broadcast(P)).then_inc(sems["m3_in"], 16)
                    sp.wait_ge(sems["seed"], before("seed"))
                    for bb in range(PAIR):
                        sp.dma_start(s0[:, bb, :, :], state_in[back][bb]).then_inc(sems["s0_in"], 16)
                if 1 in streams:
                    if phase != "first":
                        sp.wait_ge(sems["masked"], before("masked"))
                    sp.dma_start(mb1[:, :, :], m1[shift:][front]).then_inc(sems["m1_in"], 16)
                if 0 in streams:
                    shift = 2 if phase == "steady" else 0
                    if phase != "start":
                        sp.wait_ge(leaves("aT"), left("aT"))
                    sp.dma_start(CX, ctx_in[shift:][entry]).then_inc(sems["c_in"], 16)
                    if phase != "start":
                        sp.wait_ge(sems["xb1"], turn("xb1"))
                    sp.dma_start(X, x[shift:][entry]).then_inc(sems["x_in"], 16)
                if 2 in streams:
                    emptied = "emptied_D", EMPTIED[phase]["D"].index("o3") + 1
                    at = counted(sp, phase, turn, emptied)
                    sp.wait_ge(s_w, WEIGHTS_IN)
                    sp.wait_ge(leaves("o3"), at[0])
                    sp.dma_start(out[back], OUT).then_inc(sems["out_done"], 16)
                if phase == "steady":
                    sp.reg_add(i_reg[sp], i_reg[sp], 1)

            program("start", None)
            sp.dma_start(W1t[:, :], wl1).then_inc(s_w1, 16)
            sp.dma_start(W0t[:, qkv:], wl0[:, qkv:]).then_inc(s_w0, 16)
            sp.dma_start(W3t[:, :], wl3).then_inc(s_w3, 16)
            sp.dma_start(W2t[:, :], wl2).then_inc(s_w2, 16)
            program("first", None)
            with sp.Fori(0, TURNS - 2) as i:
                program("steady", i)
            program("closing", None)
            program("last", None)
            sp.wait_ge(sems["out_done"], TURNS * 16 + 1)

        @block.tensor
        def _(pe):
            pe.wait_ge(s_setup_d, 4)
            pe.wait_ge(s_w, WEIGHTS_IN)

            def program(phase, i):
                turn, before, product, left = counts(phase, i)
                first_job = FIRST[phase]

                def start(name):
                    n = PRODUCTS[phase].index(name)
                    if n >= BANKS:
                        last = PRODUCTS[phase][n - BANKS]
                        pe.wait_ge(leaves(last), left(last))
                    elif phase != "start":
                        pe.wait_ge(sems["emptied_A"], before("emptied_A"))
                        pe.wait_ge(sems["emptied_D"], before("emptied_D"))
                    return bank(phase, name)

                def transposes(name, src):
                    b = start(name)
                    for a in range(2):
                        for c in range(2):
                            m = pe.transpose(b[:, c, a * P:(a + 1) * P], src[:, a, c * P:(c + 1) * P], ident[:, :])
                    m.then_inc(sems["product"], 1)

                def channel_major(name, w, src, tiles=2, m0=0):
                    b = start(name)
                    kt = w.shape[1]
                    for a in range(tiles):
                        for k in range(kt):
                            m = pe.matmul(b[:, a, :], w[:, k, m0 + a * P:m0 + (a + 1) * P], src[:, k, :],
                                          start=(k == 0), stop=(k == kt - 1))
                    m.then_inc(sems["product"], 1)

                def token_major(name, src, w):
                    b = start(name)
                    kt, n = w.shape[1], w.shape[2]
                    for bb in range(PAIR):
                        for k in range(kt):
                            m = pe.matmul(b[:, bb, 0:n], src[:, k, bb * P:(bb + 1) * P], w[:, k, :],
                                          start=(k == 0), stop=(k == kt - 1))
                    m.then_inc(sems["product"], 1)

                def scores(layer, n):
                    g = first_job[layer] + n
                    t, bb, _ = attention_jobs(layer)[n]
                    if n == 0:
                        if layer == 0:
                            pe.wait_ge(sems["emptied_D"], before("emptied_D"))
                            pe.wait_ge(sems["emptied_A"], before("emptied_A"))
                        else:
                            q = {1: "q1", 3: "q3"}[layer]
                            pe.wait_ge(leaves(q), left(q))
                    if g >= 2:
                        pe.wait_ge(sems["masked"], turn("masked", g - 1))
                    elif phase != "first":
                        pe.wait_ge(sems["masked"], before("masked"))
                    pe.wait_ge(sems["keys"], turn("keys", g + 1))
                    queries = (Q0 if layer == 0 else Q)[:, t, bb * P:(bb + 1) * P]
                    pe.matmul(psS[g % 2][:, :], queries, keys[:, g % RING_K, :], start=True, stop=True)\
                        .then_inc(sems["scores"], 1)

                def turn_over(layer, n):
                    g = first_job[layer] + n
                    pe.wait_ge(sems["exps"], turn("exps", g + 1))
                    if g >= 2:
                        pe.wait_ge(sems["copied"], turn("copied", g - 1))
                    elif phase != "first":
                        pe.wait_ge(sems["copied"], before("copied"))
                    for k in range(4):
                        m = pe.transpose(psT[g % 2][:, k, :], E[:, g % RING_E, k * P:(k + 1) * P], ident[:, :])
                    m.then_inc(sems["turned"], 1)

                def weigh(layer, n):
                    g = first_job[layer] + n
                    t, bb, j = attention_jobs(layer)[n]
                    cols_ = slice(bb * P, (bb + 1) * P)
                    if layer == 0 and n == 1 and phase != "first":
                        pe.wait_ge(sems["attn3"], before("attn3"))
                    if layer == 1 and n == 0:
                        if phase == "first":
                            pe.wait_ge(sems["attn0"], turn("attn0"))
                        else:
                            pe.wait_ge(sems["y"], turn("y"))
                    if layer == 3 and n == 0:
                        if phase != "last":
                            pe.wait_ge(sems["attn1"], turn("attn1"))
                        else:
                            pe.wait_ge(sems["y"], turn("y"))
                    if layer == 0 and n % 2 == 0:
                        return
                    pe.wait_ge(sems["copied"], turn("copied", g + 1))
                    if layer == 0:
                        par = j // 4
                        for sblk in range(2):
                            for s in range(4):
                                e = ET[:, (g - 1 + s // 2) % 4, (s % 2) * 2 + sblk, :]
                                m = pe.matmul(psO[32 * s:32 * s + 32, t, cols_],
                                              V0[:, sblk, bb, par, t * P + 32 * s:t * P + 32 * s + 32], e,
                                              start=(par == 0 and sblk == 0), stop=(par == 1 and sblk == 1),
                                              skip_group_check=True)
                        m.then_inc(sems["pv"], 2)
                        return
                    if layer == 3:
                        V, ct, kept, last = V3, t, j // 4, 1
                    else:
                        V, ct, kept, last = V1, (j % 8) // 4, 2 * t + j // 8, 3
                    for s in range(4):
                        m = pe.matmul(psO[32 * s:32 * s + 32, ct, cols_],
                                      V[:, bb, kept, ct * P + 32 * s:ct * P + 32 * s + 32],
                                      ET[:, g % 4, s, :], start=(kept == 0), stop=(kept == last),
                                      skip_group_check=True)
                    m.then_inc(sems["pv"], 1)

                def spread_v(u):
                    ct, j = u // 4, 2 * (u % 4)
                    b = start(f"vr{u}")
                    for a in range(2):
                        m = pe.matmul(b[:, a, :], spread_j[:, j + a, :], vT[:, ct, :], start=True, stop=True)
                    m.then_inc(sems["product"], 1)

                def gather_y(u):
                    ct, j = u // 4, 2 * (u % 4)
                    if u == 0:
                        if phase != "last":
                            pe.wait_ge(sems["attn0"], turn("attn0"))
                        else:
                            pe.wait_ge(sems["attn3"], before("attn3"))
                    pe.wait_ge(sems["z"], turn("z", u + 1))
                    for a in range(2):
                        m = pe.matmul(psO[:, ct, :], gather_j[:, j + a, :], Z[:, u % 2, a, :],
                                      start=(j + a == 0), stop=(j + a == 7), skip_group_check=True)
                    m.then_inc(sems["gathered"], 1)

                for step in steps_of(phase):
                    if step[0] == "job":
                        _, layer, n = step
                        if n < NJ[layer]:
                            scores(layer, n)
                        if 0 <= n - 2 < NJ[layer]:
                            turn_over(layer, n - 2)
                        if 0 <= n - 4 < NJ[layer]:
                            weigh(layer, n - 4)
                    elif step in ("sum0", "sum1", "sum3"):
                        pe.wait_ge(sems["summed" + step[3]], turn("summed" + step[3]))
                        transposes(step, EW)
                    elif step == "xT":
                        pe.wait_ge(sems["x_in"], turn("x_in"))
                        transposes("xT", X)
                    elif step == "cT":
                        pe.wait_ge(sems["c_in"], turn("c_in"))
                        transposes("cT", CX)
                    elif step == "q0":
                        pe.wait_ge(leaves("xT"), left("xT"))
                        channel_major("q0", W0["q"], xT)
                    elif step == "k0c":
                        pe.wait_ge(leaves("cT"), left("cT"))
                        channel_major("k0c", W0["k"], cT)
                    elif step == "k0l":
                        channel_major("k0l", W0["k"], xT)
                    elif step == "v0c":
                        token_major("v0c", cT, W0["v"])
                    elif step == "v0l":
                        token_major("v0l", xT, W0["v"])
                    elif step == "o0":
                        pe.wait_ge(sems["attn0"], turn("attn0"))
                        if phase == "first":
                            pe.wait_ge(s_w0, 16)
                        token_major("o0", attnT, W0["o"])
                    elif step == "nT":
                        pe.wait_ge(sems["hn"], turn("hn"))
                        transposes("nT", HN)
                    elif step in ("u0", "u1", "u2", "u3"):
                        pe.wait_ge(leaves("nT"), left("nT"))
                        channel_major(step, W0["w1"], nT, m0=int(step[1]) * C)
                    elif step == "m2":
                        pe.wait_ge(leaves("u3"), left("u3"))
                        token_major("m2", hT, W0["w2"])
                    elif step == "k1":
                        if phase == "start":
                            pe.wait_ge(s_w1, 16)
                        channel_major("k1", W1["k"], cT, tiles=1)
                    elif step == "v1":
                        token_major("v1", cT, W1["v"])
                    elif step == "x1T":
                        pe.wait_ge(leaves("m2"), left("m2"))
                        transposes("x1T", X1)
                    elif step == "q1":
                        pe.wait_ge(leaves("x1T"), left("x1T"))
                        channel_major("q1", W1["q"], x1T)
                    elif step == "o1":
                        pe.wait_ge(sems["attn1"], turn("attn1"))
                        token_major("o1", attnT, W1["o"])
                    elif step == "xaT":
                        pe.wait_ge(sems["n2"], before("n2"))
                        transposes("xaT", N2)
                    elif step == "t":
                        pe.wait_ge(sems["xxx"], turn("xxx"))
                        b = start("t")
                        for a, n in ((0, P), (1, LORA)):
                            for k in range(CT):
                                m = pe.matmul(b[0:n, a, :], W2["m1"][:, k, a * P:a * P + n], xxx[:, k, :],
                                              start=(k == 0), stop=(k == CT - 1))
                        m.then_inc(sems["product"], 1)
                    elif step in ("mw", "mk", "mv", "mr", "mg"):
                        f = ("mw", "mk", "mv", "mr", "mg").index(step)
                        pe.wait_ge(leaves("t"), left("t"))
                        b = start(step)
                        r0 = 32 * (f % 4)
                        lora = W2["m2"] if f < 4 else W2["m2g"]
                        for a in range(CT):
                            m = pe.matmul(b[:, a, :], lora[r0:r0 + 32, 0, a * P:(a + 1) * P],
                                          tT[r0:r0 + 32, f // 4, :], start=True, stop=True)
                        m.then_inc(sems["product"], 1)
                    elif step == "d1":
                        pe.wait_ge(sems["xf"], turn("xf", 1))
                        b = start("d1")
                        for k in range(CT):
                            m = pe.matmul(b[0:DECAY, 0, :], W2["d1"][:, k, :], xf[0][:, k, :],
                                          start=(k == 0), stop=(k == CT - 1))
                        m.then_inc(sems["product"], 1)
                    elif step == "d2":
                        pe.wait_ge(leaves("d1"), left("d1"))
                        b = start("d2")
                        for a in range(CT):
                            m = pe.matmul(b[:, a, :], W2["d2"][0:DECAY, 0, a * P:(a + 1) * P], dT[0:DECAY, 0, :],
                                          start=True, stop=True)
                        m.then_inc(sems["product"], 1)
                    elif step in ("k2", "v2", "r2", "g2"):
                        f = {"k2": 1, "v2": 2, "r2": 3, "g2": 4}[step]
                        pe.wait_ge(sems["xf"], turn("xf", f + 1))
                        channel_major(step, W2[step[0]], xf[f])
                    elif step == "bonus":
                        pe.wait_ge(sems["ruk"], turn("ruk"))
                        b = start("bonus")
                        for a in range(CT):
                            m = pe.matmul(b[:, a, :], ones8[:, :], ruk[:, a, :], start=True, stop=True)
                        m.then_inc(sems["product"], 1)
                    elif step[0:2] == "vr":
                        pe.wait_ge(leaves("v2"), left("v2"))
                        spread_v(int(step[2]))
                    elif step[0] == "gather":
                        gather_y(step[1])
                    elif step == "yT":
                        pe.wait_ge(sems["y"], turn("y"))
                        transposes("yT", y)
                    elif step == "ynT":
                        pe.wait_ge(sems["yn"], turn("yn"))
                        transposes("ynT", yn)
                    elif step == "o2":
                        pe.wait_ge(sems["y2"], turn("y2"))
                        token_major("o2", y2, W2["o"])
                    elif step == "xcT":
                        pe.wait_ge(sems["n4"], turn("n4"))
                        transposes("xcT", N4)
                    elif step == "fr":
                        pe.wait_ge(sems["xr2"], turn("xr2"))
                        token_major("fr", xr2, W2["fr"])
                    elif step == "fk":
                        pe.wait_ge(sems["xk2"], turn("xk2"))
                        channel_major("fk", W2["fk"], xk2)
                    elif step == "fv":
                        pe.wait_ge(sems["kk"], turn("kk"))
                        token_major("fv", kk, W2["fv"])
                    elif step == "aT":
                        pe.wait_ge(sems["cn"], turn("cn"))
                        transposes("aT", CN)
                    elif step == "k3":
                        if phase == "first":
                            pe.wait_ge(s_w3, 16)
                        pe.wait_ge(leaves("aT"), left("aT"))
                        channel_major("k3", W3["k"], aT)
                    elif step == "v3":
                        token_major("v3", aT, W3["v"])
                    elif step == "x4T":
                        pe.wait_ge(sems["x4"], turn("x4"))
                        transposes("x4T", X4)
                    elif step == "q3":
                        pe.wait_ge(leaves("x4T"), left("x4T"))
                        channel_major("q3", W3["q"], x4T)
                    elif step == "o3":
                        pe.wait_ge(sems["attn3"], turn("attn3"))
                        token_major("o3", attnT, W3["o"])

            program("start", None)
            program("first", None)
            pe.wait_ge(s_w2, 16)
            with pe.Fori(0, TURNS - 2) as i:
                program("steady", i)
            program("closing", None)
            program("last", None)

        @block.scalar
        def _(act):
            act.wait_ge(s_w, WEIGHTS_IN)
            act.wait_ge(s_const, 3)
            act.activation(gate_t[:, 1:2], gate_t[:, 0:1], ACT.Tanh).then_inc(s_setup, 1)

            def program(phase, i):
                turn, before, product, left = counts(phase, i)
                first_job = FIRST[phase]

                def copy_out(name, dst, scale=1.0):
                    act.wait_ge(sems["product"], product(name))
                    act.activation(dst, bank(phase, name), ACT.Copy, scale=scale).then_inc(sems["emptied_A"], 1)

                def affine(name, dsts, scale, bias, func=ACT.Identity):
                    act.wait_ge(sems["product"], product(name))
                    for a, d in enumerate(dsts):
                        kw = {}
                        if bias is not None:
                            kw["bias"] = bias[a]
                        if scale is not None:
                            kw["scale"] = scale[a]
                        ins = act.activation(d, bank(phase, name)[:, a, :] if len(d.shape) == 2 else
                                             bank(phase, name)[:, a, :].rearrange("p (b t) -> p b t", b=PAIR), func,
                                             **kw)
                    ins.then_inc(sems["emptied_A"], 1)

                def exps(layer, n):
                    g = first_job[layer] + n
                    t, bb, j = attention_jobs(layer)[n]
                    act.wait_ge(sems["masked"], turn("masked", g + 1))
                    if g >= RING_E:
                        act.wait_ge(sems["turned"], turn("turned", g - RING_E + 1))
                    elif phase != "first":
                        act.wait_ge(sems["turned"], before("turned"))
                    heads = 2 if layer == 0 else 4
                    w = 512 // heads
                    for h in range(heads):
                        jj = j + h
                        if layer == 1:
                            at = (jj % 8) * 4 + 2 * t + jj // 8
                        else:
                            at = t * 8 + (jj % 4) * 2 + jj // 4
                        ins = act.activation(E[:, g % RING_E, h * w:(h + 1) * w], S[:, g % RING_S, h * w:(h + 1) * w],
                                             ACT.Exp, bias=nmax[:, g % 4, h:h + 1], scale=-1.0,
                                             accum_out=esum[layer][:, bb, at:at + 1])
                    ins.then_inc(sems["exps"], 1)

                for step in steps_of(phase):
                    if step[0] == "job":
                        _, layer, n = step
                        if n < NJ[layer]:
                            exps(layer, n)
                    elif step in ("sum0", "sum1", "sum3"):
                        copy_out(step, sumT)
                    elif step == "xT":
                        copy_out("xT", xT)
                    elif step in ("k0c", "k0l"):
                        if step == "k0c" and phase != "start":
                            act.wait_ge(sems["keys"], turn("keys", NJ[0]))
                        at = 0 if step == "k0c" else P
                        affine(step, [k0T[:, a, :, at:at + P] for a in range(CT)], None, col["k0_b"])
                    elif step == "aT":
                        affine("aT", [aT[:, a, :] for a in range(CT)], col["ln3_w"], col["ln3_b"])
                    elif step == "k3":
                        if phase != "first":
                            act.wait_ge(sems["keys"], turn("keys"))
                        copy_out("k3", k3T[:, :, :])
                    elif step == "hn":
                        act.wait_ge(leaves("o0"), left("o0"))
                        for bb in range(PAIR):
                            ins = act.activation(junk[:, bb, :], H[:, bb, :], ACT.Square, scale=C ** -0.5,
                                                 accum_out=ssq[:, bb:bb + 1])
                        ins.then_inc(sems["ssq"], 1)
                    elif step == "apply0":
                        act.wait_ge(sems["rstd0"], turn("rstd0"))
                        for bb in range(PAIR):
                            ins = act.activation(HN[:, bb, :], H[:, bb, :], ACT.Copy, scale=rs[0][:, bb:bb + 1])
                        ins.then_inc(sems["hn"], 1)
                    elif step in ("u0", "u1", "u2", "u3"):
                        u = int(step[1])
                        affine(step, [hT[:, 2 * u + a, :] for a in range(2)], None, col[f"b1_{u}"],
                               ACT.Gelu_apprx_tanh)
                    elif step == "x1T":
                        copy_out("x1T", x1T)
                    elif step == "k1":
                        if phase != "start":
                            act.wait_ge(sems["keys"], turn("keys", NJ[0] + NJ[1]))
                        act.wait_ge(sems["product"], product("k1"))
                        act.activation(k1T[:, :], bank(phase, "k1")[:, 0, :], ACT.Identity,
                                       bias=col["k1_b"][0]).then_inc(sems["emptied_A"], 1)
                    elif step == "xaT":
                        affine("xaT", [shifted[:, a, :, 1:P + 1] for a in range(CT)], col["ln1_w"], col["ln1_b"])
                    elif step == "t":
                        act.wait_ge(sems["product"], product("t"))
                        act.activation(tT[:, 0, :], bank(phase, "t")[:, 0, :], ACT.Tanh)
                        act.activation(tT[0:LORA, 1, :], bank(phase, "t")[0:LORA, 1, :], ACT.Tanh)\
                            .then_inc(sems["emptied_A"], 1)
                    elif step == "d1":
                        act.wait_ge(sems["product"], product("d1"))
                        act.activation(dT[0:DECAY, 0, :], bank(phase, "d1")[0:DECAY, 0, :], ACT.Tanh)\
                            .then_inc(sems["emptied_A"], 1)
                    elif step == "d2":
                        affine("d2", [w0[:, a, :] for a in range(CT)], None, col["decay"], ACT.Exp)
                    elif step == "decay":
                        act.wait_ge(leaves("d2"), left("d2"))
                        for a in range(CT):
                            ins = act.activation(wP[:, a, :, 1:P + 1],
                                                 w0[:, a, :].rearrange("p (b t) -> p b t", b=PAIR), ACT.Exp,
                                                 scale=-1.0)
                        ins.then_inc(sems["w"], 1)
                    elif step == "k2":
                        copy_out("k2", kT)
                    elif step == "r2":
                        act.wait_ge(sems["out_done"], before("out_done"))
                        copy_out("r2", rT)
                    elif step == "g2":
                        act.wait_ge(sems["product"], product("g2"))
                        act.activation(gT, bank(phase, "g2"), ACT.Tanh, scale=0.5).then_inc(sems["gate_tanh"], 1)
                    elif step == "yT":
                        copy_out("yT", yt)
                    elif step == "group":
                        act.wait_ge(sems["yc"], turn("yc"))
                        act.activation(sq, yc, ACT.Square).then_inc(sems["sq"], 1)
                    elif step == "yn":
                        act.wait_ge(sems["gvar"], turn("gvar"))
                        act.activation(gdev[:, :], gvar[:, :], ACT.Sqrt, scale=1.0 / 8, bias=eps_g[:, :])\
                            .then_inc(sems["gdev"], 1)
                    elif step == "ynT":
                        affine("ynT", [y2a[:, a, :] for a in range(CT)], col["gn_w"], col["gn_b"])
                    elif step == "xcT":
                        affine("xcT", [shifted[:, a, :, 1:P + 1] for a in range(CT)], col["ln2_w"], col["ln2_b"])
                    elif step == "fr":
                        act.wait_ge(sems["product"], product("fr"))
                        act.activation(rr, bank(phase, "fr"), ACT.Tanh, scale=0.5).then_inc(sems["emptied_A"], 1)
                    elif step == "fk":
                        act.wait_ge(sems["product"], product("fk"))
                        act.activation(kk, bank(phase, "fk"), ACT.Relu).then_inc(sems["emptied_A"], 1)
                        act.wait_ge(leaves("fk"), left("fk"))
                        act.activation(kk, kk, ACT.Square).then_inc(sems["kk"], 1)
                    elif step == "x4T":
                        copy_out("x4T", x4T)
                    elif step == "q3":
                        copy_out("q3", Q, 0.25)

            program("start", None)
            program("first", None)
            with act.Fori(0, TURNS - 2) as i:
                program("steady", i)
            program("closing", None)
            program("last", None)

        @block.vector
        def _(dve):
            dve.wait_ge(s_const, 3)
            dve.tensor_reduce(head8[:, :], ident[:, :].rearrange("p (a b) -> p a b", b=8), AX.X, ALU.add)\
                .then_inc(s_setup_d, 1)
            dve.tensor_reduce(head16[:, :, :], ident[:, :].rearrange("p (s r d) -> p r s d", r=2, d=16), AX.X,
                              ALU.add).then_inc(s_setup_d, 1)
            dve.tensor_reduce(lane8[:, :], ident[:, :].rearrange("p (a b) -> p b a", b=8), AX.X, ALU.add)\
                .then_inc(s_setup_d, 1)
            dve.wait_ge(s_setup_d, 3)
            dve.tensor_copy(ones8[:, :].rearrange("p (a b) -> p a b", b=8),
                            head8[:, :].unsqueeze(2).to_broadcast([P, 16, 8]))
            for j in range(8):
                dve.tensor_scalar(spread_j[:, j, :].rearrange("p (a b) -> p a b", b=8),
                                  head8[:, :].unsqueeze(2).to_broadcast([P, 16, 8]), lane8[:, j:j + 1], None,
                                  ALU.mult)
            for j in range(8):
                ins = dve.tensor_copy(gather_j[:, j, :].rearrange("p (a b) -> p a b", b=8)[:, :, j], head8[:, :])
            ins.then_inc(s_setup_d, 1)
            dve.wait_ge(s_w, WEIGHTS_IN)
            dve.wait_ge(s_setup, 1)

            waited_in[dve] = [dve.alloc_register(f"count{n}_dve") for n in range(3)]
            i_reg[dve] = dve.alloc_register("turn_dve")
            dve.reg_mov(i_reg[dve], 0)

            def program(phase, i):
                turn, before, product, left = counts(phase, i)
                first_job = FIRST[phase]

                def norm_stats(src, n):
                    for bb in range(PAIR):
                        ins = dve.bn_stats(bst[n][:, bb, :], src[:, bb, :])
                    ins.then_inc(sems[f"halves{n}"], 1)
                    at = counted(dve, phase, turn, (f"halves{n}", None))
                    dve.wait_ge(s_w, WEIGHTS_IN)
                    dve.wait_ge(sems[f"halves{n}"], at[0])
                    for bb in range(PAIR):
                        ins = dve.bn_aggr(mv[n][:, bb, :], bst[n][:, bb, :])
                    ins.then_inc(sems[f"stats{n}"], 1)

                def normalise(dst, src, n, name):
                    dve.wait_ge(sems[f"stats{n}"], turn(f"stats{n}"))
                    dve.wait_ge(sems[f"rstd{n}"], turn(f"rstd{n}"))
                    for bb in range(PAIR):
                        ins = dve.tensor_scalar(dst[:, bb, :], src[:, bb, :], mv[n][:, bb, 0:1],
                                                rs[n][:, bb:bb + 1], ALU.subtract, ALU.mult)
                    ins.then_inc(sems[name], 1)

                def mask(layer, n):
                    g = first_job[layer] + n
                    _, bb, _ = attention_jobs(layer)[n]
                    bias = {0: mb0, 1: mb1, 3: mb3}[layer]
                    if n == 0:
                        if layer == 0:
                            dve.wait_ge(sems["mask_bias0"], turn("mask_bias0"))
                        elif layer == 3:
                            dve.wait_ge(sems["mask_bias3"], turn("mask_bias3"))
                        else:
                            dve.wait_ge(sems["m1_in"], turn("m1_in"))
                    held = max(g - RING_S + 1, 0)
                    at = counted(dve, phase, turn, ("scores", g + 1), ("exps", held))
                    dve.wait_ge(s_w, WEIGHTS_IN)
                    dve.wait_ge(sems["scores"], at[0])
                    if held > 0 or phase != "first":
                        dve.wait_ge(sems["exps"], at[1])
                    heads = 2 if layer == 0 else 4
                    w = 512 // heads
                    for h in range(heads):
                        ins = dve.tensor_tensor_reduce(S[:, g % RING_S, h * w:(h + 1) * w],
                                                       psS[g % 2][:, h * w:(h + 1) * w], bias[:, bb, :],
                                                       -1.0, HUGE, ALU.add, ALU.min,
                                                       nmax[:, g % 4, h:h + 1])
                    ins.then_inc(sems["masked"], 1)

                def copy_turned(layer, n):
                    g = first_job[layer] + n
                    dve.wait_ge(sems["turned"], turn("turned", g + 1))
                    if g >= 4:
                        dve.wait_ge(sems["pv"], turn("pv", g - 3))
                    elif phase != "first":
                        dve.wait_ge(sems["pv"], before("pv"))
                    dve.tensor_copy(ET[:, g % 4, :, :], psT[g % 2][:, :, :]).then_inc(sems["copied"], 1)

                def inverse_sums(layer):
                    dve.wait_ge(sems["exps"], turn("exps", first_job[layer] + NJ[layer]))
                    heads = 16 if layer != 1 else 32
                    inv = einv[layer][:, :, 0:heads]
                    dve.reciprocal(inv, esum[layer][:, :, 0:heads]).then_inc(sems[f"inverse{layer}"], 1)
                    dve.wait_ge(sems[f"inverse{layer}"], turn(f"inverse{layer}"))
                    dve.tensor_copy(EW.rearrange("p b (h d) -> p b h d", h=heads),
                                    inv.unsqueeze(3).to_broadcast([P, PAIR, heads, C // heads]))\
                        .then_inc(sems[f"summed{layer}"], 1)

                def attended(layer):
                    dve.wait_ge(leaves(f"sum{layer}"), left(f"sum{layer}"))
                    dve.wait_ge(sems["pv"], turn("pv", first_job[layer] + NJ[layer]))
                    dve.tensor_tensor(attnT, psO[:, :, :], sumT, ALU.mult).then_inc(sems[f"attn{layer}"], 1)

                def values16(name, dst):
                    dve.wait_ge(sems["product"], product(name))
                    for par in range(2):
                        d = dst[:, :, par, :].rearrange("p b (s r d) -> p b s r d", r=2, d=16)[:, :, :, par, :]
                        v = bank(phase, name).rearrange("p b (s r d) -> p b s r d", r=2, d=16)[:, :, :, par, :]
                        if name == "v3":
                            ins = dve.tensor_copy(d, v)
                        else:
                            bias = row["v0_b"].rearrange("p (s r d) -> p s r d", r=2, d=16)[:, :, par, :]
                            ins = dve.tensor_tensor(d, v, bias.unsqueeze(1).to_broadcast([P, PAIR, 8, 16]), ALU.add)
                    ins.then_inc(sems["emptied_D"], 1)

                def now(a):
                    return shifted[:, a, :, 1:P + 1]

                def halves(ap):
                    return ap.rearrange("p (b t) -> p b t", b=PAIR)

                def token_shift(state_col, dst):
                    n = 2 - state_col
                    dve.tensor_copy(shifted[:, :, :, 0:1], state_cols[:, :, :, state_col:state_col + 1])\
                        .then_inc(sems["first_token"], 1)
                    dve.wait_ge(sems["first_token"], turn("first_token", n))
                    dve.tensor_tensor(dst.rearrange("p k (b t) -> p k b t", b=PAIR), shifted[:, :, :, 0:P],
                                      shifted[:, :, :, 1:P + 1], ALU.subtract).then_inc(sems["shift"], 1)
                    dve.wait_ge(sems["shift"], turn("shift", n))

                for step in steps_of(phase):
                    if step[0] == "job":
                        _, layer, n = step
                        if n < NJ[layer]:
                            mask(layer, n)
                        if 0 <= n - 2 < NJ[layer]:
                            copy_turned(layer, n - 2)
                    elif step in ("sum0", "sum1", "sum3"):
                        attended(int(step[3]))
                    elif step in ("inv0", "inv1", "inv3"):
                        inverse_sums(int(step[3]))
                    elif step == "cT":
                        dve.wait_ge(sems["product"], product("cT"))
                        dve.tensor_copy(cT, bank(phase, "cT")).then_inc(sems["emptied_D"], 1)
                    elif step == "mask0":
                        dve.wait_ge(sems["m0_in"], turn("m0_in"))
                        dve.tensor_scalar(mb0[:, :, 0:P], m0i[:, :, :], 0.0, -BIG, ALU.is_equal, ALU.mult)\
                            .then_inc(sems["mask_bias0"], 1)
                        dve.memset(mb0[:, :, P:2 * P], 0.0).then_inc(sems["mask_bias0"], 1)
                    elif step == "q0":
                        dve.wait_ge(sems["product"], product("q0"))
                        for a in range(CT):
                            ins = dve.tensor_scalar(Q0[:, a, :], bank(phase, "q0")[:, a, :], col["q0_b"][a], 1.0 / 16,
                                                    ALU.add, ALU.mult)
                        ins.then_inc(sems["emptied_D"], 1)
                    elif step == "norm3":
                        norm_stats(CX, 3)
                    elif step == "apply3":
                        normalise(CN, CX, 3, "cn")
                    elif step == "cols":
                        dve.wait_ge(sems["emptied_D"], before("emptied_D"))
                        dve.tensor_copy(new_cols[:, :, :, :],
                                        cT.rearrange("p k (b t) -> p k b t", b=PAIR)[:, :, :, 0:2])\
                            .then_inc(sems["new_cols"], 1)
                    elif step == "v0c":
                        values16("v0c", V0[:, 0, :, :, :])
                    elif step == "v0l":
                        values16("v0l", V0[:, 1, :, :, :])
                    elif step == "o0":
                        dve.wait_ge(sems["xo"], turn("xo"))
                        dve.wait_ge(sems["product"], product("o0"))
                        dve.tensor_tensor(H, bank(phase, "o0"), XO, ALU.add).then_inc(sems["emptied_D"], 1)
                    elif step == "nT":
                        dve.wait_ge(sems["product"], product("nT"))
                        for a in range(CT):
                            ins = dve.tensor_scalar(nT[:, a, :], bank(phase, "nT")[:, a, :], col["post_w"][a], None,
                                                    ALU.mult)
                        ins.then_inc(sems["emptied_D"], 1)
                    elif step == "m2":
                        dve.wait_ge(sems["xb2"], turn("xb2"))
                        dve.wait_ge(sems["product"], product("m2"))
                        dve.tensor_tensor(X1, bank(phase, "m2"), XB2, ALU.add).then_inc(sems["emptied_D"], 1)
                    elif step == "v1":
                        dve.wait_ge(sems["product"], product("v1"))
                        for g in range(4):
                            d = V1[:, :, g, :].rearrange("p b (k g d) -> p b k g d", g=4, d=8)[:, :, :, g, :]
                            v = bank(phase, "v1")[:, :, 0:64].rearrange("p b (k d) -> p b k d", d=8)
                            bias = row["v1_b"][:, 0:64].rearrange("p (k d) -> p k d", d=8)
                            ins = dve.tensor_tensor(d, v, bias.unsqueeze(1).to_broadcast([P, PAIR, 8, 8]), ALU.add)
                        ins.then_inc(sems["emptied_D"], 1)
                    elif step == "q1":
                        dve.wait_ge(sems["product"], product("q1"))
                        for a in range(CT):
                            ins = dve.tensor_scalar(Q[:, a, :], bank(phase, "q1")[:, a, :], col["q1_b"][a], 8.0 ** -0.5,
                                                    ALU.add, ALU.mult)
                        ins.then_inc(sems["emptied_D"], 1)
                    elif step == "o1":
                        dve.wait_ge(sems["xb1"], turn("xb1"))
                        dve.wait_ge(sems["product"], product("o1"))
                        dve.tensor_tensor(Y1, bank(phase, "o1"), XB1, ALU.add).then_inc(sems["emptied_D"], 1)
                    elif step == "norm1":
                        dve.wait_ge(leaves("o1"), left("o1"))
                        norm_stats(Y1, 1)
                    elif step == "apply1":
                        normalise(N1, Y1, 1, "n1")
                    elif step == "norm2":
                        dve.wait_ge(sems["x2"], turn("x2"))
                        norm_stats(X2, 2)
                    elif step == "apply2":
                        normalise(N2, X2, 2, "n2")
                        dve.wait_ge(sems["new_cols"], turn("new_cols"))
                        dve.tensor_copy(state_cols[:, :, :, :], new_cols[:, :, :, :]).then_inc(sems["state_cols"], 1)
                    elif step == "shift1":
                        dve.wait_ge(sems["state_cols"], before("state_cols"))
                        dve.wait_ge(leaves("xaT"), left("xaT"))
                        token_shift(1, sx)
                        for a in range(CT):
                            ins = dve.scalar_tensor_tensor(halves(xxx[:, a, :]), halves(sx[:, a, :]), col["maa_x"][a],
                                                           now(a), ALU.mult, ALU.add)
                        ins.then_inc(sems["xxx"], 1)
                    elif step in ("mw", "mk", "mv", "mr", "mg"):
                        f = ("mw", "mk", "mv", "mr", "mg").index(step)
                        dve.wait_ge(sems["product"], product(step))
                        if f >= 3:
                            dve.wait_ge(sems["product"], product(("d1", "k2")[f - 3]))
                        for a in range(CT):
                            ins = dve.scalar_tensor_tensor(xf[f][:, a, :], bank(phase, step)[:, a, :],
                                                           col["maa_" + step[1]][a], sx[:, a, :], ALU.add, ALU.mult)
                        ins.then_inc(sems["emptied_D"], 1)
                        dve.wait_ge(leaves(step), left(step))
                        mixed = xf[f].rearrange("p k (b t) -> p k b t", b=PAIR)
                        dve.tensor_tensor(mixed, mixed, shifted[:, :, :, 1:P + 1], ALU.add).then_inc(sems["xf"], 1)
                    elif step == "v2":
                        dve.wait_ge(sems["product"], product("v2"))
                        dve.tensor_copy(vT, bank(phase, "v2")).then_inc(sems["emptied_D"], 1)
                    elif step == "ruk":
                        dve.wait_ge(leaves("r2"), left("r2"))
                        for a in range(CT):
                            ins = dve.scalar_tensor_tensor(ruk[:, a, :], rT[:, a, :], col["bonus"][a], kT[:, a, :],
                                                           ALU.mult, ALU.mult)
                        ins.then_inc(sems["ruk"], 1)
                    elif step == "g2":
                        dve.wait_ge(sems["gate_tanh"], turn("gate_tanh"))
                        dve.scalar_tensor_tensor(gT, gT, 1.0, bank(phase, "g2"), ALU.add, ALU.mult)\
                            .then_inc(sems["emptied_D"], 1)
                    elif step == "bonus":
                        dve.wait_ge(sems["product"], product("bonus"))
                        dve.wait_ge(leaves("v2"), left("v2"))
                        dve.tensor_tensor(Dv, bank(phase, "bonus"), vT, ALU.mult).then_inc(sems["emptied_D"], 1)
                    elif step[0:2] == "vr":
                        u = int(step[2])
                        ct = u // 4
                        if u == 0:
                            dve.wait_ge(sems["w"], turn("w"))
                        dve.wait_ge(sems["product"], product(step))
                        if u >= 2:
                            dve.wait_ge(sems["scan"], turn("scan", u - 1))
                        dve.wait_ge(sems["seed"], turn("seed", u + 1))
                        k_ = kT[:, ct, :].rearrange("p (b t) -> p b t", b=PAIR).unsqueeze(1)\
                            .to_broadcast([P, 2, PAIR, P])
                        dve.tensor_tensor(kv[:, u % 2, :, :, 1:P + 1],
                                          bank(phase, step).rearrange("p a (b t) -> p a b t", b=PAIR), k_,
                                          ALU.mult).then_inc(sems["emptied_D"], 1)
                        dve.wait_ge(leaves(step), left(step))
                        if u >= 2:
                            dve.wait_ge(sems["z"], turn("z", u - 1))
                        for a in range(2):
                            ins = dve.tensor_tensor_scan(SS[:, u % 2, a, :, :].rearrange("p b t -> p (b t)"),
                                                         wP[:, ct, :, :].rearrange("p b t -> p (b t)"),
                                                         kv[:, u % 2, a, :, :].rearrange("p b t -> p (b t)"),
                                                         0.0, ALU.mult, ALU.add)
                        ins.then_inc(sems["scan"], 1)
                    elif step == "yT":
                        dve.wait_ge(sems["gathered"], turn("gathered"))
                        dve.tensor_tensor(y, psO[:, :, :], Dv, ALU.add).then_inc(sems["y"], 1)
                    elif step == "group":
                        dve.wait_ge(leaves("yT"), left("yT"))
                        groups = yt.rearrange("p b (h d) -> p (b h) d", d=8)
                        dve.tensor_reduce(gsum[:, :], groups, AX.X, ALU.add).then_inc(sems["gsum"], 1)
                        dve.wait_ge(sems["gsum"], turn("gsum"))
                        dve.scalar_tensor_tensor(yc.rearrange("p b (h d) -> p (b h) d", d=8),
                                                 gsum[:, :].unsqueeze(2).to_broadcast([P, 64, 8]), -1.0 / 8,
                                                 groups, ALU.mult, ALU.add).then_inc(sems["yc"], 1)
                    elif step == "yn":
                        dve.wait_ge(sems["sq"], turn("sq"))
                        dve.tensor_reduce(gvar[:, :], sq.rearrange("p b (h d) -> p (b h) d", d=8), AX.X, ALU.add)\
                            .then_inc(sems["gvar"], 1)
                        dve.wait_ge(sems["gdev"], turn("gdev"))
                        dve.reciprocal(grs[:, :], gdev[:, :]).then_inc(sems["rstd_g"], 1)
                        dve.wait_ge(sems["rstd_g"], turn("rstd_g"))
                        dve.tensor_tensor(yn.rearrange("p b (h d) -> p (b h) d", d=8),
                                          yc.rearrange("p b (h d) -> p (b h) d", d=8),
                                          grs[:, :].unsqueeze(2).to_broadcast([P, 64, 8]), ALU.mult)\
                            .then_inc(sems["yn"], 1)
                    elif step == "y2":
                        dve.wait_ge(leaves("ynT"), left("ynT"))
                        dve.scalar_tensor_tensor(y2, y2a, 0.5, gT, ALU.mult, ALU.mult).then_inc(sems["y2"], 1)
                    elif step == "o2":
                        dve.wait_ge(sems["product"], product("o2"))
                        dve.tensor_tensor(X3, bank(phase, "o2"), X2, ALU.add).then_inc(sems["emptied_D"], 1)
                    elif step == "norm4":
                        dve.wait_ge(leaves("o2"), left("o2"))
                        norm_stats(X3, 4)
                    elif step == "apply4":
                        normalise(N4, X3, 4, "n4")
                    elif step == "shift0":
                        dve.wait_ge(leaves("xcT"), left("xcT"))
                        token_shift(0, sxc)
                        for name, dst in (("fmaa_r", xr2), ("fmaa_k", xk2)):
                            for a in range(CT):
                                ins = dve.scalar_tensor_tensor(halves(dst[:, a, :]), halves(sxc[:, a, :]), col[name][a],
                                                               now(a), ALU.mult, ALU.add)
                            ins.then_inc(sems["xr2" if name == "fmaa_r" else "xk2"], 1)
                    elif step == "fv":
                        dve.wait_ge(sems["product"], product("fv"))
                        dve.wait_ge(leaves("fr"), left("fr"))
                        dve.scalar_tensor_tensor(tmpv, rr, 1.0, bank(phase, "fv"), ALU.add, ALU.mult)\
                            .then_inc(sems["emptied_D"], 1)
                        dve.wait_ge(leaves("fv"), left("fv"))
                        dve.scalar_tensor_tensor(X4, tmpv, 0.5, X3, ALU.mult, ALU.add).then_inc(sems["x4"], 1)
                        dve.wait_ge(sems["m3_in"], turn("m3_in"))
                        dve.tensor_scalar(mb3[:, :, :], m3i[:, :, :], 0.0, -BIG, ALU.is_equal, ALU.mult)\
                            .then_inc(sems["mask_bias3"], 1)
                    elif step == "v3":
                        values16("v3", V3[:, :, :, :])
                    elif step == "o3":
                        dve.wait_ge(sems["product"], product("o3"))
                        dve.wait_ge(sems["x4"], turn("x4"))
                        dve.scalar_tensor_tensor(OUT, bank(phase, "o3"), gate_t[:, 1:2], X4, ALU.mult, ALU.add)\
                            .then_inc(sems["emptied_D"], 1)
                if phase == "steady":
                    dve.reg_add(i_reg[dve], i_reg[dve], 1)

            program("start", None)
            program("first", None)
            with dve.Fori(0, TURNS - 2) as i:
                program("steady", i)
            program("closing", None)
            program("last", None)

        @block.gpsimd
        def _(pool):
            for name in sorted(AHEAD):
                pool.sem_inc(sems[name], 1)
            pool.memset(ident[:, :], 0.0).then_inc(s_const, 1)
            pool.wait_ge(s_const, 1)
            pool.affine_select(out=ident[:, :], in_=ident[:, :], compare_op=ALU.not_equal, fill=1.0, base=0,
                               pattern=[[-1, P]], channel_multiplier=1).then_inc(s_const, 1)
            for buf in (gather_j, V0, V1, V3, wP):
                shape = buf.shape
                pool.memset(buf[tuple(slice(None) for _ in shape)], 0.0)
            pool.memset(minus_half[:, :], -0.5)
            pool.memset(eps_g[:, :], 1e-5).then_inc(s_const, 1)
            pool.wait_ge(s_w, WEIGHTS_IN)
            pool.wait_ge(s_setup_d, 3)

            waited_in[pool] = [pool.alloc_register(f"count{n}_pool") for n in range(3)]
            i_reg[pool] = pool.alloc_register("turn_pool")
            pool.reg_mov(i_reg[pool], 0)

            def program(phase, i):
                turn, before, product, left = counts(phase, i)

                def masked_keys(g):
                    layer, n = ALL_JOBS[phase][g]
                    t, bb, j = attention_jobs(layer)[n]
                    if n == 0:
                        pool.wait_ge(sems["emptied_A"], before("emptied_A"))
                    if g >= RING_K:
                        pool.wait_ge(sems["scores"], turn("scores", g - RING_K + 1))
                    elif phase != "first":
                        pool.wait_ge(sems["scores"], before("scores"))
                    if layer == 0:
                        k_, head, heads = k0T[:, t, bb, :], head16[:, j // 4, j % 4:j % 4 + 2], 2
                    elif layer == 1:
                        k_, head, heads = k1T[:, bb * P:(bb + 1) * P], head8[:, j:j + 4], 4
                    else:
                        k_, head, heads = k3T[:, t, bb * P:(bb + 1) * P], head16[:, j // 4, 0:4], 4
                    shape = [P, heads, 512 // heads]
                    pool.tensor_tensor(keys[:, g % RING_K, :].rearrange("p (h s) -> p h s", h=heads),
                                       k_.unsqueeze(1).to_broadcast(shape), head.unsqueeze(2).to_broadcast(shape),
                                       ALU.mult).then_inc(sems["keys"], 1)

                def states_by_r(v):
                    ct = v // 4
                    pool.wait_ge(sems["scan"], turn("scan", v + 1))
                    if v >= 2:
                        pool.wait_ge(sems["gathered"], turn("gathered", v - 1))
                    r = rT[:, ct, :].rearrange("p (b t) -> p b t", b=PAIR).unsqueeze(1).to_broadcast([P, 2, PAIR, P])
                    pool.tensor_tensor(Z[:, v % 2, :, :].rearrange("p a (b t) -> p a b t", b=PAIR),
                                       SS[:, v % 2, :, :, 0:P], r, ALU.mult).then_inc(sems["z"], 1)

                def seed(u):
                    if u == 0:
                        pool.wait_ge(sems["s0_in"], turn("s0_in"))
                    if u >= 2:
                        pool.wait_ge(sems["scan"], turn("scan", u - 1))
                    ct, j = u // 4, 2 * (u % 4)
                    pool.tensor_tensor(kv[:, u % 2, :, :, 0], s0[:, :, ct, j:j + 2].rearrange("p b j -> p j b"),
                                       wP[:, :, :, 0], ALU.add).then_inc(sems["seed"], 1)

                def inverse_root(var, eps, n):
                    await_ = "ssq" if n == 0 else f"stats{n}"
                    at = counted(pool, phase, turn, (await_, None))
                    pool.wait_ge(s_w, WEIGHTS_IN)
                    pool.wait_ge(sems[await_], at[0])
                    pool.tensor_scalar(veps[n][:, :], var, eps, None, ALU.add).then_inc(sems[f"veps{n}"], 1)
                    pool.wait_ge(sems[f"veps{n}"], turn(f"veps{n}"))
                    pool.tensor_tensor(rs[n][:, :], veps[n][:, :], minus_half[:, :], ALU.pow)\
                        .then_inc(sems[f"rstd{n}"], 1)

                for step in steps_of(phase):
                    if step[0] == "job":
                        _, layer, n = step
                        if n < NJ[layer]:
                            g = FIRST[phase][layer] + n
                            for later in range(RING_K) if g == 0 else (g + RING_K - 1,):
                                if later < len(ALL_JOBS[phase]):
                                    masked_keys(later)
                    elif step == "sum0":
                        pool.wait_ge(sems["product"], before("product"))
                        pool.tensor_tensor(XO, X, row["o0_b"].unsqueeze(1).to_broadcast([P, PAIR, C]), ALU.add)\
                            .then_inc(sems["xo"], 1)
                        pool.tensor_tensor(XB2, X, row["b2"].unsqueeze(1).to_broadcast([P, PAIR, C]), ALU.add)\
                            .then_inc(sems["xb2"], 1)
                    elif step == "x1T":
                        pool.wait_ge(leaves("m2"), left("m2"))
                        pool.wait_ge(leaves("x1T"), left("x1T"))
                        pool.tensor_tensor(XB1, X1, row["o1_b"].unsqueeze(1).to_broadcast([P, PAIR, C]), ALU.add)\
                            .then_inc(sems["xb1"], 1)
                    elif step == "hn":
                        inverse_root(ssq[:, :], 1e-6, 0)
                    elif step in ("norm3", "norm2", "norm4"):
                        n = int(step[4])
                        inverse_root(mv[n][:, :, 1], 1e-5, n)
                    elif step == "norm1":
                        inverse_root(mv[1][:, :, 1], 1e-6, 1)
                    elif step == "apply1":
                        pool.wait_ge(sems["n1"], turn("n1"))
                        pool.tensor_tensor(B16, N1, row["gamma"].unsqueeze(1).to_broadcast([P, PAIR, C]), ALU.mult)\
                            .then_inc(sems["gamma"], 1)
                        if phase != "first":
                            pool.wait_ge(leaves("o2"), left("o2"))
                        pool.wait_ge(sems["gamma"], turn("gamma"))
                        pool.tensor_tensor(X2, B16, row["beta"].unsqueeze(1).to_broadcast([P, PAIR, C]), ALU.add)\
                            .then_inc(sems["x2"], 1)
                    elif step[0:2] == "vr":
                        u = int(step[2])
                        if u == 0:
                            pool.wait_ge(leaves("r2"), left("r2"))
                        seed(u)
                    elif step[0] == "gather":
                        states_by_r(step[1])
                if phase == "steady":
                    pool.reg_add(i_reg[pool], i_reg[pool], 1)

            program("start", None)
            program("first", None)
            with pool.Fori(0, TURNS - 2) as i:
                program("steady", i)
            program("closing", None)
            program("last", None)


def kernel(**inputs):
    import numpy as np
    import concourse.bacc as bacc
    from concourse.bass_utils import run_bass_kernel_spmd

    a = {k: np.ascontiguousarray(v) for k, v in inputs.items()}

    def l(n, k):
        return a[f"L{n}_xattn_{k}"]

    def tiles(w):
        return w.reshape(-1, P, w.shape[1]).transpose(1, 0, 2).reshape(P, -1)

    def pad(w):
        return np.concatenate([w, np.zeros((P - w.shape[0], w.shape[1]), w.dtype)], 0) if w.shape[0] < P else w

    def column(v):
        return v.reshape(-1, P).T

    kvw = l(0, "kv_w").reshape(C, C, 2)
    kvb = l(0, "kv_b").reshape(C, 2)
    wl0 = dict(q=l(0, "q_w"), k=kvw[:, :, 0], v=kvw[:, :, 1], o=l(0, "out_w"), w1=l(0, "mlp_w1"), w2=l(0, "mlp_w2"))
    def by_group(w):
        return w.reshape(-1, 8, 4, 8).transpose(0, 2, 1, 3).reshape(-1, C)

    wl1 = dict(q=by_group(l(1, "Wq")), k=np.concatenate([l(1, "Wk")] * 2, 1), v=l(1, "Wv"), o=l(1, "Wo"))
    m2 = l(2, "maa_w2")
    wl2 = dict(m1=l(2, "maa_w1"), d1=l(2, "decay_w1"), r=l(2, "Wr").T, k=l(2, "Wk").T, v=l(2, "Wv").T,
               g=l(2, "Wg").T, o=l(2, "Wo").T, fr=l(2, "fWr").T, fk=l(2, "fWk").T, fv=l(2, "fWv").T,
               m2=m2[0:4].reshape(P, C), m2g=pad(m2[4]), d2=pad(l(2, "decay_w2")))
    wl3 = {k: l(3, "W" + k).T for k in "qkvo"}
    b1 = l(0, "mlp_b1").reshape(4, C)
    cols = dict(q0_b=l(0, "q_b"), k0_b=kvb[:, 0], b1_0=b1[0], b1_1=b1[1], b1_2=b1[2], b1_3=b1[3],
                post_w=l(0, "postnorm_w"), q1_b=by_group(l(1, "bq"))[0], k1_b=np.concatenate([l(1, "bk")] * 4),
                ln1_w=l(2, "ln1_w"), ln1_b=l(2, "ln1_b"), maa_x=l(2, "maa_x"), maa_w=l(2, "maa_w"),
                maa_k=l(2, "maa_k"), maa_v=l(2, "maa_v"), maa_r=l(2, "maa_r"), maa_g=l(2, "maa_g"),
                decay=l(2, "time_decay"), bonus=l(2, "faaaa").reshape(C), gn_w=l(2, "gn_w"), gn_b=l(2, "gn_b"),
                ln2_w=l(2, "ln2_w"), ln2_b=l(2, "ln2_b"), fmaa_k=l(2, "fmaa_k"), fmaa_r=l(2, "fmaa_r"),
                ln3_w=l(3, "ln_gamma"), ln3_b=l(3, "ln_beta"))
    rows = dict(v0_b=kvb[:, 1], o0_b=l(0, "out_b"), b2=l(0, "mlp_b2"), o1_b=l(1, "bo"), gamma=l(1, "gamma"),
                beta=l(1, "beta"), v1_b=np.concatenate([l(1, "bv")] * 4))
    arrays = dict(
        x=a["x"], ctx=a["ctx_2048"], m0=a["mask_BxS2_ik0"], m1=a["mask_Bx1xSxS2_ff0"].reshape(BATCH, P, P),
        m3=a["mask_BxS2_bf1"].view(np.uint8),
        wl0=np.concatenate([tiles(wl0[k]) for k in W_L0], 1), wl1=np.concatenate([tiles(wl1[k]) for k in W_L1], 1),
        wl2=np.concatenate([tiles(wl2[k]) for k in W_L2], 1), wl3=np.concatenate([tiles(wl3[k]) for k in W_L3], 1),
        cols=np.stack([column(cols[k]) for k in COLS], 1), rows=np.stack([rows[k] for k in ROWS])[None],
        gate=l(3, "gate").reshape(1, 1))
    nc = bacc.Bacc("TRN2", target_bir_lowering=False, num_devices=1)
    arrays = {f"in_{k}": np.ascontiguousarray(v) for k, v in arrays.items()}
    args = [nc.dram_tensor(k, v.shape, mybir.dt.from_np(v.dtype), kind="ExternalInput").ap()
            for k, v in arrays.items()]
    out = nc.dram_tensor("out", (BATCH, P, C), F32, kind="ExternalOutput").ap()
    build(nc, *args, out)
    return run_bass_kernel_spmd(nc, [arrays], core_ids=[0]).results[0]["out"]
```
